# Optimizing a Trainium2 kernel written in Bass

```python
import numpy as np
import jax
import jax.numpy as jnp

def _softmax(x, axis=-1):
    return jax.nn.softmax(x, axis=axis)

def _gelu(x):
    return jax.nn.gelu(x, approximate=True)

def _silu(x):
    return jax.nn.silu(x)

def _sigmoid(x):
    return jax.nn.sigmoid(x)

def _layernorm(x, axis=-1, eps=1e-05):
    m = jnp.mean(x, axis=axis, keepdims=True)
    v = jnp.var(x, axis=axis, keepdims=True)
    return (x - m) / jnp.sqrt(v + eps)

def _scatter_add(tgt, idx, src, axis=0):
    return tgt.at[idx].add(src)

def _segment_sum(src, seg, n):
    return jax.ops.segment_sum(src, seg, n)
kernel_name = 'mk_hybrid_d2_jaxref_r8_275564'

def setup_inputs(seed: int=0):
    np.random.seed(seed)
    _w = jnp.asarray

    def _L0_attn_a_setup():
        import jax, jax.numpy as jnp
        import numpy as np
        import math

        def _alibi_slopes(n_heads):

            def pow2(n):
                start = 2 ** (-2 ** (-(math.log2(n) - 3)))
                return [start ** i for i in range(n)]
            if math.log2(n_heads).is_integer():
                slopes = pow2(n_heads)
            else:
                closest = 2 ** math.floor(math.log2(n_heads))
                slopes = pow2(closest) + _alibi_slopes(2 * closest).tolist()[0::2][:n_heads - closest]
            return np.asarray(slopes, dtype=np.float32)
        key = jax.random.key(seed)
        ks = jax.random.split(key, 4)
        B, L, D = (2, 256, 128)
        s = 1.0 / math.sqrt(D)
        return {'x': jax.random.normal(ks[0], (B, L, D), jnp.float32), 'Wqkv': jax.random.normal(ks[1], (D, 3 * D), jnp.float32) * s, 'bqkv': jnp.zeros((3 * D,), jnp.float32), 'Wout': jax.random.normal(ks[2], (D, D), jnp.float32) * s, 'bout': jnp.zeros((D,), jnp.float32)}
    _L0_attn_a_in = _L0_attn_a_setup()

    def _L0_attn_b_setup():
        import jax, jax.numpy as jnp
        import numpy as np
        B, S, E, H = (2, 256, 128, 16)
        D = E // H
        key = jax.random.key(seed)
        ks = jax.random.split(key, 6)
        scale = 1.0 / np.sqrt(E)
        return {'x': jax.random.normal(ks[0], (B, S, E), dtype=jnp.float32), 'Wqkv_w': jax.random.normal(ks[1], (3 * E, E), dtype=jnp.float32) * scale, 'Wqkv_b': jax.random.normal(ks[2], (3 * E,), dtype=jnp.float32) * 0.01, 'out_w': jax.random.normal(ks[3], (E, E), dtype=jnp.float32) * scale, 'out_b': jax.random.normal(ks[4], (E,), dtype=jnp.float32) * 0.01, 'distance_decay': jax.random.normal(ks[5], (1,), dtype=jnp.float32)}
    _L0_attn_b_in = _L0_attn_b_setup()

    def _L0_ffn_setup():
        import jax, jax.numpy as jnp
        import numpy as np
        LOOPS = 2
        NUM_GROUPS = 4
        EXPERTS_PER_GROUP = 2
        NUM_EXPERTS = NUM_GROUPS * EXPERTS_PER_GROUP
        GROUPS_TOP_K = 2
        TOP_K = 1
        RMS_EPS = 1e-06
        EPS = 1e-09

        def _rmsnorm(x, w):
            return x * jax.lax.rsqrt(jnp.mean(x * x, axis=-1, keepdims=True) + RMS_EPS) * w

        def _combine_weights(x_flat, w_macro, w_micro):
            T = x_flat.shape[0]
            macro = jax.nn.softmax(x_flat @ w_macro.T, axis=-1)
            mvals, midx = jax.lax.top_k(macro, GROUPS_TOP_K)
            mvals = mvals / (jnp.sum(mvals, axis=-1, keepdims=True) + EPS)
            micro = jax.nn.softmax(jnp.einsum('td,ged->tge', x_flat, w_micro), axis=-1)
            uvals, uidx = jax.lax.top_k(micro, TOP_K)
            uvals = uvals / (jnp.sum(uvals, axis=-1, keepdims=True) + EPS)
            tok = jnp.arange(T)
            combine = jnp.zeros((T, NUM_EXPERTS), x_flat.dtype)
            for s in range(GROUPS_TOP_K):
                g = midx[:, s]
                wg = mvals[:, s:s + 1]
                li = uidx[tok, g]
                lv = uvals[tok, g]
                eidx = g[:, None] * EXPERTS_PER_GROUP + li
                combine = combine.at[tok[:, None], eidx].add(lv * wg)
            return combine
        key = jax.random.key(seed)
        ks = jax.random.split(key, 6)
        B, S, D, F = (2, 128, 128, 256)
        return {'z': jax.random.normal(ks[0], (B, S, D), jnp.float32), 'norm_w': jnp.ones((D,), jnp.float32), 'w_macro': jax.random.normal(ks[1], (NUM_GROUPS, D), jnp.float32) * D ** (-0.5), 'w_micro': jax.random.normal(ks[2], (NUM_GROUPS, EXPERTS_PER_GROUP, D), jnp.float32) * D ** (-0.5), 'w1': jax.random.normal(ks[3], (NUM_EXPERTS, F, D), jnp.float32) * D ** (-0.5), 'w2': jax.random.normal(ks[4], (NUM_EXPERTS, D, F), jnp.float32) * F ** (-0.5)}
    _L0_ffn_in = _L0_ffn_setup()

    def _L1_attn_a_setup():
        import jax, jax.numpy as jnp
        import numpy as np
        from jax import lax
        N_HEAD, D_HEAD, D_MODEL = (16, 64, 128)
        LN_EPS = 1e-05

        def _layer_norm(x, g, b):
            mu = jnp.mean(x, -1, keepdims=True)
            var = jnp.mean((x - mu) ** 2, -1, keepdims=True)
            return (x - mu) * lax.rsqrt(var + LN_EPS) * g + b
        key = jax.random.key(seed)
        ks = jax.random.split(key, 3)
        slen, bsz = (128, 16)
        h = jax.random.normal(ks[0], (slen, bsz, D_MODEL), dtype=jnp.float32)
        W_qkvb = jax.random.normal(ks[1], (N_HEAD * (3 * D_HEAD + 1), D_MODEL), dtype=jnp.float32) * D_MODEL ** (-0.5)
        W_o = jax.random.normal(ks[2], (D_MODEL, N_HEAD * D_HEAD), dtype=jnp.float32) * (N_HEAD * D_HEAD) ** (-0.5)
        ln_g = jnp.ones((D_MODEL,), dtype=jnp.float32)
        ln_b = jnp.zeros((D_MODEL,), dtype=jnp.float32)
        return {'h': h, 'W_qkvb': W_qkvb, 'W_o': W_o, 'ln_g': ln_g, 'ln_b': ln_b}
    _L1_attn_a_in = _L1_attn_a_setup()

    def _L1_attn_b_setup():
        import jax, jax.numpy as jnp
        import numpy as np
        NUM_HEADS = 16
        key = jax.random.key(seed)
        x = jax.random.normal(key, (4, 256, 128), dtype=jnp.float32)
        return {'x': x}
    _L1_attn_b_in = _L1_attn_b_setup()

    def _L1_ffn_setup():
        import jax, jax.numpy as jnp
        import numpy as np
        B, S, IN, OUT, E, R = (8, 512, 128, 128, 8, 8)
        LORA_ALPHA = 16
        SCALING = LORA_ALPHA / R
        key = jax.random.key(seed)
        k = jax.random.split(key, 6)
        x = jax.random.normal(k[0], (B, S, IN), dtype=jnp.float32)
        base_w = jax.random.normal(k[1], (OUT, IN), dtype=jnp.float32) * 0.02
        base_b = jnp.zeros((OUT,), dtype=jnp.float32)
        lora_A = jax.random.normal(k[2], (IN, R), dtype=jnp.float32) * 0.02
        lora_B = jax.random.normal(k[3], (E, R, OUT), dtype=jnp.float32) * 0.02
        router_w = jax.random.normal(k[4], (E, IN), dtype=jnp.float32) * 0.02
        router_b = jnp.zeros((E,), dtype=jnp.float32)
        return {'x': x, 'base_w': base_w, 'base_b': base_b, 'lora_A': lora_A, 'lora_B': lora_B, 'router_w': router_w, 'router_b': router_b}
    _L1_ffn_in = _L1_ffn_setup()
    _d = {'L0_attn_a_x': _L0_attn_a_in['x'], 'L0_attn_a_Wqkv': _L0_attn_a_in['Wqkv'], 'L0_attn_a_bqkv': _L0_attn_a_in['bqkv'], 'L0_attn_a_Wout': _L0_attn_a_in['Wout'], 'L0_attn_a_bout': _L0_attn_a_in['bout'], 'L0_attn_b_Wqkv_w': _L0_attn_b_in['Wqkv_w'], 'L0_attn_b_Wqkv_b': _L0_attn_b_in['Wqkv_b'], 'L0_attn_b_out_w': _L0_attn_b_in['out_w'], 'L0_attn_b_out_b': _L0_attn_b_in['out_b'], 'L0_attn_b_distance_decay': _L0_attn_b_in['distance_decay'], 'L0_ffn_norm_w': _L0_ffn_in['norm_w'], 'L0_ffn_w_macro': _L0_ffn_in['w_macro'], 'L0_ffn_w_micro': _L0_ffn_in['w_micro'], 'L0_ffn_w1': _L0_ffn_in['w1'], 'L0_ffn_w2': _L0_ffn_in['w2'], 'L1_attn_a_W_qkvb': _L1_attn_a_in['W_qkvb'], 'L1_attn_a_W_o': _L1_attn_a_in['W_o'], 'L1_attn_a_ln_g': _L1_attn_a_in['ln_g'], 'L1_attn_a_ln_b': _L1_attn_a_in['ln_b'], 'L1_ffn_base_w': _L1_ffn_in['base_w'], 'L1_ffn_base_b': _L1_ffn_in['base_b'], 'L1_ffn_lora_A': _L1_ffn_in['lora_A'], 'L1_ffn_lora_B': _L1_ffn_in['lora_B'], 'L1_ffn_router_w': _L1_ffn_in['router_w'], 'L1_ffn_router_b': _L1_ffn_in['router_b']}
    _x0 = _d['L0_attn_a_x']
    _d['L0_attn_a_x'] = jax.random.normal(jax.random.fold_in(jax.random.key(seed), 1), (4, 1024, 128), dtype=_x0.dtype)
    del _x0
    return _d

def reference(L0_attn_a_x, L0_attn_a_Wqkv, L0_attn_a_bqkv, L0_attn_a_Wout, L0_attn_a_bout, L0_attn_b_Wqkv_w, L0_attn_b_Wqkv_b, L0_attn_b_out_w, L0_attn_b_out_b, L0_attn_b_distance_decay, L0_ffn_norm_w, L0_ffn_w_macro, L0_ffn_w_micro, L0_ffn_w1, L0_ffn_w2, L1_attn_a_W_qkvb, L1_attn_a_W_o, L1_attn_a_ln_g, L1_attn_a_ln_b, L1_ffn_base_w, L1_ffn_base_b, L1_ffn_lora_A, L1_ffn_lora_B, L1_ffn_router_w, L1_ffn_router_b):

    def _L0_attn_a_ref(x, Wqkv, bqkv, Wout, bout):
        import jax, jax.numpy as jnp
        import numpy as np
        import math

        def _alibi_slopes(n_heads):

            def pow2(n):
                start = 2 ** (-2 ** (-(math.log2(n) - 3)))
                return [start ** i for i in range(n)]
            if math.log2(n_heads).is_integer():
                slopes = pow2(n_heads)
            else:
                closest = 2 ** math.floor(math.log2(n_heads))
                slopes = pow2(closest) + _alibi_slopes(2 * closest).tolist()[0::2][:n_heads - closest]
            return np.asarray(slopes, dtype=np.float32)
        n_heads = 16
        B, L, D = x.shape
        head_dim = D // n_heads
        qkv = (x @ Wqkv + bqkv).reshape(B, L, 3, n_heads, head_dim)
        q, k, v = (qkv[:, :, 0], qkv[:, :, 1], qkv[:, :, 2])
        scores = jnp.einsum('bqhd,bkhd->bhqk', q, k) / math.sqrt(head_dim)
        pos = jnp.arange(L)
        bias = -jnp.abs(pos[None, :] - pos[:, None]).astype(jnp.float32)
        slopes = jnp.asarray(_alibi_slopes(n_heads))
        scores = scores + slopes[None, :, None, None] * bias[None, None]
        probs = jax.nn.softmax(scores, axis=-1)
        out = jnp.einsum('bhqk,bkhd->bqhd', probs, v).reshape(B, L, D)
        return out @ Wout + bout

    def _L0_attn_b_ref(x, Wqkv_w, Wqkv_b, out_w, out_b, distance_decay):
        import jax, jax.numpy as jnp
        import numpy as np
        B, S, E, H = (2, 256, 128, 16)
        D = E // H
        b, s, e = x.shape
        qkv = x @ Wqkv_w.T + Wqkv_b
        qkv = qkv.reshape(b, s, 3, H, D).transpose(2, 0, 3, 1, 4)
        q, k, v = (qkv[0], qkv[1], qkv[2])
        scores = jnp.einsum('bhsd,bhtd->bhst', q, k) / jnp.sqrt(jnp.asarray(D, x.dtype))
        idx = jnp.arange(s, dtype=x.dtype)
        dist = jnp.abs(idx[:, None] - idx[None, :])
        decay = jnp.exp(-jnp.abs(distance_decay[0]) * dist)
        scores = scores * decay
        attn = jax.nn.softmax(scores, axis=-1)
        out = jnp.einsum('bhst,bhtd->bhsd', attn, v)
        out = out.transpose(0, 2, 1, 3).reshape(b, s, e)
        return out @ out_w.T + out_b

    def _L0_ffn_ref(z, norm_w, w_macro, w_micro, w1, w2):
        import jax, jax.numpy as jnp
        import numpy as np
        LOOPS = 2
        NUM_GROUPS = 4
        EXPERTS_PER_GROUP = 2
        NUM_EXPERTS = NUM_GROUPS * EXPERTS_PER_GROUP
        GROUPS_TOP_K = 2
        TOP_K = 1
        RMS_EPS = 1e-06
        EPS = 1e-09

        def _rmsnorm(x, w):
            return x * jax.lax.rsqrt(jnp.mean(x * x, axis=-1, keepdims=True) + RMS_EPS) * w

        def _combine_weights(x_flat, w_macro, w_micro):
            T = x_flat.shape[0]
            macro = jax.nn.softmax(x_flat @ w_macro.T, axis=-1)
            mvals, midx = jax.lax.top_k(macro, GROUPS_TOP_K)
            mvals = mvals / (jnp.sum(mvals, axis=-1, keepdims=True) + EPS)
            micro = jax.nn.softmax(jnp.einsum('td,ged->tge', x_flat, w_micro), axis=-1)
            uvals, uidx = jax.lax.top_k(micro, TOP_K)
            uvals = uvals / (jnp.sum(uvals, axis=-1, keepdims=True) + EPS)
            tok = jnp.arange(T)
            combine = jnp.zeros((T, NUM_EXPERTS), x_flat.dtype)
            for s in range(GROUPS_TOP_K):
                g = midx[:, s]
                wg = mvals[:, s:s + 1]
                li = uidx[tok, g]
                lv = uvals[tok, g]
                eidx = g[:, None] * EXPERTS_PER_GROUP + li
                combine = combine.at[tok[:, None], eidx].add(lv * wg)
            return combine
        B, S, D = z.shape
        T = B * S
        for _ in range(LOOPS):
            zn = _rmsnorm(z, norm_w)
            x = zn.reshape(T, D)
            combine = _combine_weights(x, w_macro, w_micro)
            h = jax.nn.silu(jnp.einsum('td,efd->tef', x, w1))
            y = jnp.einsum('tef,edf->ted', h, w2)
            mixed = jnp.einsum('ted,te->td', y, combine)
            z = z + mixed.reshape(B, S, D)
        return z

    def _L1_attn_a_ref(h, W_qkvb, W_o, ln_g, ln_b):
        import jax, jax.numpy as jnp
        import numpy as np
        from jax import lax
        N_HEAD, D_HEAD, D_MODEL = (16, 64, 128)
        LN_EPS = 1e-05

        def _layer_norm(x, g, b):
            mu = jnp.mean(x, -1, keepdims=True)
            var = jnp.mean((x - mu) ** 2, -1, keepdims=True)
            return (x - mu) * lax.rsqrt(var + LN_EPS) * g + b
        slen, bsz, _ = h.shape
        BH = bsz * N_HEAD
        qkvb = jnp.einsum('sbd,ed->sbe', h, W_qkvb).reshape(slen, BH, 3 * D_HEAD + 1)
        q, k, v, beta = jnp.split(qkvb, [D_HEAD, 2 * D_HEAD, 3 * D_HEAD], axis=-1)
        beta = jax.nn.sigmoid(beta)
        q = jax.nn.elu(q) + 1.0
        k = jax.nn.elu(k) + 1.0
        q = q / jnp.sum(q, -1, keepdims=True)
        k = k / jnp.sum(k, -1, keepdims=True)

        def step(W, inp):
            k_t, v_t, q_t, b_t = inp
            v_old = jnp.einsum('bij,bj->bi', W, k_t)
            v_ins = b_t * (v_t - v_old)
            W = W + v_ins[:, :, None] * k_t[:, None, :]
            out = jnp.einsum('bij,bj->bi', W, q_t)
            return (W, out)
        W0 = jnp.zeros((BH, D_HEAD, D_HEAD), dtype=h.dtype)
        _, outs = lax.scan(step, W0, (k, v, q, beta))
        scale = 1.0 / D_HEAD ** 0.5
        layer_out = (scale * outs).reshape(slen, bsz, N_HEAD * D_HEAD)
        attn_out = jnp.einsum('sbe,de->sbd', layer_out, W_o)
        return _layer_norm(h + attn_out, ln_g, ln_b)

    def _L1_attn_b_ref(x):
        import jax, jax.numpy as jnp
        import numpy as np
        NUM_HEADS = 16
        B, T, D = x.shape
        H = NUM_HEADS
        hd = D // H
        xh = x.reshape(B, T, H, hd)
        x_centered = xh - jnp.mean(xh, axis=1, keepdims=True)
        corr = jnp.einsum('bthd,bThd->bhtT', x_centered, x_centered)
        corr = jax.nn.softmax(corr, axis=-1)
        out = jnp.einsum('bhtT,bThd->bthd', corr, xh)
        return out.reshape(B, T, D)

    def _L1_ffn_ref(x, base_w, base_b, lora_A, lora_B, router_w, router_b):
        import jax, jax.numpy as jnp
        import numpy as np
        B, S, IN, OUT, E, R = (8, 512, 128, 128, 8, 8)
        LORA_ALPHA = 16
        SCALING = LORA_ALPHA / R
        result = jnp.einsum('bsd,od->bso', x, base_w) + base_b
        logits = jnp.einsum('bsd,ed->bse', x, router_w) + router_b
        gating = jax.nn.softmax(logits, axis=-1).astype(jnp.bfloat16)
        mid = jnp.einsum('bsd,dr->bsr', x, lora_A)
        lora_out = jnp.einsum('bsr,erd,bse->bsd', mid, lora_B, gating.astype(jnp.float32))
        return result + lora_out * SCALING
    x = L0_attn_a_x
    x = x + _L0_attn_a_ref(_layernorm(x, axis=-1), L0_attn_a_Wqkv, L0_attn_a_bqkv, L0_attn_a_Wout, L0_attn_a_bout)
    x = x + _L0_ffn_ref(_layernorm(x, axis=-1), L0_ffn_norm_w, L0_ffn_w_macro, L0_ffn_w_micro, L0_ffn_w1, L0_ffn_w2)
    x = x + _L0_attn_b_ref(_layernorm(x, axis=-1), L0_attn_b_Wqkv_w, L0_attn_b_Wqkv_b, L0_attn_b_out_w, L0_attn_b_out_b, L0_attn_b_distance_decay)
    x = x + _L0_ffn_ref(_layernorm(x, axis=-1), L0_ffn_norm_w, L0_ffn_w_macro, L0_ffn_w_micro, L0_ffn_w1, L0_ffn_w2)
    x = x + _L1_attn_a_ref(_layernorm(x, axis=-1), L1_attn_a_W_qkvb, L1_attn_a_W_o, L1_attn_a_ln_g, L1_attn_a_ln_b)
    x = x + _L1_ffn_ref(_layernorm(x, axis=-1), L1_ffn_base_w, L1_ffn_base_b, L1_ffn_lora_A, L1_ffn_lora_B, L1_ffn_router_w, L1_ffn_router_b)
    x = x + _L1_attn_b_ref(_layernorm(x, axis=-1))
    x = x + _L1_ffn_ref(_layernorm(x, axis=-1), L1_ffn_base_w, L1_ffn_base_b, L1_ffn_lora_A, L1_ffn_lora_B, L1_ffn_router_w, L1_ffn_router_b)
    return x

_drawn_inputs = setup_inputs


def setup_inputs(seed=0):
    import zlib

    import numpy as np

    out = dict(_drawn_inputs(seed))
    spreads = {'L0_attn_a_bqkv': (0.0, 0.1),
     'L0_attn_a_bout': (0.0, 0.1),
     'L0_ffn_norm_w': (1.0, 0.2),
     'L1_attn_a_ln_g': (1.0, 0.2),
     'L1_attn_a_ln_b': (0.0, 0.398),
     'L1_ffn_base_b': (0.0, 0.1),
     'L1_ffn_router_b': (0.0, 0.8)}
    factors = {'L0_attn_b_Wqkv_b': 4.404,
     'L0_attn_b_out_b': 5.98,
     'L1_attn_a_W_qkvb': 8.0,
     'L1_attn_a_W_o': 8.0,
     'L1_ffn_lora_A': 8.0,
     'L1_ffn_lora_B': 8.0,
     'L1_ffn_router_w': 8.0}
    for name, (base, spread) in spreads.items():
        noise = np.random.default_rng([zlib.crc32(name.encode()), seed]).standard_normal(out[name].shape)
        drawn = base * np.exp(spread * noise) if base else spread * noise
        out[name] = jnp.asarray(drawn.astype(out[name].dtype))
    for name, factor in factors.items():
        out[name] = (out[name] * factor).astype(out[name].dtype)
    return out
```

```python
import math
from contextlib import ExitStack

import concourse.bass as bass
from concourse import mybir

ALU = mybir.AluOpType
ACT = mybir.ActivationFunctionType
F32 = mybir.dt.float32
BF16 = mybir.dt.bfloat16
I32 = mybir.dt.int32
AX = mybir.AxisListType.X

P = 128
D = 128
BATCH, SEQ = 4, 1024
TOK = BATCH * SEQ
TILES = TOK // P
TPB = SEQ // P
HEADS, HD = 16, 8
LN_EPS = 1e-5
CHUNK = 512
BANK = 512


class Kit:

    def __init__(self, nc, stack, shared=None):
        self.nc, self.stack = nc, stack
        self.shared = shared

    def sb(self, name, shape, dt=F32):
        return self.stack.enter_context(self.nc.sbuf_tensor(name, shape, dt))

    def ps(self, name, shape):
        return self.stack.enter_context(self.nc.psum_tensor(name, shape, F32))

    def sem(self, name):
        return self.nc.alloc_semaphore(name)


def counter(engine, sem, base=0):
    count = [0]

    def link(ins):
        count[0] += 1
        ins.then_inc(sem, 1)
        engine.wait_ge(sem, base + count[0])
    link.count = count
    return link


def over(ap, n):
    return ap.unsqueeze(len(ap.shape)).to_broadcast(list(ap.shape) + [n])


def over_mid(ap, n):
    return ap.unsqueeze(1).to_broadcast([ap.shape[0], n, ap.shape[1]])


def layer_norm(nc, tag, X, XN, XT, ident, gain=None, shift=None):
    GROUP = 8
    STEPS = TILES // GROUP
    with ExitStack() as stack:
        k = Kit(nc, stack)
        squares = k.sb(f"{tag}_squares", [P, TILES, D])
        mean = k.sb(f"{tag}_mean", [P, TILES])
        var = k.sb(f"{tag}_var", [P, TILES])
        std = k.sb(f"{tag}_std", [P, TILES])
        rstd = k.sb(f"{tag}_rstd", [P, TILES])
        eps = k.sb(f"{tag}_eps", [P, 1])
        turned_ps = k.ps(f"{tag}_turned_ps", [P, 2, GROUP, P])
        step_done = k.sem(f"{tag}_step_done")
        centred = k.sem(f"{tag}_centred")
        squared = k.sem(f"{tag}_squared")
        var_ready = k.sem(f"{tag}_var_ready")
        std_ready = k.sem(f"{tag}_std_ready")
        normed = k.sem(f"{tag}_normed")
        turned = k.sem(f"{tag}_turned")
        copied = k.sem(f"{tag}_copied")
        block = stack.enter_context(nc.Block())
        cut = [slice(GROUP * s, GROUP * (s + 1)) for s in range(STEPS)]

        @block.vector
        def _(dve):
            link = counter(dve, step_done)
            link(dve.memset(eps[:], LN_EPS))
            for c in cut:
                link(dve.tensor_reduce(mean[:, c], X[:, c, :], AX, ALU.add))
                link(dve.tensor_scalar(mean[:, c], mean[:, c], 1.0 / D, None, ALU.mult))
                dve.tensor_tensor(XN[:, c, :], X[:, c, :], over(mean[:, c], D),
                                  ALU.subtract).then_inc(centred, 1)
            for s, c in enumerate(cut):
                dve.wait_ge(squared, s + 1)
                dve.tensor_reduce(var[:, c], squares[:, c, :], AX, ALU.add).then_inc(var_ready, 1)
            for s, c in enumerate(cut):
                dve.wait_ge(std_ready, s + 1)
                link(dve.reciprocal(rstd[:, c], std[:, c]))
                scaled = dve.tensor_tensor(XN[:, c, :], XN[:, c, :], over(rstd[:, c], D), ALU.mult)
                if gain is not None:
                    link(scaled)
                    link(dve.tensor_tensor(XN[:, c, :], XN[:, c, :], over_mid(gain, GROUP), ALU.mult))
                    scaled = dve.tensor_tensor(XN[:, c, :], XN[:, c, :], over_mid(shift, GROUP), ALU.add)
                scaled.then_inc(normed, 1)

        @block.scalar
        def _(act):
            for s, c in enumerate(cut):
                act.wait_ge(centred, s + 1)
                act.activation(squares[:, c, :], XN[:, c, :], ACT.Square).then_inc(squared, 1)
            for s, c in enumerate(cut):
                act.wait_ge(var_ready, s + 1)
                act.activation(std[:, c], var[:, c], ACT.Sqrt, bias=eps[:, 0:1],
                               scale=1.0 / D).then_inc(std_ready, 1)
            if XT is not None:
                for s in range(STEPS):
                    act.wait_ge(turned, s + 1)
                    act.copy(XT[:, GROUP * P * s:GROUP * P * (s + 1)],
                             turned_ps[:, s % 2, :, :].rearrange("p t q -> p (t q)")).then_inc(copied, 1)

        if XT is not None:
            @block.tensor
            def _(pe):
                for s in range(STEPS):
                    pe.wait_ge(normed, s + 1)
                    if s >= 2:
                        pe.wait_ge(copied, s - 1)
                    for t in range(GROUP):
                        last = pe.transpose(turned_ps[:, s % 2, t, :], XN[:, GROUP * s + t, :], ident)
                    last.then_inc(turned, 1)


Q_PARTS = (0, 0, 1, 1, 0, 2)
K_PARTS = (0, 1, 0, 1, 2, 0)
ROWS = HD * len(Q_PARTS)
GH = 4
VW = 32
WIN = 2 * SEQ - P


def project_qkv(nc, tag, XT, w_qkv, b_qk, b_v, V, parts_dram, scale, head_of, longest2):
    CH = TOK // CHUNK
    with ExitStack() as stack:
        kk = Kit(nc, stack)
        full = kk.sb(f"{tag}_full", [P, 2, CHUNK])
        rest = kk.sb(f"{tag}_rest", [P, 2, CHUNK])
        parts = kk.sb(f"{tag}_parts", [P, 2, 3, CHUNK], BF16)
        squares = kk.sb(f"{tag}_squares", [P, 2, CHUNK])
        norm2_ps = kk.ps(f"{tag}_norm2_ps", [HEADS, 2, BANK])
        squared = kk.sem(f"{tag}_squared")
        norm2_done = kk.sem(f"{tag}_norm2_done")
        longest_done = kk.sem(f"{tag}_longest_done")
        qk_ps = kk.ps(f"{tag}_qk_ps", [P, 2, BANK])
        v_ps = kk.ps(f"{tag}_v_ps", [P, 2, 4, D])
        projected = kk.sem(f"{tag}_projected")
        biased = kk.sem(f"{tag}_biased")
        part1 = kk.sem(f"{tag}_part1")
        rest1 = kk.sem(f"{tag}_rest1")
        part2 = kk.sem(f"{tag}_part2")
        part3 = kk.sem(f"{tag}_part3")
        stored = [kk.sem(f"{tag}_stored{b}") for b in range(2)]
        v_done = kk.sem(f"{tag}_v_done")
        v_out = kk.sem(f"{tag}_v_out")
        block = stack.enter_context(nc.Block())
        UNITS = 2 * CH

        @block.tensor
        def _(pe):
            def norms(u):
                pe.wait_ge(squared, u + 1)
                if u >= 2:
                    pe.wait_ge(longest_done, u - 1)
                pe.matmul(norm2_ps[:, u % 2, :], head_of, squares[:, u % 2, :], start=True,
                          stop=True).then_inc(norm2_done, 1)

            for u in range(UNITS):
                c, w = divmod(u, 2)
                if u >= 2:
                    pe.wait_ge(biased, u - 1)
                pe.matmul(qk_ps[:, u % 2, :], w_qkv[:, w * D:(w + 1) * D],
                          XT[:, c * CHUNK:(c + 1) * CHUNK], start=True, stop=True).then_inc(projected, 1)
                if u >= 1:
                    norms(u - 1)
            norms(UNITS - 1)
            for s in range(TILES // 4):
                if s >= 2:
                    pe.wait_ge(v_out, s - 1)
                for t in range(4):
                    last = pe.matmul(v_ps[:, s % 2, t, :], XT[:, (4 * s + t) * P:(4 * s + t + 1) * P],
                                     w_qkv[:, 2 * D:3 * D], start=True, stop=True)
                last.then_inc(v_done, 1)

        @block.vector
        def _(dve):
            for u in range(UNITS):
                w, b = u % 2, u % 2
                dve.wait_ge(projected, u + 1)
                if u >= 2:
                    dve.wait_ge(squared, u - 1)
                dve.tensor_scalar(full[:, b, :], qk_ps[:, b, :], b_qk[:, w:w + 1],
                                  scale if w == 0 else 1.0, ALU.add, ALU.mult).then_inc(biased, 1)
                dve.wait_ge(part1, u + 1)
                dve.wait_ge(biased, u + 1)
                dve.tensor_tensor(rest[:, b, :], full[:, b, :], parts[:, b, 0, :],
                                  ALU.subtract).then_inc(rest1, 1)
                dve.wait_ge(part2, u + 1)
                dve.wait_ge(rest1, u + 1)
                dve.tensor_tensor(parts[:, b, 2, :], rest[:, b, :], parts[:, b, 1, :],
                                  ALU.subtract).then_inc(part3, 1)
                dve.wait_ge(norm2_done, u + 1)
                dve.tensor_reduce(longest2[:, w, u // 2:u // 2 + 1], norm2_ps[:, b, :], AX,
                                  ALU.max).then_inc(longest_done, 1)
            for s in range(TILES // 4):
                dve.wait_ge(v_done, s + 1)
                dve.tensor_tensor(V[:, 4 * s:4 * s + 4, :], v_ps[:, s % 2, :, :], over_mid(b_v, 4),
                                  ALU.add).then_inc(v_out, 1)

        @block.scalar
        def _(act):
            for u in range(UNITS):
                b = u % 2
                act.wait_ge(biased, u + 1)
                if u >= 2:
                    act.wait_ge(stored[b], 16 * (u // 2))
                act.copy(parts[:, b, 0, :], full[:, b, :]).then_inc(part1, 1)
                if u >= 2:
                    act.wait_ge(norm2_done, u - 1)
                act.activation(squares[:, b, :], full[:, b, :], ACT.Square).then_inc(squared, 1)
                act.wait_ge(rest1, u + 1)
                act.copy(parts[:, b, 1, :], rest[:, b, :]).then_inc(part2, 1)

        @block.sync
        def _(sp):
            for u in range(UNITS):
                c, w = divmod(u, 2)
                sp.wait_ge(part3, u + 1)
                sp.dma_start(parts_dram[w].rearrange("s f t -> f s t")[:, :, c * CHUNK:(c + 1) * CHUNK],
                             parts[:, u % 2, :, :]).then_inc(stored[u % 2], 16)
            for b in range(2):
                sp.wait_ge(stored[b], 16 * CH)


SAFE_SCORE = 60.0


def bound_scores(nc, tag, longest2, wide, ident):
    with ExitStack() as stack:
        k = Kit(nc, stack)
        longest = k.sb(f"{tag}_longest", [HEADS, 2])
        square = k.sb(f"{tag}_square", [HEADS, 1])
        top = k.sb(f"{tag}_top", [1, 1])
        row_ps = k.ps(f"{tag}_row_ps", [1, HEADS])
        step_done = k.sem(f"{tag}_step_done")
        square_done = k.sem(f"{tag}_square_done")
        row_done = k.sem(f"{tag}_row_done")
        top_done = k.sem(f"{tag}_top_done")
        with nc.Block() as block:
            @block.vector
            def _(dve):
                link = counter(dve, step_done)
                link(dve.tensor_reduce(longest[:, :], longest2[:, :, :], AX, ALU.max))
                dve.tensor_tensor(square[:, :], longest[:, 0:1], longest[:, 1:2], ALU.mult).then_inc(square_done, 1)
                dve.wait_ge(row_done, 1)
                dve.tensor_reduce(top[:, :], row_ps[:, :], AX, ALU.max).then_inc(top_done, 1)
                dve.wait_ge(top_done, 1)
                dve.tensor_scalar(wide[:, :], top[:, :], SAFE_SCORE ** 2, None, ALU.is_gt)

            @block.tensor
            def _(pe):
                pe.wait_ge(square_done, 1)
                pe.matmul(row_ps[:, :], square[:, :], ident[0:HEADS, 0:HEADS], start=True, stop=True).then_inc(row_done, 1)


def attend(nc, tag, V, parts_dram, tables, op, out_all, ident):
    QT = TPB
    UNITS = QT * GH
    RING = 6
    LAG = 3
    AHEAD = 4
    with ExitStack() as stack:
        k = Kit(nc, stack)
        q_rows = k.sb(f"{tag}_q_rows", [P, 2, GH, SEQ], BF16)
        k_rows = k.sb(f"{tag}_k_rows", [P, 2, GH, SEQ], BF16)
        v_cols = k.sb(f"{tag}_v_cols", [P, 2, TPB, GH, VW])
        table = tables["buffer"]
        probs = k.sb(f"{tag}_probs", [P, RING, SEQ])
        row_max = k.sb(f"{tag}_row_max", [P, UNITS])
        tick = k.sb(f"{tag}_tick", [P, UNITS + 1])
        zero = k.sb(f"{tag}_zero", [P, 1])
        neg_max = k.sb(f"{tag}_neg_max", [P, UNITS])
        probs_t = k.sb(f"{tag}_probs_t", [P, 2, GH, TPB, P])
        out_t = k.sb(f"{tag}_out_t", [P, P])
        inv_sum = k.sb(f"{tag}_inv_sum", [P, QT, GH])
        s_ps = k.ps(f"{tag}_s_ps", [P, 2, SEQ])
        t_ps = k.ps(f"{tag}_t_ps", [P, 2, 4, P])
        o_ps = k.ps(f"{tag}_o_ps", [P, BANK])
        ot_ps = k.ps(f"{tag}_ot_ps", [P, BANK])
        loaded = [k.sem(f"{tag}_loaded{half}") for half in range(2)]
        group_done = k.sem(f"{tag}_group_done")
        padded = k.sem(f"{tag}_padded")
        table_set = k.sem(f"{tag}_table_set")
        v_set = k.sem(f"{tag}_v_set")
        scored = k.sem(f"{tag}_scored")
        maxed = k.sem(f"{tag}_maxed")
        negated = k.sem(f"{tag}_negated")
        exped = k.sem(f"{tag}_exped")
        turned = k.sem(f"{tag}_turned")
        left_out = k.sem(f"{tag}_left_out")
        right_out = k.sem(f"{tag}_right_out")
        summed = k.sem(f"{tag}_summed")
        o_out = k.sem(f"{tag}_o_out")
        o_turned = k.sem(f"{tag}_o_turned")
        inverted = k.sem(f"{tag}_inverted")
        normed = k.sem(f"{tag}_normed")
        block = stack.enter_context(nc.Block())
        LOADS = 2 * len(Q_PARTS)

        @block.sync
        def _(sp):
            sp.wait_ge(padded, 3)
            with sp.Fori(0, HEADS // GH) as hg:
                with sp.Fori(0, BATCH // 2) as bp:
                    for half in range(2):
                        sp.wait_ge(group_done, hg * 4 + bp * 2 + (half + 1))
                        for rows, which, order in ((q_rows, 0, Q_PARTS), (k_rows, 1, K_PARTS)):
                            for n, part in enumerate(order):
                                src = parts_dram[0 if tables.get("same") else which, part].rearrange("(h e) t -> e h t", e=HD)
                                sp.dma_start(
                                    rows[n * HD:(n + 1) * HD, half, :, :],
                                    src[:, bass.ds(hg * GH, GH), bass.ds(bp * (2 * SEQ) + half * SEQ, SEQ)],
                                ).then_inc(loaded[half], 16)

        @block.gpsimd
        def _(pool):
            pool.memset(q_rows[:].bitcast(F32), 0.0).then_inc(padded, 1)
            pool.memset(k_rows[:].bitcast(F32), 0.0).then_inc(padded, 1)
            pool.memset(v_cols[:], 0.0).then_inc(padded, 1)
            pool.wait_ge(padded, 3)
            pool.memset(v_cols[:, :, :, :, HD:HD + 1], 1.0).then_inc(padded, 1)
            pool.memset(zero[:, :], 0.0).then_inc(padded, 1)
            pool.wait_ge(padded, 5)
            with pool.Fori(0, HEADS // GH) as hg:
                if tables.get("per_group"):
                    for j in range(GH):
                        if j == 0:
                            pool.wait_ge(tables["free"], hg + 1)
                        pool.wait_ge(padded, 5)
                        pool.tensor_tensor(table[:, j, :], tables["distance"][:, :],
                                           tables["slopes"][:, bass.ds(hg * GH + j, 1)].to_broadcast([P, WIN]),
                                           ALU.mult).then_inc(table_set, 1)
                with pool.Fori(0, BATCH // 2) as bp:
                    for half in range(2):
                        g = hg * 4 + bp * 2
                        pool.wait_ge(group_done, g + (half + 1))
                        src = V[:, bass.ds(bp * (2 * TPB) + half * TPB, TPB), bass.ds(hg * (GH * HD), GH * HD)]
                        pool.tensor_copy(v_cols[:, half, :, :, 0:HD],
                                         src.rearrange("p t (h e) -> p t h e", e=HD)).then_inc(v_set, 1)
                        for n in range(UNITS):
                            pool.wait_ge(maxed, (g + half) * UNITS + (n + 1))
                            pool.tensor_tensor(neg_max[:, n:n + 1], zero[:, :], row_max[:, n:n + 1],
                                               ALU.subtract).then_inc(negated, 1)

        @block.tensor
        def _(pe):
            pe.sem_inc(group_done, 2)
            pe.wait_ge(padded, 5)
            with pe.Fori(0, HEADS // GH) as hg:
                with pe.Fori(0, BATCH // 2) as bp:
                    for half in range(2):
                        g = hg * 4 + (bp * 2 + half)

                        def scores(n):
                            qt, j = divmod(n, GH)
                            if n >= 2:
                                pe.wait_ge(maxed, g * UNITS + (n - 1))
                            for c in range(2):
                                last = pe.matmul(s_ps[:, n % 2, c * BANK:(c + 1) * BANK],
                                                 q_rows[:, half, j, qt * P:(qt + 1) * P],
                                                 k_rows[:, half, j, c * BANK:(c + 1) * BANK],
                                                 start=True, stop=True)
                            last.then_inc(scored, 1)

                        def turn(n):
                            pe.wait_ge(exped, g * UNITS + (n + 1))
                            for side in range(2):
                                if n >= 1:
                                    pe.wait_ge((left_out, right_out)[side], g * UNITS + n)
                                for t in range(4):
                                    kt = 4 * side + t
                                    last = pe.transpose(t_ps[:, side, t, :],
                                                        probs[:, n % RING, kt * P:(kt + 1) * P], ident)
                                last.then_inc(turned, 1)

                        def sum_up(qt):
                            pe.wait_ge(left_out, g * UNITS + GH * (qt + 1))
                            pe.wait_ge(right_out, g * UNITS + GH * (qt + 1))
                            if qt >= 1:
                                pe.wait_ge(o_out, g * QT + qt)
                            for kt in range(TPB):
                                for j in range(GH):
                                    last = pe.matmul(o_ps[VW * j:VW * (j + 1), 0:P], v_cols[:, half, kt, j, :],
                                                     probs_t[:, qt % 2, j, kt, :], start=(kt == 0),
                                                     stop=(kt == TPB - 1))
                            last.then_inc(summed, 1)

                        def turn_sum(qt):
                            pe.wait_ge(o_out, g * QT + (qt + 1))
                            if qt >= 1:
                                pe.wait_ge(normed, g * QT + qt)
                            pe.transpose(ot_ps[:, 0:P], out_t[:, :], ident).then_inc(o_turned, 1)

                        pe.wait_ge(loaded[half], (hg * 2 + bp + 1) * (16 * LOADS))
                        pe.wait_ge(v_set, g + 1)
                        for n in range(AHEAD):
                            scores(n)
                        for n in range(UNITS):
                            if n + AHEAD < UNITS:
                                scores(n + AHEAD)
                            turn(n)
                            if n % GH == 1 and n > GH:
                                sum_up(n // GH - 1)
                            if n % GH == 2 and n > GH:
                                turn_sum(n // GH - 1)
                        sum_up(QT - 1)
                        pe.wait_ge(o_out, g * QT + QT)
                        pe.wait_ge(normed, g * QT + (QT - 1))
                        pe.transpose(ot_ps[:, 0:P], out_t[:, :], ident).then_inc(o_turned, 1)
                        pe.wait_ge(o_turned, g * QT + QT)
                        pe.sem_inc(group_done, 1)

        @block.vector
        def _(dve):
            if tables.get("per_group"):
                dve.sem_inc(tables["free"], 1)
            with dve.Fori(0, HEADS // GH) as hg:
                if tables.get("per_group"):
                    dve.wait_ge(table_set, (hg + 1) * GH)
                    dve.memset(tick[:, UNITS:UNITS + 1], 0.0)
                with dve.Fori(0, BATCH // 2) as bp:
                    for half in range(2):
                        g = hg * 4 + (bp * 2 + half)

                        def left(n):
                            dve.wait_ge(turned, g * (2 * UNITS) + (2 * n + 1))
                            if n // GH >= 2:
                                dve.wait_ge(summed, g * QT + (n // GH - 1))
                            dve.tensor_copy(probs_t[:, (n // GH) % 2, n % GH, 0:4, :],
                                            t_ps[:, 0, :, :]).then_inc(left_out, 1)

                        def norm(qt):
                            dve.wait_ge(o_turned, g * QT + (qt + 1))
                            heads = ot_ps[:, 0:P].rearrange("p (h e) -> p h e", e=VW)
                            dve.reciprocal(inv_sum[:, qt, :], heads[:, :, HD]).then_inc(inverted, 1)
                            dve.wait_ge(inverted, g * QT + (qt + 1))
                            dst = out_all[:, bass.ds(bp * (2 * TPB) + (half * TPB + qt), 1),
                                          bass.ds(hg * (GH * HD), GH * HD)]
                            dve.tensor_tensor(dst.rearrange("p o (h e) -> p (o h) e", e=HD),
                                              heads[:, :, 0:HD], over(inv_sum[:, qt, :], HD),
                                              ALU.mult).then_inc(normed, 1)

                        for n in range(UNITS):
                            qt, j = divmod(n, GH)
                            dve.wait_ge(scored, g * UNITS + (n + 1))
                            if n >= RING:
                                dve.wait_ge(turned, g * (2 * UNITS) + 2 * (n - RING + 1))
                            dve.memset(tick[:, n:n + 1], 0.0)
                            at = SEQ - P - qt * P
                            t = table[:, j if tables.get("per_group") else 0, at:at + SEQ]
                            dve.tensor_tensor_reduce(out=probs[:, n % RING, :], in0=s_ps[:, n % 2, :], in1=t,
                                                     scale=1.0, scalar=-3e38, op0=op, op1=ALU.max,
                                                     accum_out=row_max[:, n:n + 1]).then_inc(maxed, 1)
                            if n >= LAG:
                                left(n - LAG)
                            if n % GH == GH - 1 and n >= 2 * GH:
                                norm(n // GH - 2)
                        for n in range(UNITS - LAG, UNITS):
                            left(n)
                        norm(QT - 2)
                        norm(QT - 1)
                if tables.get("per_group"):
                    dve.wait_ge(maxed, (hg + 1) * (BATCH * UNITS))
                    dve.sem_inc(tables["free"], 1)

        @block.scalar
        def _(act):
            with act.Fori(0, HEADS // GH) as hg:
                with act.Fori(0, BATCH // 2) as bp:
                    for half in range(2):
                        g = hg * 4 + (bp * 2 + half)

                        def right(n):
                            act.wait_ge(turned, g * (2 * UNITS) + (2 * n + 2))
                            if n // GH >= 2:
                                act.wait_ge(summed, g * QT + (n // GH - 1))
                            act.copy(probs_t[:, (n // GH) % 2, n % GH, 4:8, :],
                                     t_ps[:, 1, :, :]).then_inc(right_out, 1)

                        def take_sum(qt):
                            act.wait_ge(summed, g * QT + (qt + 1))
                            if qt >= 1:
                                act.wait_ge(o_turned, g * QT + qt)
                            act.copy(out_t[:, :], o_ps[:, 0:P]).then_inc(o_out, 1)

                        for n in range(UNITS):
                            act.wait_ge(negated, g * UNITS + (n + 1))
                            act.activation(probs[:, n % RING, :], probs[:, n % RING, :], ACT.Exp,
                                           bias=neg_max[:, n:n + 1]).then_inc(exped, 1)
                            if n >= 1:
                                right(n - 1)
                            if n % GH == 2 and n > GH:
                                take_sum(n // GH - 1)
                        right(UNITS - 1)
                        take_sum(QT - 1)


def attend_transposed(nc, tag, V, parts_dram, out_t, shift_dram=None, table=None, slopes=None):
    by_dve = table is not None
    JT = TPB
    UNITS = JT * GH
    NG = (HEADS // GH) * BATCH
    SLOTS = 3
    SHIFT_ROW = 64
    with ExitStack() as stack:
        k = Kit(nc, stack)
        q_rows = k.sb(f"{tag}_q_rows", [P, 2, GH, SEQ], BF16)
        k_rows = k.sb(f"{tag}_k_rows", [P, 2, GH, SEQ], BF16)
        v_cols = k.sb(f"{tag}_v_cols", [P, 2, TPB, GH, VW])
        probs = k.sb(f"{tag}_probs", [P, 2, GH, SEQ])
        s_ps = k.ps(f"{tag}_s_ps", [P, SLOTS, SEQ])
        o_ps = k.ps(f"{tag}_o_ps", [P, 2, BANK])
        loaded = [k.sem(f"{tag}_loaded{half}") for half in range(2)]
        padded = k.sem(f"{tag}_padded")
        v_set = k.sem(f"{tag}_v_set")
        scored = k.sem(f"{tag}_scored")
        exped = k.sem(f"{tag}_exped")
        summed = k.sem(f"{tag}_summed")
        o_out = k.sem(f"{tag}_o_out")
        block = stack.enter_context(nc.Block())
        adjusted = k.sem(f"{tag}_adjusted") if by_dve else None
        slot_read = adjusted if by_dve else exped
        LOADS = 2 * len(Q_PARTS) + (not by_dve)

        @block.sync
        def _(sp):
            sp.wait_ge(padded, 5)
            with sp.Fori(0, HEADS // GH) as hg:
                with sp.Fori(0, BATCH // 2) as bp:
                    for half in range(2):
                        sp.wait_ge(o_out, hg * 8 + bp * 4 + (2 * half + 2))
                        at = bass.ds(bp * (2 * SEQ) + half * SEQ, SEQ)
                        for rows, which, order in ((q_rows, 0, Q_PARTS), (k_rows, int(by_dve), K_PARTS)):
                            for n, part in enumerate(order):
                                src = parts_dram[which, part].rearrange("(h e) t -> e h t", e=HD)
                                sp.dma_start(rows[n * HD:(n + 1) * HD, half, :, :],
                                             src[:, bass.ds(hg * GH, GH), at]).then_inc(loaded[half], 16)
                        if not by_dve:
                            sp.dma_start(q_rows[SHIFT_ROW:SHIFT_ROW + 1, half, :, :],
                                         shift_dram.unsqueeze(0)[:, bass.ds(hg * GH, GH), at]
                                         ).then_inc(loaded[half], 16)

        @block.gpsimd
        def _(pool):
            pool.memset(v_cols[:], 0.0).then_inc(padded, 1)
            pool.wait_ge(padded, 3)
            pool.memset(v_cols[:, :, :, :, HD:HD + 1], 1.0).then_inc(padded, 1)
            pool.wait_ge(padded, 5)
            with pool.Fori(0, HEADS // GH) as hg:
                with pool.Fori(0, BATCH // 2) as bp:
                    for half in range(2):
                        pool.wait_ge(o_out, hg * 8 + bp * 4 + (2 * half + 2))
                        src = V[:, bass.ds(bp * (2 * TPB) + half * TPB, TPB), bass.ds(hg * (GH * HD), GH * HD)]
                        pool.tensor_copy(v_cols[:, half, :, :, 0:HD],
                                         src.rearrange("p t (h e) -> p t h e", e=HD)).then_inc(v_set, 1)

        @block.tensor
        def _(pe):
            pe.sem_inc(summed, 2)

            def scores(half, n, i):
                g = i * 2 + half
                J, j = divmod(n, GH)
                if n == 0:
                    pe.wait_ge(loaded[half], i * (16 * LOADS) + 16 * LOADS)
                back = n - SLOTS if n >= SLOTS else max(m for m in range(-SLOTS, 0) if (m + UNITS) % SLOTS == n)
                pe.wait_ge(slot_read, g * UNITS + (back + 1 + SLOTS))
                for c in range(2):
                    last = pe.matmul(s_ps[:, n % SLOTS, c * BANK:(c + 1) * BANK],
                                     k_rows[:, half, j, J * P:(J + 1) * P],
                                     q_rows[:, half, j, c * BANK:(c + 1) * BANK], start=True, stop=True)
                last.then_inc(scored, 1)

            def sum_up(half, J, c, i):
                g = i * 2 + half
                if c == 0:
                    if J == 0:
                        pe.wait_ge(o_out, g * 2 + 4)
                        pe.wait_ge(v_set, g + 1)
                    pe.wait_ge(exped, g * UNITS + (GH * (J + 1) + SLOTS))
                for j in range(GH):
                    last = pe.matmul(o_ps[VW * j:VW * (j + 1), c, :], v_cols[:, half, J, j, :],
                                     probs[:, J % 2, j, c * BANK:(c + 1) * BANK], start=(J == 0),
                                     stop=(J == JT - 1))
                if c == 1:
                    last.then_inc(summed, 1)

            def pair(i, final):
                for half in range(2):
                    for n in range(UNITS):
                        m = n + SLOTS
                        if m < UNITS:
                            scores(half, m, i)
                        elif half == 0:
                            scores(1, m - UNITS, i)
                        elif not final:
                            scores(0, m - UNITS, i + 1)
                        if n % GH == GH - 1:
                            sum_up(half, n // GH, 0, i)
                            if n + 1 == UNITS:
                                sum_up(half, n // GH, 1, i)
                        if n % GH == 1 and n > GH:
                            sum_up(half, n // GH - 1, 1, i)

            pe.wait_ge(padded, 5)
            for n in range(SLOTS):
                scores(0, n, 0)
            with pe.Fori(0, NG // 2 - 1) as i:
                pair(i, False)
            pair(NG // 2 - 1, True)

        @block.scalar
        def _(act):
            act.sem_inc(exped, SLOTS)
            with act.Fori(0, NG) as g:
                for n in range(UNITS):
                    J, j = divmod(n, GH)
                    if by_dve:
                        act.wait_ge(adjusted, g * UNITS + (n + 1 + SLOTS))
                        act.activation(probs[:, J % 2, j, :], probs[:, J % 2, j, :],
                                       ACT.Exp).then_inc(exped, 1)
                        continue
                    act.wait_ge(scored, g * UNITS + (n + 1))
                    if j == 0:
                        act.wait_ge(summed, g * JT + (J + 1))
                    act.activation(probs[:, J % 2, j, :], s_ps[:, n % SLOTS, :], ACT.Exp).then_inc(exped, 1)
                if by_dve:
                    act.wait_ge(summed, g * JT + (JT + 2))
                    for c in range(2):
                        dst = out_t[:, bass.ds(g, 1), c * BANK:(c + 1) * BANK].rearrange("p o q -> p (o q)")
                        act.copy(dst, o_ps[:, c, :]).then_inc(o_out, 1)

        @block.vector
        def _(dve):
            dve.memset(q_rows[:].bitcast(F32), 0.0).then_inc(padded, 1)
            dve.memset(k_rows[:].bitcast(F32), 0.0).then_inc(padded, 1)
            dve.wait_ge(padded, 3)
            dve.memset(k_rows[SHIFT_ROW:SHIFT_ROW + 1, :, :, :], 1.0).then_inc(padded, 1)
            dve.sem_inc(o_out, 4)
            if not by_dve:
                with dve.Fori(0, NG) as g:
                    dve.wait_ge(summed, g * JT + (JT + 2))
                    for c in range(2):
                        dst = out_t[:, bass.ds(g, 1), c * BANK:(c + 1) * BANK].rearrange("p o q -> p (o q)")
                        dve.tensor_copy(dst, o_ps[:, c, :]).then_inc(o_out, 1)
                return
            dve.sem_inc(adjusted, SLOTS)
            with dve.Fori(0, HEADS // GH) as hg:
                with dve.Fori(0, BATCH) as b:
                    g = hg * BATCH + b
                    for n in range(UNITS):
                        J, j = divmod(n, GH)
                        dve.wait_ge(scored, g * UNITS + (n + 1))
                        if j == 0:
                            dve.wait_ge(summed, g * JT + (J + 1))
                        near = table[:, SEQ - P - J * P:2 * SEQ - P - J * P]
                        out, scores_ = probs[:, J % 2, j, :], s_ps[:, n % SLOTS, :]
                        if slopes is None:
                            ins = dve.tensor_tensor(out, scores_, near, ALU.mult)
                        else:
                            ins = dve.scalar_tensor_tensor(out=out, in0=near, scalar=slopes[:, bass.ds(hg * GH + j, 1)],
                                                           in1=scores_, op0=ALU.mult, op1=ALU.add)
                        ins.then_inc(adjusted, 1)


def normalise(nc, tag, out_t, out_all, ident):
    NH = HEADS // GH
    with ExitStack() as stack:
        k = Kit(nc, stack)
        inv = k.sb(f"{tag}_inv", [P, TILES, HEADS])
        t_ps = k.ps(f"{tag}_t_ps", [P, 4, NH, P])
        turned = k.sem(f"{tag}_turned")
        inverted = k.sem(f"{tag}_inverted")
        normed = k.sem(f"{tag}_normed")
        block = stack.enter_context(nc.Block())

        @block.tensor
        def _(pe):
            for t in range(TILES):
                b, qt = divmod(t, TPB)
                if t >= 4:
                    pe.wait_ge(normed, t - 3)
                for hg in range(NH):
                    last = pe.transpose(t_ps[:, t % 4, hg, :], out_t[:, hg * BATCH + b, qt * P:(qt + 1) * P], ident)
                last.then_inc(turned, 1)

        @block.vector
        def _(dve):
            for t in range(TILES):
                heads = t_ps[:, t % 4, :, :].rearrange("p g (h e) -> p (g h) e", e=VW)
                dve.wait_ge(turned, t + 1)
                dve.reciprocal(inv[:, t, :], heads[:, :, HD]).then_inc(inverted, 1)
                dve.wait_ge(inverted, t + 1)
                dve.tensor_tensor(out_all[:, t, :].rearrange("p (h e) -> p h e", e=HD), heads[:, :, 0:HD],
                                  over(inv[:, t, :], HD), ALU.mult).then_inc(normed, 1)


def project_out(nc, tag, out_all, w_out, b_out, X, ident):
    with ExitStack() as stack:
        k = Kit(nc, stack)
        out_t = k.sb(f"{tag}_out_t", [P, 2, 4, P])
        t_ps = k.ps(f"{tag}_t_ps", [P, 2, 4, P])
        y_ps = k.ps(f"{tag}_y_ps", [P, 2, 4, D])
        turned = k.sem(f"{tag}_turned")
        copied = k.sem(f"{tag}_copied")
        projected = k.sem(f"{tag}_projected")
        biased = k.sem(f"{tag}_biased")
        added = k.sem(f"{tag}_added")
        block = stack.enter_context(nc.Block())
        STEPS = TILES // 4

        @block.tensor
        def _(pe):
            def turn(s):
                if s >= 2:
                    pe.wait_ge(copied, s - 1)
                for t in range(4):
                    last = pe.transpose(t_ps[:, s % 2, t, :], out_all[:, 4 * s + t, :], ident)
                last.then_inc(turned, 1)
            turn(0)
            for s in range(STEPS):
                if s + 1 < STEPS:
                    turn(s + 1)
                pe.wait_ge(copied, s + 1)
                if s >= 2:
                    pe.wait_ge(added, s - 1)
                for t in range(4):
                    last = pe.matmul(y_ps[:, s % 2, t, :], out_t[:, s % 2, t, :], w_out, start=True, stop=True)
                last.then_inc(projected, 1)

        @block.scalar
        def _(act):
            for s in range(STEPS):
                act.wait_ge(turned, s + 1)
                if s >= 2:
                    act.wait_ge(projected, s - 1)
                act.copy(out_t[:, s % 2, :, :], t_ps[:, s % 2, :, :]).then_inc(copied, 1)

        @block.vector
        def _(dve):
            for s in range(STEPS):
                x = X[:, 4 * s:4 * s + 4, :]
                dve.tensor_tensor(x, x, over_mid(b_out, 4), ALU.add).then_inc(biased, 1)
                dve.wait_ge(projected, s + 1)
                dve.wait_ge(biased, s + 1)
                dve.tensor_tensor(x, x, y_ps[:, s % 2, :, :], ALU.add).then_inc(added, 1)


def alibi_slopes():
    start = 2.0 ** (-2.0 ** (-(math.log2(HEADS) - 3)))
    return [start ** i for i in range(HEADS)]


def distances(nc, tag, k, distance):
    distance = distance[:, :]
    whole = k.sb(f"{tag}_whole", [P, WIN], I32)
    counted = k.sem(f"{tag}_counted")
    made = k.sem(f"{tag}_made")
    with nc.Block() as block:
        @block.gpsimd
        def _(pool):
            pool.iota(whole[:, :], pattern=[[1, WIN]], base=-(SEQ - P), channel_multiplier=-1).then_inc(counted, 1)

        @block.vector
        def _(dve):
            dve.wait_ge(counted, 1)
            dve.tensor_copy(distance[:, :], whole[:, :]).then_inc(made, 1)

        @block.scalar
        def _(act):
            act.wait_ge(made, 1)
            act.activation(distance[:, :], distance[:, :], ACT.Abs).then_inc(made, 1)


def attention_layer(nc, tag, X, w, ident, parts_dram, head_of, attend_all):
    with ExitStack() as stack:
        k = Kit(nc, stack)
        XN = k.sb(f"{tag}_XN", [P, TILES, D])
        V = k.sb(f"{tag}_V", [P, TILES, D])
        longest2 = k.sb(f"{tag}_longest2", [HEADS, 2, TOK // CHUNK])
        wide = k.sb(f"{tag}_wide", [1, 1], I32)
        with ExitStack() as inner:
            XT = Kit(nc, inner).sb(f"{tag}_XT", [P, TOK])
            layer_norm(nc, f"{tag}_ln", X, XN, XT, ident)
            project_qkv(nc, f"{tag}_qkv", XT, w["qkv"], w["b_qk"], w["b_v"], V, parts_dram,
                        1.0 / math.sqrt(HD), head_of, longest2)
        bound_scores(nc, f"{tag}_bound", longest2, wide, ident)
        attend_all(wide, V, XN)
        project_out(nc, f"{tag}_out", XN, w["out"], w["b_out"], X, ident)


def choose(nc, tag, wide, direct, general):
    is_wide = nc.values_load(wide[0:1, 0:1], min_val=0, max_val=1)
    with nc.If(is_wide == 1):
        general()
    with nc.Else():
        direct()


def alibi_attention(nc, tag, X, w, ident, parts_dram, head_of):
    def attend_all(wide, V, out):
        with ExitStack() as stack:
            k = Kit(nc, stack)
            distance = k.sb(f"{tag}_distance", [P, WIN])
            slopes = k.sb(f"{tag}_slopes", [P, HEADS])
            free = k.sem(f"{tag}_table_free")
            with ExitStack() as small:
                distances(nc, f"{tag}_dist", Kit(nc, small), distance)
            with nc.Block() as block:
                @block.vector
                def _(dve):
                    for h, s in enumerate(alibi_slopes()):
                        dve.memset(slopes[:, h:h + 1], -s)

            def direct():
                with ExitStack() as inner:
                    out_t = Kit(nc, inner).sb(f"{tag}_out_t", [P, (HEADS // GH) * BATCH, SEQ])
                    attend_transposed(nc, f"{tag}_direct", V, parts_dram, out_t, table=distance, slopes=slopes)
                    normalise(nc, f"{tag}_norm", out_t, out, ident)

            def general():
                with ExitStack() as inner:
                    table = Kit(nc, inner).sb(f"{tag}_table", [P, GH, WIN])
                    attend(nc, f"{tag}_att", V, parts_dram, {"buffer": table, "per_group": True,
                           "distance": distance, "slopes": slopes, "free": free}, ALU.add, out, ident)
            choose(nc, tag, wide, direct, general)
    attention_layer(nc, tag, X, w, ident, parts_dram, head_of, attend_all)


def decay_attention(nc, tag, X, w, ident, parts_dram, head_of):
    def attend_all(wide, V, out):
        with ExitStack() as stack:
            k2 = Kit(nc, stack)
            table = k2.sb(f"{tag}_table", [P, 1, WIN])
            with ExitStack() as small:
                k3 = Kit(nc, small)
                distances(nc, f"{tag}_dist", k3, table[:, 0, :])
                rate = k3.sb(f"{tag}_rate", [P, 1])
                rate_set = k3.sem(f"{tag}_rate_set")
                with nc.Block() as block:
                    @block.scalar
                    def _(act):
                        act.activation(rate[:, :], w["decay"], ACT.Abs).then_inc(rate_set, 1)
                        act.wait_ge(rate_set, 1)
                        act.mul(rate[:, :], rate[:, :], -1.0).then_inc(rate_set, 1)
                        act.wait_ge(rate_set, 2)
                        act.activation(table[:, 0, :], table[:, 0, :], ACT.Exp, scale=rate[:, 0:1])

            def direct():
                with ExitStack() as inner:
                    out_t = Kit(nc, inner).sb(f"{tag}_out_t", [P, (HEADS // GH) * BATCH, SEQ])
                    attend_transposed(nc, f"{tag}_direct", V, parts_dram, out_t, table=table[:, 0, :])
                    normalise(nc, f"{tag}_norm", out_t, out, ident)

            def general():
                attend(nc, f"{tag}_att", V, parts_dram, {"buffer": table}, ALU.mult, out, ident)
            choose(nc, tag, wide, direct, general)
    attention_layer(nc, tag, X, w, ident, parts_dram, head_of, attend_all)


def centred_attention(nc, tag, X, ident, parts_dram, shift_dram, head_of):
    with ExitStack() as stack:
        k = Kit(nc, stack)
        XN = k.sb(f"{tag}_XN", [P, TILES, D])
        with ExitStack() as inner:
            XT = Kit(nc, inner).sb(f"{tag}_XT", [P, TOK])
            layer_norm(nc, f"{tag}_ln", X, XN, XT, ident)
            centre_and_split(nc, f"{tag}_split", XT, parts_dram, shift_dram, head_of)
        out_t = k.sb(f"{tag}_out_t", [P, (HEADS // GH) * BATCH, SEQ])
        attend_transposed(nc, f"{tag}_att", XN, parts_dram, out_t, shift_dram=shift_dram)
        normalise(nc, f"{tag}_norm", out_t, XN, ident)
        with nc.Block() as block:
            @block.vector
            def _(dve):
                dve.tensor_tensor(X[:, :, :], X[:, :, :], XN[:, :, :], ALU.add)


def centre_and_split(nc, tag, XT, parts_dram, shift_dram, head_of):
    with ExitStack() as stack:
        k = Kit(nc, stack)
        total = k.sb(f"{tag}_total", [P, BATCH])
        rest = k.sb(f"{tag}_rest", [P, TOK])
        parts = k.sb(f"{tag}_parts", [P, 3, TOK], BF16)
        squares = k.sb(f"{tag}_squares", [P, TOK])
        norm2 = k.sb(f"{tag}_norm2", [HEADS, TOK])
        norm = k.sb(f"{tag}_norm", [HEADS, TOK])
        longest = k.sb(f"{tag}_longest", [HEADS, BATCH])
        shift = k.sb(f"{tag}_shift", [HEADS, TOK], BF16)
        norm_ps = k.ps(f"{tag}_norm_ps", [HEADS, TOK])
        step_done = k.sem(f"{tag}_step_done")
        centred = k.sem(f"{tag}_centred")
        part1 = k.sem(f"{tag}_part1")
        rest1 = k.sem(f"{tag}_rest1")
        part2 = k.sem(f"{tag}_part2")
        part3 = k.sem(f"{tag}_part3")
        stored = k.sem(f"{tag}_stored")
        squared = k.sem(f"{tag}_squared")
        norm2_done = k.sem(f"{tag}_norm2_done")
        norm_done = k.sem(f"{tag}_norm_done")
        shift_done = k.sem(f"{tag}_shift_done")
        block = stack.enter_context(nc.Block())
        cut = [slice(b * SEQ, (b + 1) * SEQ) for b in range(BATCH)]

        @block.vector
        def _(dve):
            link = counter(dve, step_done)
            for b, c in enumerate(cut):
                link(dve.tensor_reduce(total[:, b:b + 1], XT[:, c], AX, ALU.add))
                link(dve.tensor_scalar(total[:, b:b + 1], total[:, b:b + 1], 1.0 / SEQ, None, ALU.mult))
                dve.tensor_scalar(XT[:, c], XT[:, c], total[:, b:b + 1], None, ALU.subtract).then_inc(centred, 1)
            for b, c in enumerate(cut):
                dve.wait_ge(centred, b + 1)
                dve.wait_ge(part1, b + 1)
                dve.tensor_tensor(rest[:, c], XT[:, c], parts[:, 0, c], ALU.subtract).then_inc(rest1, 1)
            for b, c in enumerate(cut):
                dve.wait_ge(rest1, b + 1)
                dve.wait_ge(part2, b + 1)
                dve.tensor_tensor(parts[:, 2, c], rest[:, c], parts[:, 1, c], ALU.subtract).then_inc(part3, 1)
            for b, c in enumerate(cut):
                dve.wait_ge(norm_done, 2 * (b + 1))
                link(dve.tensor_reduce(longest[:, b:b + 1], norm[:, c], AX, ALU.max))
                link(dve.scalar_tensor_tensor(out=norm[:, c], in0=norm[:, c], scalar=longest[:, b:b + 1],
                                              in1=norm2[:, c], op0=ALU.mult, op1=ALU.add))
                dve.tensor_scalar(shift[:, c], norm[:, c], -0.5, None, ALU.mult).then_inc(shift_done, 1)

        @block.tensor
        def _(pe):
            for n in range(TOK // BANK):
                pe.wait_ge(squared, n // (SEQ // BANK) + 1)
                pe.matmul(norm_ps[:, n * BANK:(n + 1) * BANK], head_of, squares[:, n * BANK:(n + 1) * BANK],
                          start=True, stop=True).then_inc(norm2_done, 1)

        @block.scalar
        def _(act):
            for b, c in enumerate(cut):
                act.wait_ge(centred, b + 1)
                act.copy(parts[:, 0, c], XT[:, c]).then_inc(part1, 1)
                act.activation(squares[:, c], XT[:, c], ACT.Square).then_inc(squared, 1)
            for b, c in enumerate(cut):
                act.wait_ge(rest1, b + 1)
                act.copy(parts[:, 1, c], rest[:, c]).then_inc(part2, 1)
            for b, c in enumerate(cut):
                act.wait_ge(norm2_done, (b + 1) * (SEQ // BANK))
                act.activation(norm[:, c], norm_ps[:, c], ACT.Sqrt).then_inc(norm_done, 1)
                act.copy(norm2[:, c], norm_ps[:, c]).then_inc(norm_done, 1)

        @block.sync
        def _(sp):
            for b, c in enumerate(cut):
                sp.wait_ge(part3, b + 1)
                sp.dma_start(parts_dram[0].rearrange("s f t -> f s t")[:, :, c], parts[:, :, c]).then_inc(stored, 16)
            for b, c in enumerate(cut):
                sp.wait_ge(shift_done, b + 1)
                sp.dma_start(shift_dram[:, c], shift[:, c]).then_inc(stored, 16)
            sp.wait_ge(stored, 16 * 2 * BATCH)


GROUPS, PER_GROUP = 4, 2
EXPERTS = GROUPS * PER_GROUP
F = 256
FT = EXPERTS * F // P
HALVES = F // P
GATES = GROUPS + EXPERTS
LOOPS = 2
RMS_EPS = 1e-6
GATE_EPS = 1e-9


def route(nc, tag, Z, ZT, combine, w, ident):
    GROUP = 8
    STEPS = TILES // GROUP
    with ExitStack() as stack:
        k = Kit(nc, stack)
        scratch = k.sb(f"{tag}_scratch", [P, TILES, D])
        ms = k.sb(f"{tag}_ms", [P, TILES])
        std = k.sb(f"{tag}_std", [P, TILES])
        rstd = k.sb(f"{tag}_rstd", [P, TILES])
        eps = k.sb(f"{tag}_eps", [P, 1])
        logits = k.sb(f"{tag}_logits", [P, TILES, GATES])
        exps = k.sb(f"{tag}_exps", [P, TILES, GATES])
        top = k.sb(f"{tag}_top", [P, TILES, 1 + GROUPS])
        total = k.sb(f"{tag}_total", [P, TILES, 1 + GROUPS])
        beats = k.sb(f"{tag}_beats", [P, TILES, GROUPS, GROUPS])
        ties = k.sb(f"{tag}_ties", [P, TILES, GROUPS, GROUPS])
        rank = k.sb(f"{tag}_rank", [P, TILES, GROUPS])
        pair = k.sb(f"{tag}_pair", [P, TILES])
        best = k.sb(f"{tag}_best", [P, TILES, GROUPS])
        inv_best = k.sb(f"{tag}_inv_best", [P, TILES, GROUPS])
        second = k.sb(f"{tag}_second", [P, TILES, GROUPS])
        turned_ps = k.ps(f"{tag}_turned_ps", [P, 2, GROUP, P])
        gate_ps = k.ps(f"{tag}_gate_ps", [P, BANK])
        step_done = k.sem(f"{tag}_step_done")
        squared = k.sem(f"{tag}_squared")
        ms_ready = k.sem(f"{tag}_ms_ready")
        std_ready = k.sem(f"{tag}_std_ready")
        normed = k.sem(f"{tag}_normed")
        turned = k.sem(f"{tag}_turned")
        copied = k.sem(f"{tag}_copied")
        gated = k.sem(f"{tag}_gated")
        shifted = k.sem(f"{tag}_shifted")
        exped = k.sem(f"{tag}_exped")
        block = stack.enter_context(nc.Block())
        cut = [slice(GROUP * s, GROUP * (s + 1)) for s in range(STEPS)]

        @block.scalar
        def _(act):
            for s, c in enumerate(cut):
                act.activation(scratch[:, c, :], Z[:, c, :], ACT.Square).then_inc(squared, 1)
            for s, c in enumerate(cut):
                act.wait_ge(ms_ready, s + 1)
                act.activation(std[:, c], ms[:, c], ACT.Sqrt, bias=eps[:, 0:1],
                               scale=1.0 / D).then_inc(std_ready, 1)
            for s in range(STEPS):
                act.wait_ge(turned, s + 1)
                act.activation(ZT[:, GROUP * P * s:GROUP * P * (s + 1)],
                               turned_ps[:, s % 2, :, :].rearrange("p t q -> p (t q)"), ACT.Copy,
                               scale=w["norm"]).then_inc(copied, 1)
            act.wait_ge(shifted, 1)
            act.activation(exps[:, :, :], logits[:, :, :], ACT.Exp).then_inc(exped, 1)

        @block.tensor
        def _(pe):
            for s in range(STEPS):
                pe.wait_ge(normed, s + 1)
                if s >= 2:
                    pe.wait_ge(copied, s - 1)
                for t in range(GROUP):
                    last = pe.transpose(turned_ps[:, s % 2, t, :], scratch[:, GROUP * s + t, :], ident)
                last.then_inc(turned, 1)
            for s in range(STEPS):
                pe.wait_ge(copied, s + 1)
                for t in range(GROUP * s, GROUP * (s + 1)):
                    last = pe.matmul(gate_ps[:, t * GATES:(t + 1) * GATES], ZT[:, t * P:(t + 1) * P], w["gates"],
                                     start=True, stop=True)
            last.then_inc(gated, 1)

        @block.vector
        def _(dve):
            link = counter(dve, step_done)
            link(dve.memset(eps[:], RMS_EPS))
            for s, c in enumerate(cut):
                dve.wait_ge(squared, s + 1)
                dve.tensor_reduce(ms[:, c], scratch[:, c, :], AX, ALU.add).then_inc(ms_ready, 1)
            for s, c in enumerate(cut):
                dve.wait_ge(std_ready, s + 1)
                link(dve.reciprocal(rstd[:, c], std[:, c]))
                dve.tensor_tensor(scratch[:, c, :], Z[:, c, :], over(rstd[:, c], D), ALU.mult).then_inc(normed, 1)
            dve.wait_ge(gated, 1)
            link(dve.tensor_copy(logits[:, :, :],
                                 gate_ps[:, 0:TILES * GATES].rearrange("p (t g) -> p t g", g=GATES)))
            fine = logits[:, :, GROUPS:].rearrange("p t (g e) -> p t g e", e=PER_GROUP)
            link(dve.tensor_reduce(top[:, :, 0], logits[:, :, 0:GROUPS], AX, ALU.max))
            link(dve.tensor_reduce(top[:, :, 1:], fine, AX, ALU.max))
            link(dve.tensor_tensor(logits[:, :, 0:GROUPS], logits[:, :, 0:GROUPS], over(top[:, :, 0], GROUPS),
                                   ALU.subtract))
            dve.tensor_tensor(fine, fine, over(top[:, :, 1:], PER_GROUP), ALU.subtract).then_inc(shifted, 1)
            dve.wait_ge(exped, 1)
            coarse = exps[:, :, 0:GROUPS]
            fine = exps[:, :, GROUPS:].rearrange("p t (g e) -> p t g e", e=PER_GROUP)
            link(dve.tensor_reduce(total[:, :, 0], coarse, AX, ALU.add))
            link(dve.tensor_reduce(total[:, :, 1:], fine, AX, ALU.add))
            link(dve.reciprocal(total[:, :, :], total[:, :, :]))
            link(dve.tensor_tensor(coarse, coarse, over(total[:, :, 0], GROUPS), ALU.mult))
            link(dve.tensor_tensor(fine, fine, over(total[:, :, 1:], PER_GROUP), ALU.mult))
            mine = over(coarse, GROUPS)
            others = coarse.unsqueeze(2).to_broadcast([P, TILES, GROUPS, GROUPS])
            before = w["before"].unsqueeze(1).to_broadcast([P, TILES, GROUPS, GROUPS])
            link(dve.tensor_tensor(beats[:, :, :, :], others, mine, ALU.is_gt))
            link(dve.tensor_tensor(ties[:, :, :, :], others, mine, ALU.is_equal))
            link(dve.tensor_tensor(ties[:, :, :, :], ties[:, :, :, :], before, ALU.mult))
            link(dve.tensor_tensor(beats[:, :, :, :], beats[:, :, :, :], ties[:, :, :, :], ALU.add))
            link(dve.tensor_reduce(rank[:, :, :], beats[:, :, :, :], AX, ALU.add))
            link(dve.tensor_scalar(rank[:, :, :], rank[:, :, :], 2.0, None, ALU.is_lt))
            link(dve.tensor_tensor(rank[:, :, :], rank[:, :, :], coarse, ALU.mult))
            link(dve.tensor_reduce(pair[:, :], rank[:, :, :], AX, ALU.add))
            link(dve.tensor_scalar(pair[:, :], pair[:, :], GATE_EPS, None, ALU.add))
            link(dve.reciprocal(pair[:, :], pair[:, :]))
            link(dve.tensor_tensor(rank[:, :, :], rank[:, :, :], over(pair[:, :], GROUPS), ALU.mult))
            link(dve.tensor_reduce(best[:, :, :], fine, AX, ALU.max))
            link(dve.tensor_scalar(inv_best[:, :, :], best[:, :, :], GATE_EPS, None, ALU.add))
            link(dve.reciprocal(inv_best[:, :, :], inv_best[:, :, :]))
            link(dve.tensor_tensor(best[:, :, :], best[:, :, :], inv_best[:, :, :], ALU.mult))
            link(dve.tensor_tensor(rank[:, :, :], rank[:, :, :], best[:, :, :], ALU.mult))
            link(dve.tensor_tensor(second[:, :, :], fine[:, :, :, 1], fine[:, :, :, 0], ALU.is_gt))
            out = combine[:, :, :].rearrange("p t (g e) -> p t g e", e=PER_GROUP)
            link(dve.tensor_tensor(out[:, :, :, 1], rank[:, :, :], second[:, :, :], ALU.mult))
            link(dve.tensor_tensor(out[:, :, :, 0], rank[:, :, :], out[:, :, :, 1], ALU.subtract))


def experts(nc, tag, Z, ZT, combine, w):
    CT = CHUNK // P
    UP_BANKS = 4
    with ExitStack() as stack:
        k = Kit(nc, stack)
        hidden = k.sb(f"{tag}_hidden", [P, FT, CHUNK])
        weighted = k.sb(f"{tag}_weighted", [P, EXPERTS, D])
        mixed = k.sb(f"{tag}_mixed", [P, D])
        up_ps = k.ps(f"{tag}_up_ps", [P, UP_BANKS, BANK])
        down_ps = k.ps(f"{tag}_down_ps", [P, 2, EXPERTS, D])
        up_done = k.sem(f"{tag}_up_done")
        silu_done = k.sem(f"{tag}_silu_done")
        down_done = k.sem(f"{tag}_down_done")
        down_out = k.sem(f"{tag}_down_out")
        summed = k.sem(f"{tag}_summed")
        z_added = k.sem(f"{tag}_z_added")
        block = stack.enter_context(nc.Block())

        @block.tensor
        def _(pe):
            with pe.Fori(0, TOK // CHUNK) as c:
                for f in range(FT):
                    if f >= UP_BANKS:
                        pe.wait_ge(silu_done, c * FT + (f - UP_BANKS + 1))
                    pe.matmul(up_ps[:, f % UP_BANKS, :], w["w1"][:, f * P:(f + 1) * P],
                              ZT[:, bass.ds(c * CHUNK, CHUNK)], start=True, stop=True).then_inc(up_done, 1)
                pe.wait_ge(silu_done, c * FT + FT)
                for t in range(CT):
                    pe.wait_ge(down_out, c * CT + (t + 1))
                    for e in range(EXPERTS):
                        for h in range(HALVES):
                            last = pe.matmul(down_ps[:, t % 2, e, :],
                                             hidden[:, e * HALVES + h, t * P:(t + 1) * P],
                                             w["w2"][:, e * HALVES + h, :], start=(h == 0),
                                             stop=(h == HALVES - 1))
                    last.then_inc(down_done, 1)

        @block.scalar
        def _(act):
            with act.Fori(0, TOK // CHUNK) as c:
                for f in range(FT):
                    act.wait_ge(up_done, c * FT + (f + 1))
                    act.activation(hidden[:, f, :], up_ps[:, f % UP_BANKS, :], ACT.Silu).then_inc(silu_done, 1)

        @block.vector
        def _(dve):
            dve.sem_inc(down_out, 2)
            with dve.Fori(0, TOK // CHUNK) as c:
                for t in range(CT):
                    n = c * CT + t
                    dve.wait_ge(down_done, n + 1)
                    gate = combine[:, bass.ds(n, 1), :].rearrange("p o e -> p (o e)")
                    dve.tensor_tensor(weighted[:, :, :], down_ps[:, t % 2, :, :], over(gate, D),
                                      ALU.mult).then_inc(down_out, 1)
                    dve.wait_ge(down_out, n + 3)
                    dve.tensor_reduce(mixed[:, :], weighted[:, :, :].rearrange("p e d -> p d e"), AX,
                                      ALU.add).then_inc(summed, 1)
                    dve.wait_ge(summed, n + 1)
                    z = Z[:, bass.ds(n, 1), :].rearrange("p o d -> p (o d)")
                    dve.tensor_tensor(z, z, mixed[:, :], ALU.add).then_inc(z_added, 1)
                    dve.wait_ge(z_added, n + 1)


def moe_ffn(nc, tag, X, w, ident):
    with ExitStack() as stack:
        k = Kit(nc, stack)
        Z = k.sb(f"{tag}_Z", [P, TILES, D])
        ZT = k.sb(f"{tag}_ZT", [P, TOK])
        combine = k.sb(f"{tag}_combine", [P, TILES, EXPERTS])
        layer_norm(nc, f"{tag}_ln", X, Z, None, ident)
        for loop in range(LOOPS):
            route(nc, f"{tag}_route{loop}", Z, ZT, combine, w, ident)
            experts(nc, f"{tag}_experts{loop}", Z, ZT, combine, w)
        with nc.Block() as block:
            @block.vector
            def _(dve):
                dve.tensor_tensor(X[:, :, :], X[:, :, :], Z[:, :, :], ALU.add)


STEPS = BATCH
FH, FD = 16, 64
FW = FH * FD


def fast_weights(nc, tag, X, w, ident):
    with ExitStack() as stack:
        k = Kit(nc, stack)
        H = k.sb(f"{tag}_H", [P, TILES, D])
        HT = k.sb(f"{tag}_HT", [P, TOK])
        layer_norm(nc, f"{tag}_ln", X, H, HT, ident)
        with ExitStack() as inner:
            recur(nc, f"{tag}_recur", Kit(nc, inner), H, HT, w, ident)
        layer_norm(nc, f"{tag}_ln2", H, H, None, ident, gain=w["ln_g"], shift=w["ln_b"])
        with nc.Block() as block:
            @block.vector
            def _(dve):
                dve.tensor_tensor(X[:, :, :], X[:, :, :], H[:, :, :], ALU.add)


def recur(nc, tag, k, H, HT, w, ident):
    BT = TPB
    ht = k.sb(f"{tag}_ht", [P, STEPS, P])
    q = k.sb(f"{tag}_q", [P, STEPS, FW])
    key = k.sb(f"{tag}_k", [P, STEPS, FW])
    v = k.sb(f"{tag}_v", [P, STEPS, FW])
    low = k.sb(f"{tag}_low", [P, 2, FW])
    prod = k.sb(f"{tag}_prod", [P, STEPS, FW])
    mixed = k.sb(f"{tag}_mixed", [P, 2, FW])
    mixed_t = k.sb(f"{tag}_mixed_t", [P, FW // P, P])
    inv_q = k.sb(f"{tag}_inv_q", [P, STEPS, FH])
    inv_k = k.sb(f"{tag}_inv_k", [P, STEPS, FH])
    beta = k.sb(f"{tag}_beta", [P, STEPS, FH])
    kk = k.sb(f"{tag}_kk", [P, STEPS, STEPS, FH])
    kq = k.sb(f"{tag}_kq", [P, STEPS, STEPS, FH])
    lower = k.sb(f"{tag}_lower", [P, STEPS, STEPS, FH])
    coef = k.sb(f"{tag}_coef", [P, STEPS, STEPS, FH])
    term = k.sb(f"{tag}_term", [P, STEPS, FH])
    qkv_ps = k.ps(f"{tag}_qkv_ps", [P, 2, FW])
    beta_ps = k.ps(f"{tag}_beta_ps", [P, BANK])
    turned_ps = k.ps(f"{tag}_turned_ps", [P, FW // P, P])
    y_ps = k.ps(f"{tag}_y_ps", [P, BANK])
    ht_set = k.sem(f"{tag}_ht_set")
    projected = k.sem(f"{tag}_projected")
    beta_done = k.sem(f"{tag}_beta_done")
    beta_exp = k.sem(f"{tag}_beta_exp")
    low_done = k.sem(f"{tag}_low_done")
    chain = k.sem(f"{tag}_chain")
    qk_out = k.sem(f"{tag}_qk_out")
    v_out = k.sem(f"{tag}_v_out")
    act_step = k.sem(f"{tag}_act_step")
    mixed_done = k.sem(f"{tag}_mixed_done")
    turned = k.sem(f"{tag}_turned")
    copied = k.sem(f"{tag}_copied")
    attended = k.sem(f"{tag}_attended")
    added = k.sem(f"{tag}_added")
    block = k.stack.enter_context(nc.Block())
    UNITS = 3 * STEPS

    @block.gpsimd
    def _(pool):
        with pool.Fori(0, BT) as bt:
            pool.wait_ge(projected, bt * UNITS)
            pool.wait_ge(beta_done, bt)
            for s in range(STEPS):
                pool.tensor_copy(ht[:, s, :], HT[:, bass.ds(bt * P + s * SEQ, P)]).then_inc(ht_set, 1)

    @block.tensor
    def _(pe):
        with pe.Fori(0, BT) as bt:
            pe.wait_ge(ht_set, bt * STEPS + STEPS)
            for u in range(UNITS):
                kind, s = divmod(u, STEPS)
                pe.wait_ge(qk_out, bt * (2 * STEPS) + min(2 * STEPS, max(u - 1, 0)))
                if u > 2 * STEPS + 1:
                    pe.wait_ge(v_out, bt * STEPS + (u - 1 - 2 * STEPS))
                if u < 2:
                    pe.wait_ge(v_out, bt * STEPS)
                for c in range(FW // BANK):
                    at = kind * FW + c * BANK
                    last = pe.matmul(qkv_ps[:, u % 2, c * BANK:(c + 1) * BANK], ht[:, s, :],
                                     w["qkv"][:, at:at + BANK], start=True, stop=True)
                last.then_inc(projected, 1)
            for s in range(STEPS):
                last = pe.matmul(beta_ps[:, s * FH:(s + 1) * FH], ht[:, s, :], w["qkv"][:, 3 * FW:3 * FW + FH],
                                 start=True, stop=True)
            last.then_inc(beta_done, 1)
            for t in range(STEPS):
                pe.wait_ge(mixed_done, bt * STEPS + (t + 1))
                pe.wait_ge(copied, bt * STEPS + t)
                for c in range(FW // P):
                    last = pe.transpose(turned_ps[:, c, :], mixed[:, t % 2, c * P:(c + 1) * P], ident)
                last.then_inc(turned, 1)
                pe.wait_ge(copied, bt * STEPS + (t + 1))
                pe.wait_ge(added, bt * STEPS + t)
                for c in range(FW // P):
                    last = pe.matmul(y_ps[:, 0:D], mixed_t[:, c, :], w["out"][:, c, :], start=(c == 0),
                                     stop=(c == FW // P - 1))
                last.then_inc(attended, 1)

    @block.scalar
    def _(act):
        with act.Fori(0, BT) as bt:
            for u in range(UNITS):
                kind, s = divmod(u, STEPS)
                act.wait_ge(projected, bt * UNITS + (u + 1))
                if kind == 2:
                    act.copy(v[:, s, :], qkv_ps[:, u % 2, :]).then_inc(v_out, 1)
                    continue
                act.wait_ge(qk_out, bt * (2 * STEPS) + max(u - 1, 0))
                act.activation(low[:, u % 2, :], qkv_ps[:, u % 2, :], ACT.Relu, scale=-1.0).then_inc(act_step, 1)
                act.wait_ge(act_step, bt * (2 * STEPS) + (u + 1))
                act.activation(low[:, u % 2, :], low[:, u % 2, :], ACT.Exp, scale=-1.0).then_inc(low_done, 1)
            act.wait_ge(beta_done, bt + 1)
            act.activation(beta[:, :, :], beta_ps[:, 0:STEPS * FH].rearrange("p (s h) -> p s h", h=FH), ACT.Exp,
                           scale=-1.0).then_inc(beta_exp, 1)
            for t in range(STEPS):
                act.wait_ge(turned, bt * STEPS + (t + 1))
                act.wait_ge(attended, bt * STEPS + t)
                act.copy(mixed_t[:, :, :], turned_ps[:, :, :]).then_inc(copied, 1)

    def heads(ap):
        return ap.rearrange("p s (h e) -> p s h e", e=FD)

    @block.vector
    def _(dve):
        LINKS = 79
        with dve.Fori(0, BT) as bt:
            link = counter(dve, chain, bt * LINKS)
            for u in range(2 * STEPS):
                kind, s = divmod(u, STEPS)
                dve.wait_ge(low_done, bt * (2 * STEPS) + (u + 1))
                dve.scalar_tensor_tensor(out=(q, key)[kind][:, s, :], in0=qkv_ps[:, u % 2, :], scalar=0.0,
                                         in1=low[:, u % 2, :], op0=ALU.max, op1=ALU.add).then_inc(qk_out, 1)
            dve.wait_ge(qk_out, bt * (2 * STEPS) + 2 * STEPS)
            for src, inv in ((q, inv_q), (key, inv_k)):
                link(dve.tensor_reduce(inv[:, :, :], heads(src[:, :, :]), AX, ALU.add))
                link(dve.reciprocal(inv[:, :, :], inv[:, :, :]))
            link(dve.tensor_scalar(inv_q[:, :, :], inv_q[:, :, :], FD ** -0.5, None, ALU.mult))
            dve.wait_ge(beta_exp, bt + 1)
            link(dve.tensor_scalar(beta[:, :, :], beta[:, :, :], 1.0, None, ALU.add))
            link(dve.reciprocal(beta[:, :, :], beta[:, :, :]))
            for t in range(STEPS):
                for dots, other, inv, n in ((kk, key, inv_k, t), (kq, q, inv_q, t + 1)):
                    if n == 0:
                        continue
                    link(dve.tensor_tensor(prod[:, 0:n, :], key[:, 0:n, :],
                                           other[:, t:t + 1, :].to_broadcast([P, n, FW]), ALU.mult))
                    link(dve.tensor_reduce(dots[:, t, 0:n, :], heads(prod[:, 0:n, :]), AX, ALU.add))
                    link(dve.tensor_tensor(dots[:, t, 0:n, :], dots[:, t, 0:n, :], inv_k[:, 0:n, :], ALU.mult))
                    link(dve.tensor_tensor(dots[:, t, 0:n, :], dots[:, t, 0:n, :],
                                           inv[:, t:t + 1, :].to_broadcast([P, n, FH]), ALU.mult))
            for t in range(STEPS):
                link(dve.tensor_copy(lower[:, t, t, :], beta[:, t, :]))
                for s in range(t):
                    n = s + 1
                    by = kk[:, t, s:s + 1, :].to_broadcast([P, n, FH])
                    if s == 0:
                        link(dve.memset(lower[:, t, 0:t, :], 0.0))
                    link(dve.tensor_tensor(term[:, 0:n, :], lower[:, s, 0:n, :], by, ALU.mult))
                    link(dve.tensor_tensor(lower[:, t, 0:n, :], lower[:, t, 0:n, :], term[:, 0:n, :],
                                           ALU.subtract))
                if t:
                    link(dve.tensor_tensor(lower[:, t, 0:t, :], lower[:, t, 0:t, :],
                                           beta[:, t:t + 1, :].to_broadcast([P, t, FH]), ALU.mult))
            for t in range(STEPS):
                for s in range(t, -1, -1):
                    n = s + 1
                    by = kq[:, t, s:s + 1, :].to_broadcast([P, n, FH])
                    if s == t:
                        link(dve.tensor_tensor(coef[:, t, 0:n, :], lower[:, s, 0:n, :], by, ALU.mult))
                    else:
                        link(dve.tensor_tensor(term[:, 0:n, :], lower[:, s, 0:n, :], by, ALU.mult))
                        link(dve.tensor_tensor(coef[:, t, 0:n, :], coef[:, t, 0:n, :], term[:, 0:n, :], ALU.add))
                n = t + 1
                if t == 0:
                    dve.wait_ge(v_out, bt * STEPS + STEPS)
                dve.wait_ge(turned, bt * STEPS + max(t - 1, 0))
                by = over(coef[:, t, 0:n, :], FD)
                dst = mixed[:, t % 2:t % 2 + 1, :] if t == 0 else prod[:, 0:n, :]
                scaled = dve.tensor_tensor(heads(dst), heads(v[:, 0:n, :]), by, ALU.mult)
                for r in range(1, n):
                    link(scaled)
                    a = prod[:, 0, :] if r == 1 else mixed[:, t % 2, :]
                    scaled = dve.tensor_tensor(mixed[:, t % 2, :], a, prod[:, r, :], ALU.add)
                scaled.then_inc(mixed_done, 1)
                dve.wait_ge(mixed_done, bt * STEPS + (t + 1))
            for t in range(STEPS):
                dve.wait_ge(attended, bt * STEPS + (t + 1))
                h = H[:, bass.ds(bt + t * BT, 1), :].rearrange("p o d -> p (o d)")
                dve.tensor_tensor(h, h, y_ps[:, 0:D], ALU.add).then_inc(added, 1)
            assert link.count[0] == LINKS, link.count[0]


LE, LR = 8, 8
LORA_SCALE = 16 / LR


def lora_ffn(nc, tag, X, w, ident):
    with ExitStack() as stack:
        k = Kit(nc, stack)
        XN = k.sb(f"{tag}_XN", [P, TILES, D])
        XT = k.sb(f"{tag}_XT", [P, TOK])
        layer_norm(nc, f"{tag}_ln", X, XN, XT, ident)
        small = k.sb(f"{tag}_small", [P, TILES, LE + LR])
        top = k.sb(f"{tag}_top", [P, TILES])
        gates = k.sb(f"{tag}_gates", [P, TILES, LE], BF16)
        outer = k.sb(f"{tag}_outer", [P, TILES, LE * LR])
        outer_t = k.sb(f"{tag}_outer_t", [LE * LR, 2, 4, P])
        small_ps = k.ps(f"{tag}_small_ps", [P, TILES, LE + LR])
        t_ps = k.ps(f"{tag}_t_ps", [LE * LR, 2, 4, P])
        y_ps = k.ps(f"{tag}_y_ps", [P, 2, 4, D])
        small_done = k.sem(f"{tag}_small_done")
        step_done = k.sem(f"{tag}_step_done")
        shifted = k.sem(f"{tag}_shifted")
        exped = k.sem(f"{tag}_exped")
        outer_done = k.sem(f"{tag}_outer_done")
        turned = k.sem(f"{tag}_turned")
        copied = k.sem(f"{tag}_copied")
        projected = k.sem(f"{tag}_projected")
        added = k.sem(f"{tag}_added")
        block = stack.enter_context(nc.Block())
        LSTEPS = TILES // 4

        @block.tensor
        def _(pe):
            for t in range(TILES):
                last = pe.matmul(small_ps[:, t, :], XT[:, t * P:(t + 1) * P], w["lora"][:, D:D + LE + LR],
                                 start=True, stop=True)
            last.then_inc(small_done, 1)

            def turn(s):
                if s >= 2:
                    pe.wait_ge(copied, s - 1)
                for t in range(4):
                    last = pe.transpose(t_ps[:, s % 2, t, :], outer[:, 4 * s + t, :], ident)
                last.then_inc(turned, 1)
            pe.wait_ge(outer_done, 1)
            turn(0)
            for s in range(LSTEPS):
                if s + 1 < LSTEPS:
                    turn(s + 1)
                pe.wait_ge(copied, s + 1)
                if s >= 2:
                    pe.wait_ge(added, s - 1)
                for t in range(4):
                    tile = 4 * s + t
                    pe.matmul(y_ps[:, s % 2, t, :], XT[:, tile * P:(tile + 1) * P], w["lora"][:, 0:D],
                              start=True, stop=False)
                    last = pe.matmul(y_ps[:, s % 2, t, :], outer_t[:, s % 2, t, :], w["lora_b"],
                                     start=False, stop=True)
                last.then_inc(projected, 1)

        @block.scalar
        def _(act):
            act.wait_ge(shifted, 1)
            act.activation(small[:, :, 0:LE], small[:, :, 0:LE], ACT.Exp).then_inc(exped, 1)
            for s in range(LSTEPS):
                act.wait_ge(turned, s + 1)
                if s >= 2:
                    act.wait_ge(projected, s - 1)
                act.copy(outer_t[:, s % 2, :, :], t_ps[:, s % 2, :, :]).then_inc(copied, 1)

        @block.vector
        def _(dve):
            link = counter(dve, step_done)
            dve.wait_ge(small_done, 1)
            logits, mid = small[:, :, 0:LE], small[:, :, LE:]
            link(dve.tensor_tensor(logits, small_ps[:, :, 0:LE], over_mid(w["router_b"], TILES), ALU.add))
            link(dve.tensor_scalar(mid, small_ps[:, :, LE:], LORA_SCALE, None, ALU.mult))
            link(dve.tensor_reduce(top[:, :], logits, AX, ALU.max))
            dve.tensor_tensor(logits, logits, over(top[:, :], LE), ALU.subtract).then_inc(shifted, 1)
            dve.wait_ge(exped, 1)
            link(dve.tensor_reduce(top[:, :], logits, AX, ALU.add))
            link(dve.reciprocal(top[:, :], top[:, :]))
            link(dve.tensor_tensor(gates[:, :, :], logits, over(top[:, :], LE), ALU.mult))
            dve.tensor_tensor(outer[:, :, :].rearrange("p t (e r) -> p t e r", r=LR), over(gates[:, :, :], LR),
                              mid.unsqueeze(2).to_broadcast([P, TILES, LE, LR]), ALU.mult).then_inc(outer_done, 1)
            for s in range(LSTEPS):
                x = X[:, 4 * s:4 * s + 4, :]
                link(dve.tensor_tensor(x, x, over_mid(w["base_b"], 4), ALU.add))
                dve.wait_ge(projected, s + 1)
                dve.tensor_tensor(x, x, y_ps[:, s % 2, :, :], ALU.add).then_inc(added, 1)


WEIGHTS = {
    "a": {"qkv": [P, 3 * D], "out": [P, D], "b_qk": [P, 2], "b_v": [D], "b_out": [D]},
    "b": {"qkv": [P, 3 * D], "out": [P, D], "b_qk": [P, 2], "b_v": [D], "b_out": [D], "decay": [1]},
    "m": {"norm": [P, 1], "gates": [P, GATES], "w1": [P, EXPERTS * F], "w2": [P, FT, D]},
    "f": {"qkv": [P, 3 * FW + FH], "out": [P, FW // P, D], "ln_g": [D], "ln_b": [D]},
    "l": {"lora": [P, D + LE + LR], "lora_b": [LE * LR, D], "router_b": [LE], "base_b": [D]},
}


def load(nc, tag, k, dram, names):
    loaded = k.sem(f"{tag}_loaded")
    tiles = {}
    for n, shape in names.items():
        tiles[n] = k.sb(f"{tag}_{n}", shape if len(shape) > 1 else [P] + shape)
    with nc.Block() as block:
        @block.sync
        def _(sp):
            for n, shape in names.items():
                src = dram[f"{tag[0]}_{n}"]
                if len(shape) == 1:
                    src = src.partition_broadcast(P)
                dst = tiles[n][:, :, :] if len(shape) == 3 else tiles[n][:, :]
                sp.dma_start(dst, src).then_inc(loaded, 16)
            sp.wait_ge(loaded, 16 * len(names))
    return {n: (t[:, :, :] if len(names[n]) == 3 else t[:, :]) for n, t in tiles.items()}


def build(nc, t, out, stages=8, first=0):
    with ExitStack() as stack:
        k = Kit(nc, stack)
        X = k.sb("X", [P, TILES, D])
        ident = k.sb("ident", [P, P])
        parts_dram = nc.dram_tensor("qk_parts", [2, 3, D, TOK], BF16, kind="Internal").ap()
        shift_dram = nc.dram_tensor("shift", [HEADS, TOK], BF16, kind="Internal").ap()
        read = k.sem("x_read")
        ident_set = k.sem("ident_set")
        x_dram = t["x"].rearrange("b (t p) d -> p (b t) d", p=P)
        with nc.Block() as block:
            @block.sync
            def _(sp):
                sp.dma_start(X[:, :, :], x_dram).then_inc(read, 16)
                sp.wait_ge(read, 16)

            @block.gpsimd
            def _(pool):
                pool.memset(ident[:, :], 0.0).then_inc(ident_set, 1)
                pool.wait_ge(ident_set, 1)
                pool.affine_select(out=ident[:, :], in_=ident[:, :], compare_op=ALU.not_equal, fill=1.0,
                                   base=0, pattern=[[-1, P]], channel_multiplier=1).then_inc(ident_set, 1)
        idn = ident[:, :]
        head_of = k.sb("head_of", [P, HEADS])
        head_of_set = k.sem("head_of_set")
        with nc.Block() as block:
            @block.gpsimd
            def _(pool):
                pool.memset(head_of[:, :], 1.0).then_inc(head_of_set, 1)
                pool.wait_ge(head_of_set, 1)
                pool.affine_select(out=head_of[:, :], in_=head_of[:, :], compare_op=ALU.is_ge, fill=0.0,
                                   base=0, pattern=[[-HD, HEADS]], channel_multiplier=1).then_inc(head_of_set, 1)
                pool.wait_ge(head_of_set, 2)
                pool.affine_select(out=head_of[:, :], in_=head_of[:, :], compare_op=ALU.is_ge, fill=0.0,
                                   base=HD - 1, pattern=[[HD, HEADS]], channel_multiplier=-1).then_inc(head_of_set, 1)

        def layer(tag, body):
            with ExitStack() as own:
                k = Kit(nc, own)
                w = load(nc, tag, k, t, WEIGHTS[tag[0]]) if tag[0] in WEIGHTS else {}
                if tag[0] == "m":
                    before = k.sb(f"{tag}_before", [P, GROUPS, GROUPS])
                    zeroed = k.sem(f"{tag}_zeroed")
                    with nc.Block() as block:
                        @block.vector
                        def _(dve):
                            dve.memset(before[:, :, :], 0.0).then_inc(zeroed, 1)
                            dve.wait_ge(zeroed, 1)
                            for g in range(1, GROUPS):
                                dve.memset(before[:, g, 0:g], 1.0)
                    w["before"] = before[:, :, :]
                body(w)

        todo = [("a", lambda w: alibi_attention(nc, "a", X, w, idn, parts_dram, head_of[:, :])),
                ("m0", lambda w: moe_ffn(nc, "m0", X, w, idn)),
                ("b", lambda w: decay_attention(nc, "b", X, w, idn, parts_dram, head_of[:, :])),
                ("m1", lambda w: moe_ffn(nc, "m1", X, w, idn)),
                ("f", lambda w: fast_weights(nc, "f", X, w, idn)),
                ("l0", lambda w: lora_ffn(nc, "l0", X, w, idn)),
                ("c", lambda w: centred_attention(nc, "c", X, idn, parts_dram, shift_dram, head_of[:, :])),
                ("l1", lambda w: lora_ffn(nc, "l1", X, w, idn))]
        for tag, body in todo[first:stages]:
            with nc.cleanup_on_exit():
                layer(tag, body)

        written = k.sem("written")
        with nc.Block() as block:
            @block.sync
            def _(sp):
                sp.dma_start(out.rearrange("b (t p) d -> p (b t) d", p=P), X[:, :, :]).then_inc(written, 16)
                sp.wait_ge(written, 16)


def layout(i):
    import numpy as np
    c = np.ascontiguousarray
    x = i["L0_attn_a_x"]
    out = {"x": x}
    for tag, name, wqkv, bqkv, wout, bout in (
            ("a", "L0_attn_a", "Wqkv", "bqkv", "Wout", "bout"),
            ("b", "L0_attn_b", "Wqkv_w", "Wqkv_b", "out_w", "out_b")):
        turn = (lambda m: m) if tag == "a" else (lambda m: c(m.T))
        b = np.asarray(i[f"{name}_{bqkv}"])
        out |= {f"{tag}_qkv": turn(np.asarray(i[f"{name}_{wqkv}"])), f"{tag}_out": turn(np.asarray(i[f"{name}_{wout}"])),
                f"{tag}_b_qk": c(b.reshape(3, D)[:2].T), f"{tag}_b_v": c(b[2 * D:]), f"{tag}_b_out": i[f"{name}_{bout}"]}
    out["b_decay"] = i["L0_attn_b_distance_decay"]
    w_macro, w_micro = np.asarray(i["L0_ffn_w_macro"]), np.asarray(i["L0_ffn_w_micro"]).reshape(EXPERTS, D)
    out["m_norm"] = np.asarray(i["L0_ffn_norm_w"]).reshape(D, 1)
    out["m_gates"] = c(np.concatenate([w_macro, w_micro]).T)
    out["m_w1"] = c(np.asarray(i["L0_ffn_w1"]).reshape(EXPERTS * F, D).T)
    out["m_w2"] = c(np.asarray(i["L0_ffn_w2"]).reshape(EXPERTS, D, HALVES, P).transpose(3, 0, 2, 1).reshape(P, FT, D))
    heads = np.asarray(i["L1_attn_a_W_qkvb"]).reshape(FH, 3 * FD + 1, D)
    rows = [heads[:, n * FD:(n + 1) * FD].reshape(FW, D) for n in range(3)] + [heads[:, 3 * FD]]
    out["f_qkv"] = c(np.concatenate(rows).T)
    out["f_out"] = c(np.asarray(i["L1_attn_a_W_o"]).reshape(D, FW // P, P).transpose(2, 1, 0))
    out["f_ln_g"], out["f_ln_b"] = i["L1_attn_a_ln_g"], i["L1_attn_a_ln_b"]
    out["l_lora"] = c(np.concatenate([np.asarray(i["L1_ffn_base_w"]).T, np.asarray(i["L1_ffn_router_w"]).T,
                                      np.asarray(i["L1_ffn_lora_A"])], axis=1))
    out["l_lora_b"] = np.asarray(i["L1_ffn_lora_B"]).reshape(LE * LR, D)
    out["l_router_b"], out["l_base_b"] = i["L1_ffn_router_b"], i["L1_ffn_base_b"]
    return {n: c(np.asarray(a)) for n, a in out.items()}


def kernel(**inputs):
    import numpy as np
    import concourse.bacc as bacc
    from concourse.bass_utils import run_bass_kernel_spmd

    nc = bacc.Bacc("TRN2", target_bir_lowering=False, num_devices=1)
    arrays = layout(inputs)
    dram = {n: nc.dram_tensor(f"in_{n}", a.shape, mybir.dt.from_np(a.dtype), kind="ExternalInput").ap()
            for n, a in arrays.items()}
    out = nc.dram_tensor("out", (BATCH, SEQ, D), F32, kind="ExternalOutput").ap()
    build(nc, dram, out)
    r = run_bass_kernel_spmd(nc, [{f"in_{n}": a for n, a in arrays.items()}], core_ids=[0])
    return r.results[0]["out"]
```

```python
import math
from contextlib import ExitStack

import concourse.bass as bass
from concourse import mybir

ALU = mybir.AluOpType
ACT = mybir.ActivationFunctionType
F32 = mybir.dt.float32
BF16 = mybir.dt.bfloat16
I32 = mybir.dt.int32
AX = mybir.AxisListType.X

P = 128
D = 128
BATCH, SEQ = 4, 1024
TOK = BATCH * SEQ
TILES = TOK // P
TPB = SEQ // P
HEADS, HD = 16, 8
LN_EPS = 1e-5
CHUNK = 512
BANK = 512


class Kit:

    def __init__(self, nc, stack, shared=None):
        self.nc, self.stack = nc, stack
        self.shared = shared

    def sb(self, name, shape, dt=F32):
        return self.stack.enter_context(self.nc.sbuf_tensor(name, shape, dt))

    def ps(self, name, shape):
        return self.stack.enter_context(self.nc.psum_tensor(name, shape, F32))

    def sem(self, name):
        return self.nc.alloc_semaphore(name)


def counter(engine, sem, base=0):
    count = [0]

    def link(ins):
        count[0] += 1
        ins.then_inc(sem, 1)
        engine.wait_ge(sem, base + count[0])
    link.count = count
    return link


def over(ap, n):
    return ap.unsqueeze(len(ap.shape)).to_broadcast(list(ap.shape) + [n])


def over_mid(ap, n):
    return ap.unsqueeze(1).to_broadcast([ap.shape[0], n, ap.shape[1]])


def layer_norm(nc, tag, X, XN, XT, ident, gain=None, shift=None, beside=None):
    beside = beside or {}
    GROUP = 8
    STEPS = TILES // GROUP
    with ExitStack() as stack:
        k = Kit(nc, stack)
        squares = k.sb(f"{tag}_squares", [P, TILES, D])
        mean = k.sb(f"{tag}_mean", [P, TILES])
        var = k.sb(f"{tag}_var", [P, TILES])
        std = k.sb(f"{tag}_std", [P, TILES])
        rstd = k.sb(f"{tag}_rstd", [P, TILES])
        eps = k.sb(f"{tag}_eps", [P, 1])
        turned_ps = k.ps(f"{tag}_turned_ps", [P, 2, GROUP, P])
        step_done = k.sem(f"{tag}_step_done")
        centred = k.sem(f"{tag}_centred")
        squared = k.sem(f"{tag}_squared")
        var_ready = k.sem(f"{tag}_var_ready")
        std_ready = k.sem(f"{tag}_std_ready")
        normed = k.sem(f"{tag}_normed")
        turned = k.sem(f"{tag}_turned")
        copied = k.sem(f"{tag}_copied")
        block = stack.enter_context(nc.Block())
        cut = [slice(GROUP * s, GROUP * (s + 1)) for s in range(STEPS)]

        @block.vector
        def _(dve):
            link = counter(dve, step_done)
            link(dve.memset(eps[:], LN_EPS))
            for c in cut:
                link(dve.tensor_reduce(mean[:, c], X[:, c, :], AX, ALU.add))
                link(dve.tensor_scalar(mean[:, c], mean[:, c], 1.0 / D, None, ALU.mult))
                dve.tensor_tensor(XN[:, c, :], X[:, c, :], over(mean[:, c], D),
                                  ALU.subtract).then_inc(centred, 1)
            for s, c in enumerate(cut):
                dve.wait_ge(squared, s + 1)
                dve.tensor_reduce(var[:, c], squares[:, c, :], AX, ALU.add).then_inc(var_ready, 1)
            for s, c in enumerate(cut):
                dve.wait_ge(std_ready, s + 1)
                link(dve.reciprocal(rstd[:, c], std[:, c]))
                scaled = dve.tensor_tensor(XN[:, c, :], XN[:, c, :], over(rstd[:, c], D), ALU.mult)
                if gain is not None:
                    link(scaled)
                    link(dve.tensor_tensor(XN[:, c, :], XN[:, c, :], over_mid(gain, GROUP), ALU.mult))
                    scaled = dve.tensor_tensor(XN[:, c, :], XN[:, c, :], over_mid(shift, GROUP), ALU.add)
                scaled.then_inc(normed, 1)

        @block.scalar
        def _(act):
            for s, c in enumerate(cut):
                act.wait_ge(centred, s + 1)
                act.activation(squares[:, c, :], XN[:, c, :], ACT.Square).then_inc(squared, 1)
            for s, c in enumerate(cut):
                act.wait_ge(var_ready, s + 1)
                act.activation(std[:, c], var[:, c], ACT.Sqrt, bias=eps[:, 0:1],
                               scale=1.0 / D).then_inc(std_ready, 1)
            if XT is not None:
                for s in range(STEPS):
                    act.wait_ge(turned, s + 1)
                    act.copy(XT[:, GROUP * P * s:GROUP * P * (s + 1)],
                             turned_ps[:, s % 2, :, :].rearrange("p t q -> p (t q)")).then_inc(copied, 1)
            if "scalar" in beside:
                beside["scalar"](act)

        if "sync" in beside:
            @block.sync
            def _(sp):
                beside["sync"](sp)

        if "gpsimd" in beside:
            @block.gpsimd
            def _(pool):
                beside["gpsimd"](pool)

        if XT is not None:
            @block.tensor
            def _(pe):
                for s in range(STEPS):
                    pe.wait_ge(normed, s + 1)
                    if s >= 2:
                        pe.wait_ge(copied, s - 1)
                    for t in range(GROUP):
                        last = pe.transpose(turned_ps[:, s % 2, t, :], XN[:, GROUP * s + t, :], ident)
                    last.then_inc(turned, 1)


Q_PARTS = (0, 0, 1, 1, 0, 2)
K_PARTS = (0, 1, 0, 1, 2, 0)
ROWS = HD * len(Q_PARTS)
GH = 4
VW = 32
WIN = 2 * SEQ - P


def project_qkv(nc, tag, XT, w_qkv, b_qk, b_v, V, parts_dram, scale, head_of, longest2):
    CH = TOK // CHUNK
    RING = 4
    with ExitStack() as stack:
        kk = Kit(nc, stack)
        full = kk.sb(f"{tag}_full", [P, RING, CHUNK])
        rest = kk.sb(f"{tag}_rest", [P, RING, CHUNK])
        parts = kk.sb(f"{tag}_parts", [P, RING, 3, CHUNK], BF16)
        squares = kk.sb(f"{tag}_squares", [P, RING, CHUNK])
        norm2_ps = kk.ps(f"{tag}_norm2_ps", [HEADS, 2, BANK])
        squared = kk.sem(f"{tag}_squared")
        norm2_done = kk.sem(f"{tag}_norm2_done")
        longest_done = kk.sem(f"{tag}_longest_done")
        qk_ps = kk.ps(f"{tag}_qk_ps", [P, RING, BANK])
        v_ps = kk.ps(f"{tag}_v_ps", [P, 2, 4, D])
        projected = kk.sem(f"{tag}_projected")
        biased = kk.sem(f"{tag}_biased")
        part1 = kk.sem(f"{tag}_part1")
        rest1 = kk.sem(f"{tag}_rest1")
        part2 = kk.sem(f"{tag}_part2")
        part3 = kk.sem(f"{tag}_part3")
        stored = [kk.sem(f"{tag}_stored{b}") for b in range(RING)]
        v_done = kk.sem(f"{tag}_v_done")
        v_out = kk.sem(f"{tag}_v_out")
        block = stack.enter_context(nc.Block())
        UNITS = 2 * CH

        @block.tensor
        def _(pe):
            def norms(u):
                pe.wait_ge(squared, u + 1)
                if u >= 2:
                    pe.wait_ge(longest_done, u - 1)
                pe.matmul(norm2_ps[:, u % 2, :], head_of, squares[:, u % RING, :], start=True,
                          stop=True).then_inc(norm2_done, 1)

            for u in range(UNITS):
                c, w = divmod(u, 2)
                if u >= RING:
                    pe.wait_ge(biased, u - RING + 1)
                pe.matmul(qk_ps[:, u % RING, :], w_qkv[:, w * D:(w + 1) * D],
                          XT[:, c * CHUNK:(c + 1) * CHUNK], start=True, stop=True).then_inc(projected, 1)
                if u >= 1:
                    norms(u - 1)
            norms(UNITS - 1)
            for s in range(TILES // 4):
                if s >= 2:
                    pe.wait_ge(v_out, s - 1)
                for t in range(4):
                    last = pe.matmul(v_ps[:, s % 2, t, :], XT[:, (4 * s + t) * P:(4 * s + t + 1) * P],
                                     w_qkv[:, 2 * D:3 * D], start=True, stop=True)
                last.then_inc(v_done, 1)

        @block.vector
        def _(dve):
            def take(u):
                w, b = u % 2, u % RING
                dve.wait_ge(projected, u + 1)
                if u >= RING:
                    dve.wait_ge(squared, u - RING + 1)
                dve.tensor_scalar(full[:, b, :], qk_ps[:, b, :], b_qk[:, w:w + 1],
                                  scale if w == 0 else 1.0, ALU.add, ALU.mult).then_inc(biased, 1)

            def rest_of(u):
                b = u % RING
                dve.wait_ge(part1, u + 1)
                dve.wait_ge(biased, u + 1)
                dve.tensor_tensor(rest[:, b, :], full[:, b, :], parts[:, b, 0, :],
                                  ALU.subtract).then_inc(rest1, 1)

            def third_part(u):
                b = u % RING
                dve.wait_ge(part2, u + 1)
                dve.wait_ge(rest1, u + 1)
                dve.tensor_tensor(parts[:, b, 2, :], rest[:, b, :], parts[:, b, 1, :],
                                  ALU.subtract).then_inc(part3, 1)
                dve.wait_ge(norm2_done, u + 1)
                dve.tensor_reduce(longest2[:, u % 2, u // 2:u // 2 + 1], norm2_ps[:, u % 2, :], AX,
                                  ALU.max).then_inc(longest_done, 1)

            for u in range(UNITS + 2):
                if u < UNITS:
                    take(u)
                if 1 <= u <= UNITS:
                    rest_of(u - 1)
                if u >= 2:
                    third_part(u - 2)
            for s in range(TILES // 4):
                dve.wait_ge(v_done, s + 1)
                dve.tensor_tensor(V[:, 4 * s:4 * s + 4, :], v_ps[:, s % 2, :, :], over_mid(b_v, 4),
                                  ALU.add).then_inc(v_out, 1)

        @block.scalar
        def _(act):
            for u in range(UNITS + 1):
                b = u % RING
                if u < UNITS:
                    act.wait_ge(biased, u + 1)
                    if u >= RING:
                        act.wait_ge(stored[b], 16 * (u // RING))
                    act.copy(parts[:, b, 0, :], full[:, b, :]).then_inc(part1, 1)
                    if u >= RING:
                        act.wait_ge(norm2_done, u - RING + 1)
                    act.activation(squares[:, b, :], full[:, b, :], ACT.Square).then_inc(squared, 1)
                if u >= 1:
                    act.wait_ge(rest1, u)
                    act.copy(parts[:, (u - 1) % RING, 1, :], rest[:, (u - 1) % RING, :]).then_inc(part2, 1)

        @block.sync
        def _(sp):
            for u in range(UNITS):
                c, w = divmod(u, 2)
                sp.wait_ge(part3, u + 1)
                sp.dma_start(parts_dram[w].rearrange("s f t -> f s t")[:, :, c * CHUNK:(c + 1) * CHUNK],
                             parts[:, u % RING, :, :]).then_inc(stored[u % RING], 16)
            for b in range(RING):
                sp.wait_ge(stored[b], 16 * (UNITS // RING))


class Operands:
    SHIFT_ROW = 64

    def __init__(self, tag, k):
        self.q_rows = k.sb(f"{tag}_q_rows", [P, 2, GH, SEQ], BF16)
        self.k_rows = k.sb(f"{tag}_k_rows", [P, 2, GH, SEQ], BF16)
        self.v_cols = k.sb(f"{tag}_v_cols", [P, 2, TPB, GH, VW])
        self.cleared = k.sem(f"{tag}_cleared")

    def clear(self, pool):
        pool.memset(self.q_rows[:].bitcast(F32), 0.0).then_inc(self.cleared, 1)
        pool.memset(self.k_rows[:].bitcast(F32), 0.0).then_inc(self.cleared, 1)
        pool.memset(self.v_cols[:], 0.0).then_inc(self.cleared, 1)
        pool.wait_ge(self.cleared, 3)
        pool.memset(self.k_rows[self.SHIFT_ROW:self.SHIFT_ROW + 1, :, :, :], 1.0).then_inc(self.cleared, 1)
        pool.wait_ge(self.cleared, 4)
        pool.memset(self.v_cols[:, :, :, :, HD:HD + 1], 1.0)


SAFE_SCORE = 60.0


def bound_scores(nc, tag, longest2, wide, ident):
    with ExitStack() as stack:
        k = Kit(nc, stack)
        longest = k.sb(f"{tag}_longest", [HEADS, 2])
        square = k.sb(f"{tag}_square", [HEADS, 1])
        top = k.sb(f"{tag}_top", [1, 1])
        row_ps = k.ps(f"{tag}_row_ps", [1, HEADS])
        step_done = k.sem(f"{tag}_step_done")
        square_done = k.sem(f"{tag}_square_done")
        row_done = k.sem(f"{tag}_row_done")
        top_done = k.sem(f"{tag}_top_done")
        with nc.Block() as block:
            @block.vector
            def _(dve):
                link = counter(dve, step_done)
                link(dve.tensor_reduce(longest[:, :], longest2[:, :, :], AX, ALU.max))
                dve.tensor_tensor(square[:, :], longest[:, 0:1], longest[:, 1:2], ALU.mult).then_inc(square_done, 1)
                dve.wait_ge(row_done, 1)
                dve.tensor_reduce(top[:, :], row_ps[:, :], AX, ALU.max).then_inc(top_done, 1)
                dve.wait_ge(top_done, 1)
                dve.tensor_scalar(wide[:, :], top[:, :], SAFE_SCORE ** 2, None, ALU.is_gt)

            @block.tensor
            def _(pe):
                pe.wait_ge(square_done, 1)
                pe.matmul(row_ps[:, :], square[:, :], ident[0:HEADS, 0:HEADS], start=True, stop=True).then_inc(row_done, 1)


def attend(nc, tag, V, operands, parts_dram, tables, op, out_all, ident):
    QT = TPB
    UNITS = QT * GH
    RING = 6
    LAG = 3
    AHEAD = 4
    with ExitStack() as stack:
        k = Kit(nc, stack)
        q_rows, k_rows, v_cols = operands.q_rows, operands.k_rows, operands.v_cols
        table = tables["buffer"]
        probs = k.sb(f"{tag}_probs", [P, RING, SEQ])
        row_max = k.sb(f"{tag}_row_max", [P, UNITS])
        tick = k.sb(f"{tag}_tick", [P, UNITS + 1])
        zero = k.sb(f"{tag}_zero", [P, 1])
        neg_max = k.sb(f"{tag}_neg_max", [P, UNITS])
        probs_t = k.sb(f"{tag}_probs_t", [P, 2, GH, TPB, P])
        out_t = k.sb(f"{tag}_out_t", [P, P])
        inv_sum = k.sb(f"{tag}_inv_sum", [P, QT, GH])
        s_ps = k.ps(f"{tag}_s_ps", [P, 2, SEQ])
        t_ps = k.ps(f"{tag}_t_ps", [P, 2, 4, P])
        o_ps = k.ps(f"{tag}_o_ps", [P, BANK])
        ot_ps = k.ps(f"{tag}_ot_ps", [P, BANK])
        loaded = [k.sem(f"{tag}_loaded{half}") for half in range(2)]
        group_done = k.sem(f"{tag}_group_done")
        zero_set = k.sem(f"{tag}_zero_set")
        table_set = k.sem(f"{tag}_table_set")
        v_set = k.sem(f"{tag}_v_set")
        scored = k.sem(f"{tag}_scored")
        maxed = k.sem(f"{tag}_maxed")
        negated = k.sem(f"{tag}_negated")
        exped = k.sem(f"{tag}_exped")
        turned = k.sem(f"{tag}_turned")
        left_out = k.sem(f"{tag}_left_out")
        right_out = k.sem(f"{tag}_right_out")
        summed = k.sem(f"{tag}_summed")
        o_out = k.sem(f"{tag}_o_out")
        o_turned = k.sem(f"{tag}_o_turned")
        inverted = k.sem(f"{tag}_inverted")
        normed = k.sem(f"{tag}_normed")
        block = stack.enter_context(nc.Block())
        LOADS = 2 * len(Q_PARTS)

        @block.sync
        def _(sp):
            with sp.Fori(0, HEADS // GH) as hg:
                with sp.Fori(0, BATCH // 2) as bp:
                    for half in range(2):
                        sp.wait_ge(group_done, hg * 4 + bp * 2 + (half + 1))
                        for rows, which, order in ((q_rows, 0, Q_PARTS), (k_rows, 1, K_PARTS)):
                            for n, part in enumerate(order):
                                src = parts_dram[which, part].rearrange("(h e) t -> e h t", e=HD)
                                sp.dma_start(
                                    rows[n * HD:(n + 1) * HD, half, :, :],
                                    src[:, bass.ds(hg * GH, GH), bass.ds(bp * (2 * SEQ) + half * SEQ, SEQ)],
                                ).then_inc(loaded[half], 16)

        @block.gpsimd
        def _(pool):
            pool.memset(zero[:, :], 0.0).then_inc(zero_set, 1)
            pool.wait_ge(zero_set, 1)
            with pool.Fori(0, HEADS // GH) as hg:
                if tables.get("per_group"):
                    for j in range(GH):
                        if j == 0:
                            pool.wait_ge(tables["free"], hg + 1)
                        pool.wait_ge(zero_set, 1)
                        pool.tensor_tensor(table[:, j, :], tables["distance"][:, :],
                                           tables["slopes"][:, bass.ds(hg * GH + j, 1)].to_broadcast([P, WIN]),
                                           ALU.mult).then_inc(table_set, 1)
                with pool.Fori(0, BATCH // 2) as bp:
                    for half in range(2):
                        g = hg * 4 + bp * 2
                        pool.wait_ge(group_done, g + (half + 1))
                        src = V[:, bass.ds(bp * (2 * TPB) + half * TPB, TPB), bass.ds(hg * (GH * HD), GH * HD)]
                        pool.tensor_copy(v_cols[:, half, :, :, 0:HD],
                                         src.rearrange("p t (h e) -> p t h e", e=HD)).then_inc(v_set, 1)
                        for n in range(UNITS):
                            pool.wait_ge(maxed, (g + half) * UNITS + (n + 1))
                            pool.tensor_tensor(neg_max[:, n:n + 1], zero[:, :], row_max[:, n:n + 1],
                                               ALU.subtract).then_inc(negated, 1)

        @block.tensor
        def _(pe):
            pe.sem_inc(group_done, 2)
            with pe.Fori(0, HEADS // GH) as hg:
                with pe.Fori(0, BATCH // 2) as bp:
                    for half in range(2):
                        g = hg * 4 + (bp * 2 + half)

                        def scores(n):
                            qt, j = divmod(n, GH)
                            if n >= 2:
                                pe.wait_ge(maxed, g * UNITS + (n - 1))
                            for c in range(2):
                                last = pe.matmul(s_ps[:, n % 2, c * BANK:(c + 1) * BANK],
                                                 q_rows[:, half, j, qt * P:(qt + 1) * P],
                                                 k_rows[:, half, j, c * BANK:(c + 1) * BANK],
                                                 start=True, stop=True)
                            last.then_inc(scored, 1)

                        def turn(n):
                            pe.wait_ge(exped, g * UNITS + (n + 1))
                            for side in range(2):
                                if n >= 1:
                                    pe.wait_ge((left_out, right_out)[side], g * UNITS + n)
                                for t in range(4):
                                    kt = 4 * side + t
                                    last = pe.transpose(t_ps[:, side, t, :],
                                                        probs[:, n % RING, kt * P:(kt + 1) * P], ident)
                                last.then_inc(turned, 1)

                        def sum_up(qt):
                            pe.wait_ge(left_out, g * UNITS + GH * (qt + 1))
                            pe.wait_ge(right_out, g * UNITS + GH * (qt + 1))
                            if qt >= 1:
                                pe.wait_ge(o_out, g * QT + qt)
                            for kt in range(TPB):
                                for j in range(GH):
                                    last = pe.matmul(o_ps[VW * j:VW * (j + 1), 0:P], v_cols[:, half, kt, j, :],
                                                     probs_t[:, qt % 2, j, kt, :], start=(kt == 0),
                                                     stop=(kt == TPB - 1))
                            last.then_inc(summed, 1)

                        def turn_sum(qt):
                            pe.wait_ge(o_out, g * QT + (qt + 1))
                            if qt >= 1:
                                pe.wait_ge(normed, g * QT + qt)
                            pe.transpose(ot_ps[:, 0:P], out_t[:, :], ident).then_inc(o_turned, 1)

                        pe.wait_ge(loaded[half], (hg * 2 + bp + 1) * (16 * LOADS))
                        pe.wait_ge(v_set, g + 1)
                        for n in range(AHEAD):
                            scores(n)
                        for n in range(UNITS):
                            if n + AHEAD < UNITS:
                                scores(n + AHEAD)
                            turn(n)
                            if n % GH == 1 and n > GH:
                                sum_up(n // GH - 1)
                            if n % GH == 2 and n > GH:
                                turn_sum(n // GH - 1)
                        sum_up(QT - 1)
                        pe.wait_ge(o_out, g * QT + QT)
                        pe.wait_ge(normed, g * QT + (QT - 1))
                        pe.transpose(ot_ps[:, 0:P], out_t[:, :], ident).then_inc(o_turned, 1)
                        pe.wait_ge(o_turned, g * QT + QT)
                        pe.sem_inc(group_done, 1)

        @block.vector
        def _(dve):
            if tables.get("per_group"):
                dve.sem_inc(tables["free"], 1)
            with dve.Fori(0, HEADS // GH) as hg:
                if tables.get("per_group"):
                    dve.wait_ge(table_set, (hg + 1) * GH)
                    dve.memset(tick[:, UNITS:UNITS + 1], 0.0)
                with dve.Fori(0, BATCH // 2) as bp:
                    for half in range(2):
                        g = hg * 4 + (bp * 2 + half)

                        def left(n):
                            dve.wait_ge(turned, g * (2 * UNITS) + (2 * n + 1))
                            if n // GH >= 2:
                                dve.wait_ge(summed, g * QT + (n // GH - 1))
                            dve.tensor_copy(probs_t[:, (n // GH) % 2, n % GH, 0:4, :],
                                            t_ps[:, 0, :, :]).then_inc(left_out, 1)

                        def norm(qt):
                            dve.wait_ge(o_turned, g * QT + (qt + 1))
                            heads = ot_ps[:, 0:P].rearrange("p (h e) -> p h e", e=VW)
                            dve.reciprocal(inv_sum[:, qt, :], heads[:, :, HD]).then_inc(inverted, 1)
                            dve.wait_ge(inverted, g * QT + (qt + 1))
                            dst = out_all[:, bass.ds(bp * (2 * TPB) + (half * TPB + qt), 1),
                                          bass.ds(hg * (GH * HD), GH * HD)]
                            dve.tensor_tensor(dst.rearrange("p o (h e) -> p (o h) e", e=HD),
                                              heads[:, :, 0:HD], over(inv_sum[:, qt, :], HD),
                                              ALU.mult).then_inc(normed, 1)

                        for n in range(UNITS):
                            qt, j = divmod(n, GH)
                            dve.wait_ge(scored, g * UNITS + (n + 1))
                            if n >= RING:
                                dve.wait_ge(turned, g * (2 * UNITS) + 2 * (n - RING + 1))
                            dve.memset(tick[:, n:n + 1], 0.0)
                            at = SEQ - P - qt * P
                            t = table[:, j if tables.get("per_group") else 0, at:at + SEQ]
                            dve.tensor_tensor_reduce(out=probs[:, n % RING, :], in0=s_ps[:, n % 2, :], in1=t,
                                                     scale=1.0, scalar=-3e38, op0=op, op1=ALU.max,
                                                     accum_out=row_max[:, n:n + 1]).then_inc(maxed, 1)
                            if n >= LAG:
                                left(n - LAG)
                            if n % GH == GH - 1 and n >= 2 * GH:
                                norm(n // GH - 2)
                        for n in range(UNITS - LAG, UNITS):
                            left(n)
                        norm(QT - 2)
                        norm(QT - 1)
                if tables.get("per_group"):
                    dve.wait_ge(maxed, (hg + 1) * (BATCH * UNITS))
                    dve.sem_inc(tables["free"], 1)

        @block.scalar
        def _(act):
            with act.Fori(0, HEADS // GH) as hg:
                with act.Fori(0, BATCH // 2) as bp:
                    for half in range(2):
                        g = hg * 4 + (bp * 2 + half)

                        def right(n):
                            act.wait_ge(turned, g * (2 * UNITS) + (2 * n + 2))
                            if n // GH >= 2:
                                act.wait_ge(summed, g * QT + (n // GH - 1))
                            act.copy(probs_t[:, (n // GH) % 2, n % GH, 4:8, :],
                                     t_ps[:, 1, :, :]).then_inc(right_out, 1)

                        def take_sum(qt):
                            act.wait_ge(summed, g * QT + (qt + 1))
                            if qt >= 1:
                                act.wait_ge(o_turned, g * QT + qt)
                            act.copy(out_t[:, :], o_ps[:, 0:P]).then_inc(o_out, 1)

                        for n in range(UNITS):
                            act.wait_ge(negated, g * UNITS + (n + 1))
                            act.activation(probs[:, n % RING, :], probs[:, n % RING, :], ACT.Exp,
                                           bias=neg_max[:, n:n + 1]).then_inc(exped, 1)
                            if n >= 1:
                                right(n - 1)
                            if n % GH == 2 and n > GH:
                                take_sum(n // GH - 1)
                        right(UNITS - 1)
                        take_sum(QT - 1)


def attend_transposed(nc, tag, V, operands, parts_dram, out_t, shift_dram=None, table=None, slopes=None):
    by_dve = table is not None
    JT = TPB
    UNITS = JT * GH
    NG = (HEADS // GH) * BATCH
    SLOTS = 3
    with ExitStack() as stack:
        k = Kit(nc, stack)
        q_rows, k_rows, v_cols = operands.q_rows, operands.k_rows, operands.v_cols
        probs = k.sb(f"{tag}_probs", [P, 2, GH, SEQ])
        s_ps = k.ps(f"{tag}_s_ps", [P, SLOTS, SEQ])
        o_ps = k.ps(f"{tag}_o_ps", [P, 2, BANK])
        loaded = [k.sem(f"{tag}_loaded{half}") for half in range(2)]
        v_set = k.sem(f"{tag}_v_set")
        scored = k.sem(f"{tag}_scored")
        exped = k.sem(f"{tag}_exped")
        summed = k.sem(f"{tag}_summed")
        o_out = k.sem(f"{tag}_o_out")
        block = stack.enter_context(nc.Block())
        adjusted = k.sem(f"{tag}_adjusted") if by_dve else None
        slot_read = adjusted if by_dve else exped
        LOADS = 2 * len(Q_PARTS) + (not by_dve)

        @block.sync
        def _(sp):
            with sp.Fori(0, HEADS // GH) as hg:
                with sp.Fori(0, BATCH // 2) as bp:
                    for half in range(2):
                        sp.wait_ge(o_out, hg * 8 + bp * 4 + (2 * half + 2))
                        at = bass.ds(bp * (2 * SEQ) + half * SEQ, SEQ)
                        for rows, which, order in ((q_rows, 0, Q_PARTS), (k_rows, int(by_dve), K_PARTS)):
                            for n, part in enumerate(order):
                                src = parts_dram[which, part].rearrange("(h e) t -> e h t", e=HD)
                                sp.dma_start(rows[n * HD:(n + 1) * HD, half, :, :],
                                             src[:, bass.ds(hg * GH, GH), at]).then_inc(loaded[half], 16)
                        if not by_dve:
                            sp.dma_start(q_rows[operands.SHIFT_ROW:operands.SHIFT_ROW + 1, half, :, :],
                                         shift_dram.unsqueeze(0)[:, bass.ds(hg * GH, GH), at]
                                         ).then_inc(loaded[half], 16)

        @block.gpsimd
        def _(pool):
            with pool.Fori(0, HEADS // GH) as hg:
                with pool.Fori(0, BATCH // 2) as bp:
                    for half in range(2):
                        pool.wait_ge(o_out, hg * 8 + bp * 4 + (2 * half + 2))
                        src = V[:, bass.ds(bp * (2 * TPB) + half * TPB, TPB), bass.ds(hg * (GH * HD), GH * HD)]
                        pool.tensor_copy(v_cols[:, half, :, :, 0:HD],
                                         src.rearrange("p t (h e) -> p t h e", e=HD)).then_inc(v_set, 1)

        @block.tensor
        def _(pe):
            pe.sem_inc(summed, 2)

            def scores(half, n, i):
                g = i * 2 + half
                J, j = divmod(n, GH)
                if n == 0:
                    pe.wait_ge(loaded[half], i * (16 * LOADS) + 16 * LOADS)
                back = n - SLOTS if n >= SLOTS else max(m for m in range(-SLOTS, 0) if (m + UNITS) % SLOTS == n)
                pe.wait_ge(slot_read, g * UNITS + (back + 1 + SLOTS))
                for c in range(2):
                    last = pe.matmul(s_ps[:, n % SLOTS, c * BANK:(c + 1) * BANK],
                                     k_rows[:, half, j, J * P:(J + 1) * P],
                                     q_rows[:, half, j, c * BANK:(c + 1) * BANK], start=True, stop=True)
                last.then_inc(scored, 1)

            def sum_up(half, J, c, i):
                g = i * 2 + half
                if c == 0:
                    if J == 0:
                        pe.wait_ge(o_out, g * 2 + 4)
                        pe.wait_ge(v_set, g + 1)
                    pe.wait_ge(exped, g * UNITS + (GH * (J + 1) + SLOTS))
                for j in range(GH):
                    last = pe.matmul(o_ps[VW * j:VW * (j + 1), c, :], v_cols[:, half, J, j, :],
                                     probs[:, J % 2, j, c * BANK:(c + 1) * BANK], start=(J == 0),
                                     stop=(J == JT - 1))
                if c == 1:
                    last.then_inc(summed, 1)

            def pair(i, final):
                for half in range(2):
                    for n in range(UNITS):
                        m = n + SLOTS
                        if m < UNITS:
                            scores(half, m, i)
                        elif half == 0:
                            scores(1, m - UNITS, i)
                        elif not final:
                            scores(0, m - UNITS, i + 1)
                        if n % GH == GH - 1:
                            sum_up(half, n // GH, 0, i)
                            if n + 1 == UNITS:
                                sum_up(half, n // GH, 1, i)
                        if n % GH == 1 and n > GH:
                            sum_up(half, n // GH - 1, 1, i)

            for n in range(SLOTS):
                scores(0, n, 0)
            with pe.Fori(0, NG // 2 - 1) as i:
                pair(i, False)
            pair(NG // 2 - 1, True)

        @block.scalar
        def _(act):
            act.sem_inc(exped, SLOTS)

            def take_sums(g):
                act.wait_ge(summed, g * JT + (JT + 2))
                for c in range(2):
                    dst = out_t[:, bass.ds(g, 1), c * BANK:(c + 1) * BANK].rearrange("p o q -> p (o q)")
                    act.copy(dst, o_ps[:, c, :]).then_inc(o_out, 1)

            def group(g, first):
                for n in range(UNITS):
                    J, j = divmod(n, GH)
                    out = probs[:, J % 2, j, :]
                    if by_dve:
                        act.wait_ge(adjusted, g * UNITS + (n + 1 + SLOTS))
                        act.activation(out, out, ACT.Exp).then_inc(exped, 1)
                        if n == 1 and not first:
                            take_sums(g - 1)
                        continue
                    act.wait_ge(scored, g * UNITS + (n + 1))
                    if j == 0:
                        act.wait_ge(summed, g * JT + (J + 1))
                    act.activation(out, s_ps[:, n % SLOTS, :], ACT.Exp).then_inc(exped, 1)

            if by_dve:
                group(0, True)
                with act.Fori(1, NG) as g:
                    group(g, False)
                take_sums(NG - 1)
            else:
                with act.Fori(0, NG) as g:
                    group(g, False)

        @block.vector
        def _(dve):
            dve.sem_inc(o_out, 4)
            if not by_dve:
                with dve.Fori(0, NG) as g:
                    dve.wait_ge(summed, g * JT + (JT + 2))
                    for c in range(2):
                        dst = out_t[:, bass.ds(g, 1), c * BANK:(c + 1) * BANK].rearrange("p o q -> p (o q)")
                        dve.tensor_copy(dst, o_ps[:, c, :]).then_inc(o_out, 1)
                return
            dve.sem_inc(adjusted, SLOTS)
            with dve.Fori(0, HEADS // GH) as hg:
                with dve.Fori(0, BATCH) as b:
                    g = hg * BATCH + b
                    for n in range(UNITS):
                        J, j = divmod(n, GH)
                        dve.wait_ge(scored, g * UNITS + (n + 1))
                        if j == 0:
                            dve.wait_ge(summed, g * JT + (J + 1))
                        near = table[:, SEQ - P - J * P:2 * SEQ - P - J * P]
                        out, scores_ = probs[:, J % 2, j, :], s_ps[:, n % SLOTS, :]
                        if slopes is None:
                            ins = dve.tensor_tensor(out, scores_, near, ALU.mult)
                        else:
                            ins = dve.scalar_tensor_tensor(out=out, in0=near, scalar=slopes[:, bass.ds(hg * GH + j, 1)],
                                                           in1=scores_, op0=ALU.mult, op1=ALU.add)
                        ins.then_inc(adjusted, 1)


def normalise(nc, tag, out_t, out_all, ident):
    NH = HEADS // GH
    with ExitStack() as stack:
        k = Kit(nc, stack)
        inv = k.sb(f"{tag}_inv", [P, TILES, HEADS])
        t_ps = k.ps(f"{tag}_t_ps", [P, 4, NH, P])
        turned = k.sem(f"{tag}_turned")
        inverted = k.sem(f"{tag}_inverted")
        normed = k.sem(f"{tag}_normed")
        block = stack.enter_context(nc.Block())

        @block.tensor
        def _(pe):
            for t in range(TILES):
                b, qt = divmod(t, TPB)
                if t >= 4:
                    pe.wait_ge(normed, t - 3)
                for hg in range(NH):
                    last = pe.transpose(t_ps[:, t % 4, hg, :], out_t[:, hg * BATCH + b, qt * P:(qt + 1) * P], ident)
                last.then_inc(turned, 1)

        @block.vector
        def _(dve):
            for t in range(TILES):
                heads = t_ps[:, t % 4, :, :].rearrange("p g (h e) -> p (g h) e", e=VW)
                dve.wait_ge(turned, t + 1)
                dve.reciprocal(inv[:, t, :], heads[:, :, HD]).then_inc(inverted, 1)
                dve.wait_ge(inverted, t + 1)
                dve.tensor_tensor(out_all[:, t, :].rearrange("p (h e) -> p h e", e=HD), heads[:, :, 0:HD],
                                  over(inv[:, t, :], HD), ALU.mult).then_inc(normed, 1)


def project_out(nc, tag, out_all, w_out, b_out, X, ident):
    with ExitStack() as stack:
        k = Kit(nc, stack)
        out_t = k.sb(f"{tag}_out_t", [P, 2, 4, P])
        t_ps = k.ps(f"{tag}_t_ps", [P, 2, 4, P])
        y_ps = k.ps(f"{tag}_y_ps", [P, 2, 4, D])
        turned = k.sem(f"{tag}_turned")
        copied = k.sem(f"{tag}_copied")
        projected = k.sem(f"{tag}_projected")
        biased = k.sem(f"{tag}_biased")
        added = k.sem(f"{tag}_added")
        block = stack.enter_context(nc.Block())
        STEPS = TILES // 4

        @block.tensor
        def _(pe):
            def turn(s):
                if s >= 2:
                    pe.wait_ge(copied, s - 1)
                for t in range(4):
                    last = pe.transpose(t_ps[:, s % 2, t, :], out_all[:, 4 * s + t, :], ident)
                last.then_inc(turned, 1)
            turn(0)
            for s in range(STEPS):
                if s + 1 < STEPS:
                    turn(s + 1)
                pe.wait_ge(copied, s + 1)
                if s >= 2:
                    pe.wait_ge(added, s - 1)
                for t in range(4):
                    last = pe.matmul(y_ps[:, s % 2, t, :], out_t[:, s % 2, t, :], w_out, start=True, stop=True)
                last.then_inc(projected, 1)

        @block.scalar
        def _(act):
            for s in range(STEPS):
                act.wait_ge(turned, s + 1)
                if s >= 2:
                    act.wait_ge(projected, s - 1)
                act.copy(out_t[:, s % 2, :, :], t_ps[:, s % 2, :, :]).then_inc(copied, 1)

        @block.vector
        def _(dve):
            for s in range(STEPS):
                x = X[:, 4 * s:4 * s + 4, :]
                dve.tensor_tensor(x, x, over_mid(b_out, 4), ALU.add).then_inc(biased, 1)
                dve.wait_ge(projected, s + 1)
                dve.wait_ge(biased, s + 1)
                dve.tensor_tensor(x, x, y_ps[:, s % 2, :, :], ALU.add).then_inc(added, 1)


def alibi_slopes():
    start = 2.0 ** (-2.0 ** (-(math.log2(HEADS) - 3)))
    return [start ** i for i in range(HEADS)]


class Distances:

    def __init__(self, tag, k):
        self.distance = k.sb(f"{tag}_distance", [P, WIN])
        self.signed = self.distance[:, :].bitcast(I32)
        self.counted = k.sem(f"{tag}_counted")

    def count(self, pool):
        pool.iota(self.signed, pattern=[[1, WIN]], base=-(SEQ - P), channel_multiplier=-1).then_inc(self.counted, 1)

    def take(self, act):
        act.wait_ge(self.counted, 1)
        return act.activation(self.distance[:, :], self.signed, ACT.Abs)


def attention_layer(nc, tag, X, w, ident, parts_dram, head_of, fetch, attend_all, gpsimd, scalar):
    with ExitStack() as stack:
        k = Kit(nc, stack)
        XN = k.sb(f"{tag}_XN", [P, TILES, D])
        V = k.sb(f"{tag}_V", [P, TILES, D])
        longest2 = k.sb(f"{tag}_longest2", [HEADS, 2, TOK // CHUNK])
        wide = k.sb(f"{tag}_wide", [1, 1], I32)
        operands = Operands(tag, k)

        def clear_too(pool):
            gpsimd(pool)
            operands.clear(pool)
        with ExitStack() as inner:
            XT = Kit(nc, inner).sb(f"{tag}_XT", [P, TOK])
            layer_norm(nc, f"{tag}_ln", X, XN, XT, ident,
                       beside={"sync": fetch, "gpsimd": clear_too, "scalar": scalar})
            project_qkv(nc, f"{tag}_qkv", XT, w["qkv"], w["b_qk"], w["b_v"], V, parts_dram,
                        1.0 / math.sqrt(HD), head_of, longest2)
        bound_scores(nc, f"{tag}_bound", longest2, wide, ident)
        attend_all(wide, V, operands, XN)
        project_out(nc, f"{tag}_out", XN, w["out"], w["b_out"], X, ident)


def choose(nc, tag, wide, direct, general):
    is_wide = nc.values_load(wide[0:1, 0:1], min_val=0, max_val=1)
    with nc.If(is_wide == 1):
        general()
    with nc.Else():
        direct()


def alibi_attention(nc, tag, X, w, ident, parts_dram, head_of, fetch):
    with ExitStack() as stack:
        k = Kit(nc, stack)
        distances = Distances(tag, k)
        slopes = k.sb(f"{tag}_slopes", [P, HEADS])
        free = k.sem(f"{tag}_table_free")

        def gpsimd(pool):
            distances.count(pool)
            for h, s in enumerate(alibi_slopes()):
                pool.memset(slopes[:, h:h + 1], -s)

        def attend_all(wide, V, operands, out):
            def direct():
                with ExitStack() as inner:
                    out_t = Kit(nc, inner).sb(f"{tag}_out_t", [P, (HEADS // GH) * BATCH, SEQ])
                    attend_transposed(nc, f"{tag}_direct", V, operands, parts_dram, out_t,
                                      table=distances.distance, slopes=slopes)
                    normalise(nc, f"{tag}_norm", out_t, out, ident)

            def general():
                with ExitStack() as inner:
                    table = Kit(nc, inner).sb(f"{tag}_table", [P, GH, WIN])
                    attend(nc, f"{tag}_att", V, operands, parts_dram, {"buffer": table, "per_group": True,
                           "distance": distances.distance, "slopes": slopes, "free": free}, ALU.add, out, ident)
            choose(nc, tag, wide, direct, general)
        attention_layer(nc, tag, X, w, ident, parts_dram, head_of, fetch, attend_all, gpsimd,
                        lambda act: distances.take(act))


def decay_attention(nc, tag, X, w, ident, parts_dram, head_of, fetch):
    with ExitStack() as stack:
        k = Kit(nc, stack)
        distances = Distances(tag, k)
        table = distances.distance[:, :].unsqueeze(1)
        rate = k.sb(f"{tag}_rate", [P, 1])
        table_step = k.sem(f"{tag}_table_step")
        decay_in = k.sem(f"{tag}_decay_in")

        def fetch_and_tell(sp):
            fetch(sp)
            sp.sem_inc(decay_in, 1)

        def make_table(act):
            distances.take(act).then_inc(table_step, 1)
            act.wait_ge(decay_in, 1)
            act.activation(rate[:, :], w["decay"], ACT.Abs).then_inc(table_step, 1)
            act.wait_ge(table_step, 2)
            act.mul(rate[:, :], rate[:, :], -1.0).then_inc(table_step, 1)
            act.wait_ge(table_step, 3)
            act.activation(table[:, 0, :], table[:, 0, :], ACT.Exp, scale=rate[:, 0:1])

        def attend_all(wide, V, operands, out):
            def direct():
                with ExitStack() as inner:
                    out_t = Kit(nc, inner).sb(f"{tag}_out_t", [P, (HEADS // GH) * BATCH, SEQ])
                    attend_transposed(nc, f"{tag}_direct", V, operands, parts_dram, out_t, table=table[:, 0, :])
                    normalise(nc, f"{tag}_norm", out_t, out, ident)

            def general():
                attend(nc, f"{tag}_att", V, operands, parts_dram, {"buffer": table}, ALU.mult, out, ident)
            choose(nc, tag, wide, direct, general)
        attention_layer(nc, tag, X, w, ident, parts_dram, head_of, fetch_and_tell, attend_all,
                        distances.count, make_table)


def centred_attention(nc, tag, X, ident, parts_dram, shift_dram, head_of):
    with ExitStack() as stack:
        k = Kit(nc, stack)
        XN = k.sb(f"{tag}_XN", [P, TILES, D])
        operands = Operands(tag, k)
        with ExitStack() as inner:
            XT = Kit(nc, inner).sb(f"{tag}_XT", [P, TOK])
            layer_norm(nc, f"{tag}_ln", X, XN, XT, ident, beside={"gpsimd": operands.clear})
            centre_and_split(nc, f"{tag}_split", XT, parts_dram, shift_dram, head_of)
        out_t = k.sb(f"{tag}_out_t", [P, (HEADS // GH) * BATCH, SEQ])
        attend_transposed(nc, f"{tag}_att", XN, operands, parts_dram, out_t, shift_dram=shift_dram)
        normalise(nc, f"{tag}_norm", out_t, XN, ident)
        with nc.Block() as block:
            @block.vector
            def _(dve):
                dve.tensor_tensor(X[:, :, :], X[:, :, :], XN[:, :, :], ALU.add)


def centre_and_split(nc, tag, XT, parts_dram, shift_dram, head_of):
    with ExitStack() as stack:
        k = Kit(nc, stack)
        total = k.sb(f"{tag}_total", [P, BATCH])
        rest = k.sb(f"{tag}_rest", [P, TOK])
        parts = k.sb(f"{tag}_parts", [P, 3, TOK], BF16)
        squares = k.sb(f"{tag}_squares", [P, TOK])
        norm2 = k.sb(f"{tag}_norm2", [HEADS, TOK])
        norm = k.sb(f"{tag}_norm", [HEADS, TOK])
        longest = k.sb(f"{tag}_longest", [HEADS, BATCH])
        shift = k.sb(f"{tag}_shift", [HEADS, TOK], BF16)
        norm_ps = k.ps(f"{tag}_norm_ps", [HEADS, TOK])
        step_done = k.sem(f"{tag}_step_done")
        centred = k.sem(f"{tag}_centred")
        part1 = k.sem(f"{tag}_part1")
        rest1 = k.sem(f"{tag}_rest1")
        part2 = k.sem(f"{tag}_part2")
        part3 = k.sem(f"{tag}_part3")
        stored = k.sem(f"{tag}_stored")
        squared = k.sem(f"{tag}_squared")
        norm2_done = k.sem(f"{tag}_norm2_done")
        norm_done = k.sem(f"{tag}_norm_done")
        shift_done = k.sem(f"{tag}_shift_done")
        block = stack.enter_context(nc.Block())
        cut = [slice(b * SEQ, (b + 1) * SEQ) for b in range(BATCH)]

        @block.vector
        def _(dve):
            link = counter(dve, step_done)
            for b, c in enumerate(cut):
                link(dve.tensor_reduce(total[:, b:b + 1], XT[:, c], AX, ALU.add))
                link(dve.tensor_scalar(total[:, b:b + 1], total[:, b:b + 1], 1.0 / SEQ, None, ALU.mult))
                dve.tensor_scalar(XT[:, c], XT[:, c], total[:, b:b + 1], None, ALU.subtract).then_inc(centred, 1)
            for b, c in enumerate(cut):
                dve.wait_ge(centred, b + 1)
                dve.wait_ge(part1, b + 1)
                dve.tensor_tensor(rest[:, c], XT[:, c], parts[:, 0, c], ALU.subtract).then_inc(rest1, 1)
            for b, c in enumerate(cut):
                dve.wait_ge(rest1, b + 1)
                dve.wait_ge(part2, b + 1)
                dve.tensor_tensor(parts[:, 2, c], rest[:, c], parts[:, 1, c], ALU.subtract).then_inc(part3, 1)
            for b, c in enumerate(cut):
                dve.wait_ge(norm_done, 2 * (b + 1))
                link(dve.tensor_reduce(longest[:, b:b + 1], norm[:, c], AX, ALU.max))
                link(dve.scalar_tensor_tensor(out=norm[:, c], in0=norm[:, c], scalar=longest[:, b:b + 1],
                                              in1=norm2[:, c], op0=ALU.mult, op1=ALU.add))
                dve.tensor_scalar(shift[:, c], norm[:, c], -0.5, None, ALU.mult).then_inc(shift_done, 1)

        @block.tensor
        def _(pe):
            for n in range(TOK // BANK):
                pe.wait_ge(squared, n // (SEQ // BANK) + 1)
                pe.matmul(norm_ps[:, n * BANK:(n + 1) * BANK], head_of, squares[:, n * BANK:(n + 1) * BANK],
                          start=True, stop=True).then_inc(norm2_done, 1)

        @block.scalar
        def _(act):
            for b, c in enumerate(cut):
                act.wait_ge(centred, b + 1)
                act.copy(parts[:, 0, c], XT[:, c]).then_inc(part1, 1)
                act.activation(squares[:, c], XT[:, c], ACT.Square).then_inc(squared, 1)
            for b, c in enumerate(cut):
                act.wait_ge(rest1, b + 1)
                act.copy(parts[:, 1, c], rest[:, c]).then_inc(part2, 1)
            for b, c in enumerate(cut):
                act.wait_ge(norm2_done, (b + 1) * (SEQ // BANK))
                act.activation(norm[:, c], norm_ps[:, c], ACT.Sqrt).then_inc(norm_done, 1)
                act.copy(norm2[:, c], norm_ps[:, c]).then_inc(norm_done, 1)

        @block.sync
        def _(sp):
            for b, c in enumerate(cut):
                sp.wait_ge(part3, b + 1)
                sp.dma_start(parts_dram[0].rearrange("s f t -> f s t")[:, :, c], parts[:, :, c]).then_inc(stored, 16)
            for b, c in enumerate(cut):
                sp.wait_ge(shift_done, b + 1)
                sp.dma_start(shift_dram[:, c], shift[:, c]).then_inc(stored, 16)
            sp.wait_ge(stored, 16 * 2 * BATCH)


GROUPS, PER_GROUP = 4, 2
EXPERTS = GROUPS * PER_GROUP
F = 256
FT = EXPERTS * F // P
HALVES = F // P
GATES = GROUPS + EXPERTS
LOOPS = 2
RMS_EPS = 1e-6
GATE_EPS = 1e-9
CT = CHUNK // P
CHUNKS = TOK // CHUNK


def mixture(nc, tag, Z, w, ident):
    UP_BANKS = 2
    NC = LOOPS * CHUNKS
    with ExitStack() as stack:
        k = Kit(nc, stack)
        scratch = k.sb(f"{tag}_scratch", [P, CT, D])
        ms = k.sb(f"{tag}_ms", [P, CT])
        std = k.sb(f"{tag}_std", [P, CT])
        eps = k.sb(f"{tag}_eps", [P, 1])
        ZT = k.sb(f"{tag}_ZT", [P, 2, CHUNK])
        logits = k.sb(f"{tag}_logits", [P, CT, GATES])
        exps = k.sb(f"{tag}_exps", [P, CT, GATES])
        top = k.sb(f"{tag}_top", [P, CT, 1 + GROUPS])
        total = k.sb(f"{tag}_total", [P, CT, 1 + GROUPS])
        beats = k.sb(f"{tag}_beats", [P, CT, GROUPS, GROUPS])
        ties = k.sb(f"{tag}_ties", [P, CT, GROUPS, GROUPS])
        rank = k.sb(f"{tag}_rank", [P, CT, GROUPS])
        pair = k.sb(f"{tag}_pair", [P, CT])
        best = k.sb(f"{tag}_best", [P, CT, GROUPS])
        inv_best = k.sb(f"{tag}_inv_best", [P, CT, GROUPS])
        second = k.sb(f"{tag}_second", [P, CT, GROUPS])
        combine = k.sb(f"{tag}_combine", [P, 2, CT, EXPERTS])
        hidden = k.sb(f"{tag}_hidden", [P, FT, CHUNK])
        weighted = k.sb(f"{tag}_weighted", [P, EXPERTS, D])
        mixed = k.sb(f"{tag}_mixed", [P, D])
        turned_ps = k.ps(f"{tag}_turned_ps", [P, CT, P])
        gate_ps = k.ps(f"{tag}_gate_ps", [P, BANK])
        up_ps = k.ps(f"{tag}_up_ps", [P, UP_BANKS, BANK])
        down_ps = k.ps(f"{tag}_down_ps", [P, 2, EXPERTS, D])
        chain = k.sem(f"{tag}_chain")
        ms_ready = k.sem(f"{tag}_ms_ready")
        std_ready = k.sem(f"{tag}_std_ready")
        normed = k.sem(f"{tag}_normed")
        turned = k.sem(f"{tag}_turned")
        zt_out = k.sem(f"{tag}_zt_out")
        gated = k.sem(f"{tag}_gated")
        logits_out = k.sem(f"{tag}_logits_out")
        shifted = k.sem(f"{tag}_shifted")
        exped = k.sem(f"{tag}_exped")
        up_done = k.sem(f"{tag}_up_done")
        silu_done = k.sem(f"{tag}_silu_done")
        down_done = k.sem(f"{tag}_down_done")
        down_out = k.sem(f"{tag}_down_out")
        summed = k.sem(f"{tag}_summed")
        z_added = k.sem(f"{tag}_z_added")
        block = stack.enter_context(nc.Block())

        def over_chunks(engine, chunk):
            with engine.Fori(0, NC // 2 - 1) as i:
                chunk(i * 2, 0, False)
                chunk(i * 2 + 1, 1, False)
            chunk(NC - 2, 0, False)
            chunk(NC - 1, 1, True)

        @block.tensor
        def _(pe):
            pe.sem_inc(down_done, CT)

            def turn(m):
                pe.wait_ge(normed, m + 1)
                pe.wait_ge(zt_out, m + 1)
                for t in range(CT):
                    last = pe.transpose(turned_ps[:, t, :], scratch[:, t, :], ident)
                last.then_inc(turned, 1)

            def gates(m, half):
                pe.wait_ge(zt_out, m + 2)
                pe.wait_ge(logits_out, m + 1)
                for t in range(CT):
                    last = pe.matmul(gate_ps[:, t * GATES:(t + 1) * GATES], ZT[:, half, t * P:(t + 1) * P],
                                     w["gates"], start=True, stop=True)
                last.then_inc(gated, 1)

            def chunk(n, half, final):
                for f in range(FT):
                    pe.wait_ge(silu_done, n * FT + (f + 1))
                    pe.matmul(up_ps[:, f % UP_BANKS, :], w["w1"][:, f * P:(f + 1) * P], ZT[:, half, :],
                              start=True, stop=True).then_inc(up_done, 1)
                pe.wait_ge(silu_done, n * FT + (FT + UP_BANKS))
                for t in range(CT):
                    pe.wait_ge(down_out, n * CT + (t + 1))
                    for e in range(EXPERTS):
                        for h in range(HALVES):
                            last = pe.matmul(down_ps[:, t % 2, e, :],
                                             hidden[:, e * HALVES + h, t * P:(t + 1) * P],
                                             w["w2"][:, e * HALVES + h, :], start=(h == 0),
                                             stop=(h == HALVES - 1))
                    last.then_inc(down_done, 1)
                    if t == 0 and not final:
                        turn(n + 1)
                    if t == 1 and not final:
                        gates(n + 1, 1 - half)

            turn(0)
            gates(0, 0)
            over_chunks(pe, chunk)

        @block.scalar
        def _(act):
            act.sem_inc(silu_done, UP_BANKS)
            act.sem_inc(zt_out, 1)

            def prepare(m, half):
                act.wait_ge(ms_ready, m + 1)
                act.activation(std[:, :], ms[:, :], ACT.Sqrt, bias=eps[:, 0:1], scale=1.0 / D).then_inc(std_ready, 1)
                act.wait_ge(turned, m + 1)
                act.activation(ZT[:, half, :], turned_ps[:, :, :].rearrange("p t q -> p (t q)"), ACT.Copy,
                               scale=w["norm"]).then_inc(zt_out, 1)
                act.wait_ge(shifted, m + 1)
                act.activation(exps[:, :, :], logits[:, :, :], ACT.Exp).then_inc(exped, 1)

            def chunk(n, half, final):
                act.wait_ge(down_done, n * CT + CT)
                for f in range(FT):
                    act.wait_ge(up_done, n * FT + (f + 1))
                    act.activation(hidden[:, f, :], up_ps[:, f % UP_BANKS, :], ACT.Silu).then_inc(silu_done, 1)
                if not final:
                    prepare(n + 1, 1 - half)

            prepare(0, 0)
            over_chunks(act, chunk)

        @block.vector
        def _(dve):
            LINKS = 29
            dve.sem_inc(down_out, 2)
            dve.sem_inc(logits_out, 1)
            dve.sem_inc(z_added, TILES)
            dve.memset(eps[:], RMS_EPS).then_inc(chain, 1)
            dve.wait_ge(chain, 1)

            def chunk_rows(m):
                return Z[:, bass.ds(m * CT, CT), :]

            def mean_square(m, link):
                dve.wait_ge(z_added, m * CT + CT)
                link(dve.tensor_tensor(scratch[:, :, :], chunk_rows(m), chunk_rows(m), ALU.mult))
                dve.tensor_reduce(ms[:, :], scratch[:, :, :], AX, ALU.add).then_inc(ms_ready, 1)

            def normalised(m, link):
                dve.wait_ge(std_ready, m + 1)
                link(dve.reciprocal(std[:, :], std[:, :]))
                dve.tensor_tensor(scratch[:, :, :], chunk_rows(m), over(std[:, :], D), ALU.mult).then_inc(normed, 1)

            def shifted_logits(m, link):
                dve.wait_ge(gated, m + 1)
                dve.tensor_copy(logits[:, :, :], gate_ps[:, 0:CT * GATES].rearrange("p (t g) -> p t g", g=GATES)
                                ).then_inc(logits_out, 1)
                dve.wait_ge(logits_out, m + 2)
                coarse = logits[:, :, 0:GROUPS]
                fine = logits[:, :, GROUPS:].rearrange("p t (g e) -> p t g e", e=PER_GROUP)
                link(dve.tensor_reduce(top[:, :, 0], coarse, AX, ALU.max))
                link(dve.tensor_reduce(top[:, :, 1:], fine, AX, ALU.max))
                link(dve.tensor_tensor(coarse, coarse, over(top[:, :, 0], GROUPS), ALU.subtract))
                dve.tensor_tensor(fine, fine, over(top[:, :, 1:], PER_GROUP), ALU.subtract).then_inc(shifted, 1)

            def gate_weights(m, half, link):
                dve.wait_ge(exped, m + 1)
                coarse = exps[:, :, 0:GROUPS]
                fine = exps[:, :, GROUPS:].rearrange("p t (g e) -> p t g e", e=PER_GROUP)
                link(dve.tensor_reduce(total[:, :, 0], coarse, AX, ALU.add))
                link(dve.tensor_reduce(total[:, :, 1:], fine, AX, ALU.add))
                link(dve.reciprocal(total[:, :, :], total[:, :, :]))
                link(dve.tensor_tensor(coarse, coarse, over(total[:, :, 0], GROUPS), ALU.mult))
                link(dve.tensor_tensor(fine, fine, over(total[:, :, 1:], PER_GROUP), ALU.mult))
                mine = over(coarse, GROUPS)
                others = coarse.unsqueeze(2).to_broadcast([P, CT, GROUPS, GROUPS])
                before = w["before"].unsqueeze(1).to_broadcast([P, CT, GROUPS, GROUPS])
                link(dve.tensor_tensor(beats[:, :, :, :], others, mine, ALU.is_gt))
                link(dve.tensor_tensor(ties[:, :, :, :], others, mine, ALU.is_equal))
                link(dve.tensor_tensor(ties[:, :, :, :], ties[:, :, :, :], before, ALU.mult))
                link(dve.tensor_tensor(beats[:, :, :, :], beats[:, :, :, :], ties[:, :, :, :], ALU.add))
                link(dve.tensor_reduce(rank[:, :, :], beats[:, :, :, :], AX, ALU.add))
                link(dve.tensor_scalar(rank[:, :, :], rank[:, :, :], 2.0, None, ALU.is_lt))
                link(dve.tensor_tensor(rank[:, :, :], rank[:, :, :], coarse, ALU.mult))
                link(dve.tensor_reduce(pair[:, :], rank[:, :, :], AX, ALU.add))
                link(dve.tensor_scalar(pair[:, :], pair[:, :], GATE_EPS, None, ALU.add))
                link(dve.reciprocal(pair[:, :], pair[:, :]))
                link(dve.tensor_tensor(rank[:, :, :], rank[:, :, :], over(pair[:, :], GROUPS), ALU.mult))
                link(dve.tensor_reduce(best[:, :, :], fine, AX, ALU.max))
                link(dve.tensor_scalar(inv_best[:, :, :], best[:, :, :], GATE_EPS, None, ALU.add))
                link(dve.reciprocal(inv_best[:, :, :], inv_best[:, :, :]))
                link(dve.tensor_tensor(best[:, :, :], best[:, :, :], inv_best[:, :, :], ALU.mult))
                link(dve.tensor_tensor(rank[:, :, :], rank[:, :, :], best[:, :, :], ALU.mult))
                link(dve.tensor_tensor(second[:, :, :], fine[:, :, :, 1], fine[:, :, :, 0], ALU.is_gt))
                out = combine[:, half, :, :].rearrange("p t (g e) -> p t g e", e=PER_GROUP)
                link(dve.tensor_tensor(out[:, :, :, 1], rank[:, :, :], second[:, :, :], ALU.mult))
                link(dve.tensor_tensor(out[:, :, :, 0], rank[:, :, :], out[:, :, :, 1], ALU.subtract))

            def mix(n, half, t):
                tile = n * CT + t
                dve.wait_ge(down_done, tile + (1 + CT))
                dve.tensor_tensor(weighted[:, :, :], down_ps[:, t % 2, :, :], over(combine[:, half, t, :], D),
                                  ALU.mult).then_inc(down_out, 1)
                dve.wait_ge(down_out, tile + 3)
                dve.tensor_reduce(mixed[:, :], weighted[:, :, :].rearrange("p e d -> p d e"), AX,
                                  ALU.add).then_inc(summed, 1)
                dve.wait_ge(summed, tile + 1)
                now, then = (Z[:, bass.ds(at, 1), :].rearrange("p o d -> p (o d)") for at in (tile, tile + TILES))
                dve.tensor_tensor(then, now, mixed[:, :], ALU.add).then_inc(z_added, 1)

            def chunk(n, half, final):
                link = counter(dve, chain, n * LINKS + (1 + LINKS))
                if final:
                    for t in range(CT):
                        mix(n, half, t)
                    return
                mean_square(n + 1, link)
                normalised(n + 1, link)
                mix(n, half, 0)
                shifted_logits(n + 1, link)
                mix(n, half, 1)
                mix(n, half, 2)
                gate_weights(n + 1, 1 - half, link)
                mix(n, half, 3)
                assert link.count[0] == LINKS, link.count[0]

            link = counter(dve, chain, 1)
            mean_square(0, link)
            normalised(0, link)
            shifted_logits(0, link)
            gate_weights(0, 0, link)
            assert link.count[0] == LINKS, link.count[0]
            over_chunks(dve, chunk)


def moe_ffn(nc, tag, X, w, ident, fetch):
    with ExitStack() as stack:
        k = Kit(nc, stack)
        Z = k.sb(f"{tag}_Z", [P, (LOOPS + 1) * TILES, D])
        before = k.sb(f"{tag}_before", [P, GROUPS, GROUPS])
        zeroed = k.sem(f"{tag}_zeroed")

        def mark_before(pool):
            pool.memset(before[:, :, :], 0.0).then_inc(zeroed, 1)
            pool.wait_ge(zeroed, 1)
            for g in range(1, GROUPS):
                pool.memset(before[:, g, 0:g], 1.0)
        w["before"] = before[:, :, :]
        layer_norm(nc, f"{tag}_ln", X, Z[:, 0:TILES, :], None, ident, beside={"sync": fetch, "gpsimd": mark_before})
        mixture(nc, f"{tag}_mix", Z[:, :, :], w, ident)
        with nc.Block() as block:
            @block.vector
            def _(dve):
                dve.tensor_tensor(X[:, :, :], X[:, :, :], Z[:, LOOPS * TILES:, :], ALU.add)


STEPS = BATCH
FH, FD = 16, 64
FW = FH * FD


def fast_weights(nc, tag, X, w, ident, fetch):
    with ExitStack() as stack:
        k = Kit(nc, stack)
        H = k.sb(f"{tag}_H", [P, TILES, D])
        HT = k.sb(f"{tag}_HT", [P, TOK])
        layer_norm(nc, f"{tag}_ln", X, H, HT, ident, beside={"sync": fetch})
        recur(nc, f"{tag}_recur", H, HT[:, :], w, ident)
        layer_norm(nc, f"{tag}_ln2", H, H, None, ident, gain=w["ln_g"], shift=w["ln_b"])
        with nc.Block() as block:
            @block.vector
            def _(dve):
                dve.tensor_tensor(X[:, :, :], X[:, :, :], H[:, :, :], ALU.add)


def recur(nc, tag, H, HT, w, ident):
    with ExitStack() as stack:
        k = Kit(nc, stack)
        kk = k.sb(f"{tag}_kk", [P, STEPS, STEPS, TPB, FH])
        kq = k.sb(f"{tag}_kq", [P, STEPS, STEPS, TPB, FH])
        sums = k.sb(f"{tag}_sums", [P, 2, STEPS, TPB, FH])
        dots(nc, f"{tag}_dots", HT, w, kk, kq, sums)
        combine_values(nc, f"{tag}_values", H, HT, w, kk, kq, sums, ident)


def heads(ap):
    return ap.rearrange("p s (h e) -> p s h e", e=FD)


def one(ap):
    return ap.rearrange("p s o h -> p s (o h)")


def stage_tokens(act, HT, ht, b):
    src = HT.rearrange("p (s t) -> p s t", s=STEPS)[:, :, bass.ds(b * P, P)]
    return act.copy(ht, src)


def dots(nc, tag, HT, w, kk, kq, sums):
    PAIR = 2 * STEPS
    SLOTS = 4
    ORDER = (("kk", 1, 0, 1), ("kk", 2, 0, 2), ("kq", 0, 0, 1), ("kq", 1, 0, 2), ("kq", 2, 0, 2), ("kq", 2, 2, 3),
             ("kq", 3, 0, 2), ("kq", 3, 2, 4))
    RING = 4
    with ExitStack() as stack:
        k = Kit(nc, stack)
        ht = k.sb(f"{tag}_ht", [P, 2, STEPS, P])
        vecs = k.sb(f"{tag}_vecs", [P, 2, PAIR, FW])
        low = k.sb(f"{tag}_low", [P, 2, FW])
        prod = k.sb(f"{tag}_prod", [P, RING, 2, FW])
        prod3 = k.sb(f"{tag}_prod3", [P, STEPS - 1, FW])
        vec_ps = k.ps(f"{tag}_vec_ps", [P, SLOTS, FW])
        ht_set = k.sem(f"{tag}_ht_set")
        projected = k.sem(f"{tag}_projected")
        negated = k.sem(f"{tag}_negated")
        low_done = k.sem(f"{tag}_low_done")
        vec_out = k.sem(f"{tag}_vec_out")
        prod_done = k.sem(f"{tag}_prod_done")
        reduced = k.sem(f"{tag}_reduced")
        prod3_done = k.sem(f"{tag}_prod3_done")
        block = stack.enter_context(nc.Block())

        @block.tensor
        def _(pe):
            with pe.Fori(0, TPB // 2) as i:
                for half in range(2):
                    b = i * 2 + half
                    pe.wait_ge(ht_set, b + 1)
                    for u in range(PAIR):
                        pe.wait_ge(vec_out, b * PAIR + (u + 1))
                        at = (FW if u < STEPS else 0) + 0
                        for c in range(FW // BANK):
                            last = pe.matmul(vec_ps[:, u % SLOTS, c * BANK:(c + 1) * BANK],
                                             ht[:, half, u % STEPS, :],
                                             w["qkv"][:, at + c * BANK:at + (c + 1) * BANK],
                                             start=True, stop=True)
                        last.then_inc(projected, 1)

        @block.scalar
        def _(act):
            def tile(b, half, last):
                if not last:
                    stage_tokens(act, HT, ht[:, 1 - half, :, :], b + 1).then_inc(ht_set, 1)
                for u in range(PAIR):
                    n = b * PAIR + (u + 1)
                    act.wait_ge(projected, n)
                    act.wait_ge(vec_out, n + 2)
                    act.activation(low[:, u % 2, :], vec_ps[:, u % SLOTS, :], ACT.Relu,
                                   scale=-1.0).then_inc(negated, 1)
                    act.wait_ge(negated, n)
                    act.activation(low[:, u % 2, :], low[:, u % 2, :], ACT.Exp,
                                   scale=-1.0).then_inc(low_done, 1)

            stage_tokens(act, HT, ht[:, 0, :, :], 0).then_inc(ht_set, 1)
            tile(0, 0, False)
            with act.Fori(0, TPB // 2 - 1) as i:
                tile(i * 2 + 1, 1, False)
                tile(i * 2 + 2, 0, False)
            tile(TPB - 1, 1, True)

        @block.gpsimd
        def _(pool):
            with pool.Fori(0, TPB // 2) as i:
                for half in range(2):
                    b = i * 2 + half
                    for m, (kind, t, s0, s1) in enumerate(ORDER):
                        other = t if kind == "kk" else STEPS + t
                        pool.wait_ge(vec_out, b * PAIR + (other + 1 + SLOTS))
                        pool.wait_ge(reduced, b * len(ORDER) + (m + 1))
                        pool.tensor_tensor(prod[:, m % RING, 0:s1 - s0, :], vecs[:, half, s0:s1, :],
                                           vecs[:, half, other:other + 1, :].to_broadcast([P, s1 - s0, FW]),
                                           ALU.mult).then_inc(prod_done, 1)

        @block.vector
        def _(dve):
            dve.sem_inc(vec_out, SLOTS)
            dve.sem_inc(reduced, RING)

            def take(b, half, u):
                dve.wait_ge(low_done, b * PAIR + (u + 1))
                dve.scalar_tensor_tensor(out=vecs[:, half, u, :], in0=vec_ps[:, u % SLOTS, :], scalar=0.0,
                                         in1=low[:, u % 2, :], op0=ALU.max, op1=ALU.add).then_inc(vec_out, 1)

            def reduce(b, m):
                kind, t, s0, s1 = ORDER[m]
                dve.wait_ge(prod_done, b * len(ORDER) + (m + 1))
                dst = (kk if kind == "kk" else kq)[:, t, s0:s1, bass.ds(b, 1), :]
                dve.tensor_reduce(one(dst), heads(prod[:, m % RING, 0:s1 - s0, :]), AX, ALU.add).then_inc(reduced, 1)

            def last_keys(b, half):
                n = STEPS - 1
                dve.tensor_tensor(prod3[:, :, :], vecs[:, half, 0:n, :],
                                  vecs[:, half, n:n + 1, :].to_broadcast([P, n, FW]), ALU.mult).then_inc(prod3_done, 1)
                for which in range(2):
                    dve.tensor_reduce(one(sums[:, which, :, bass.ds(b, 1), :]),
                                      heads(vecs[:, half, which * STEPS:(which + 1) * STEPS, :]), AX, ALU.add)
                dve.wait_ge(prod3_done, b + 1)
                dve.tensor_reduce(one(kk[:, n, 0:n, bass.ds(b, 1), :]), heads(prod3[:, :, :]), AX, ALU.add)

            def tile(b, half):
                for u in range(PAIR):
                    take(b, half, u)
                    if u == 0:
                        dve.wait_ge(vec_out, b * PAIR + SLOTS)
                        last_keys(b - 1, 1 - half)
                    reduce(b - 1, u)

            for u in range(PAIR):
                take(0, 0, u)
            with dve.Fori(0, TPB // 2 - 1) as i:
                tile(i * 2 + 1, 1)
                tile(i * 2 + 2, 0)
            tile(TPB - 1, 1)
            dve.wait_ge(vec_out, TPB * PAIR + SLOTS)
            last_keys(TPB - 1, 1)
            for m in range(len(ORDER)):
                reduce(TPB - 1, m)


def combine_values(nc, tag, H, HT, w, kk, kq, sums, ident):
    with ExitStack() as stack:
        k = Kit(nc, stack)
        ht = k.sb(f"{tag}_ht", [P, 2, STEPS, P])
        v = k.sb(f"{tag}_v", [P, 2, STEPS, FW])
        prod1 = k.sb(f"{tag}_prod1", [P, 2, 2, FW])
        prod2 = k.sb(f"{tag}_prod2", [P, 2, 3, FW])
        prod3 = k.sb(f"{tag}_prod3", [P, 4, FW])
        mixed = k.sb(f"{tag}_mixed", [P, 2, FW])
        mixed_t = k.sb(f"{tag}_mixed_t", [P, 2, FW // P, P])
        beta = k.sb(f"{tag}_beta", [P, STEPS, TPB, FH])
        lower = mixed[:, :, :].rearrange("p a (t r b h) -> p (a t) r b h", t=2, r=STEPS, b=TPB)
        coef = k.sb(f"{tag}_coef", [P, STEPS, STEPS, TPB, FH])
        term = k.sb(f"{tag}_term", [P, STEPS, TPB, FH])
        v_ps = k.ps(f"{tag}_v_ps", [P, 2, FW])
        turned_ps = k.ps(f"{tag}_turned_ps", [P, FW // P, P])
        y_ps = k.ps(f"{tag}_y_ps", [P, 2, BANK])
        beta_ps = y_ps[:, 1, :].rearrange("p (t h) -> p t h", h=FH)
        beta_done = k.sem(f"{tag}_beta_done")
        beta_exp = k.sem(f"{tag}_beta_exp")
        chain = k.sem(f"{tag}_chain")
        coef_done = k.sem(f"{tag}_coef_done")
        ht_set = k.sem(f"{tag}_ht_set")
        projected = k.sem(f"{tag}_projected")
        v_out = k.sem(f"{tag}_v_out")
        scaled = k.sem(f"{tag}_scaled")
        scaled3 = k.sem(f"{tag}_scaled3")
        summing = k.sem(f"{tag}_summing")
        mixed_done = k.sem(f"{tag}_mixed_done")
        turned = k.sem(f"{tag}_turned")
        copied = k.sem(f"{tag}_copied")
        attended = k.sem(f"{tag}_attended")
        added = k.sem(f"{tag}_added")
        block = stack.enter_context(nc.Block())

        @block.tensor
        def _(pe):
            pe.sem_inc(turned, 2)
            pe.sem_inc(attended, 2)

            def project(b, half, s):
                pe.wait_ge(v_out, b * STEPS + (s + 1))
                for c in range(FW // BANK):
                    at = 2 * FW + c * BANK
                    last = pe.matmul(v_ps[:, s % 2, c * BANK:(c + 1) * BANK], ht[:, half, s, :],
                                     w["qkv"][:, at:at + BANK], start=True, stop=True)
                last.then_inc(projected, 1)

            def tile(b, half, final):
                if not final:
                    pe.wait_ge(ht_set, b + 2)
                for t in range(STEPS):
                    n = b * STEPS + (t + 1)
                    pe.wait_ge(mixed_done, n + STEPS)
                    pe.wait_ge(copied, n)
                    for c in range(FW // P):
                        last = pe.transpose(turned_ps[:, c, :], mixed[:, t % 2, c * P:(c + 1) * P], ident)
                    last.then_inc(turned, 1)
                    if not final:
                        project(b + 1, 1 - half, t)
                    pe.wait_ge(copied, n + 1)
                    pe.wait_ge(added, n)
                    for c in range(FW // P):
                        last = pe.matmul(y_ps[:, t % 2, 0:D], mixed_t[:, t % 2, c, :], w["out"][:, c, :],
                                         start=(c == 0), stop=(c == FW // P - 1))
                    last.then_inc(attended, 1)

            for t in range(TILES):
                last = pe.matmul(beta_ps[:, t, :], HT[:, t * P:(t + 1) * P], w["qkv"][:, 3 * FW:3 * FW + FH],
                                 start=True, stop=True)
            last.then_inc(beta_done, 1)
            pe.wait_ge(ht_set, 1)
            for s in range(STEPS):
                project(0, 0, s)
            with pe.Fori(0, TPB // 2 - 1) as i:
                tile(i * 2, 0, False)
                tile(i * 2 + 1, 1, False)
            tile(TPB - 2, 0, False)
            tile(TPB - 1, 1, True)

        @block.scalar
        def _(act):
            act.sem_inc(v_out, 2)
            act.sem_inc(copied, 1)

            def take_value(b, half, s):
                act.wait_ge(projected, b * STEPS + (s + 1))
                act.copy(v[:, half, s, :], v_ps[:, s % 2, :]).then_inc(v_out, 1)

            def tile(b, half, final):
                if not final:
                    stage_tokens(act, HT, ht[:, 1 - half, :, :], b + 1).then_inc(ht_set, 1)
                for t in range(STEPS):
                    n = b * STEPS + (t + 1)
                    act.wait_ge(turned, n + 2)
                    act.wait_ge(attended, n)
                    act.copy(mixed_t[:, t % 2, :, :], turned_ps[:, :, :]).then_inc(copied, 1)
                    if not final:
                        if t == 0:
                            act.wait_ge(mixed_done, b * STEPS + STEPS)
                        take_value(b + 1, 1 - half, t)

            act.wait_ge(beta_done, 1)
            act.activation(beta[:, :, :, :].rearrange("p s b h -> p (s b) h"), beta_ps[:, :, :], ACT.Exp,
                           scale=-1.0).then_inc(beta_exp, 1)
            stage_tokens(act, HT, ht[:, 0, :, :], 0).then_inc(ht_set, 1)
            for s in range(STEPS):
                take_value(0, 0, s)
            with act.Fori(0, TPB // 2 - 1) as i:
                tile(i * 2, 0, False)
                tile(i * 2 + 1, 1, False)
            tile(TPB - 2, 0, False)
            tile(TPB - 1, 1, True)

        def of_tile(b, t, n):
            return over(one(coef[:, t, 0:n, bass.ds(b, 1), :]), FD)

        @block.gpsimd
        def _(pool):
            pool.wait_ge(coef_done, 1)
            with pool.Fori(0, TPB // 2) as i:
                for half in range(2):
                    b = i * 2 + half
                    for t, prod in ((1, prod1), (2, prod2)):
                        pool.wait_ge(v_out, b * STEPS + (t + 3))
                        pool.tensor_tensor(heads(prod[:, half, :, :]), heads(v[:, half, 0:t + 1, :]),
                                           of_tile(b, t, t + 1), ALU.mult).then_inc(scaled, 1)

        @block.vector
        def _(dve):
            dve.sem_inc(mixed_done, STEPS)
            dve.sem_inc(added, 2)
            link = counter(dve, chain)
            link(dve.reciprocal(sums[:, :, :, :, :], sums[:, :, :, :, :]))
            inv_k, inv_q = sums[:, 0, :, :, :], sums[:, 1, :, :, :]
            link(dve.tensor_scalar(inv_q, inv_q, FD ** -0.5, None, ALU.mult))
            for t in range(STEPS):
                for table, inv, n in ((kk, inv_k, t), (kq, inv_q, t + 1)):
                    if n:
                        row = table[:, t, 0:n, :, :]
                        link(dve.tensor_tensor(row, row, inv_k[:, 0:n, :, :], ALU.mult))
                        link(dve.tensor_tensor(row, row, inv[:, t:t + 1, :, :].to_broadcast([P, n, TPB, FH]), ALU.mult))
            dve.wait_ge(beta_exp, 1)
            link(dve.tensor_scalar(beta[:, :, :, :], beta[:, :, :, :], 1.0, None, ALU.add))
            link(dve.reciprocal(beta[:, :, :, :], beta[:, :, :, :]))

            def by(table, t, s):
                return table[:, t, s:s + 1, :, :].to_broadcast([P, s + 1, TPB, FH])
            for t in range(STEPS):
                link(dve.tensor_copy(lower[:, t, t, :, :], beta[:, t, :, :]))
                if t:
                    link(dve.memset(lower[:, t, 0:t, :, :], 0.0))
                for s in range(t):
                    link(dve.tensor_tensor(term[:, 0:s + 1, :, :], lower[:, s, 0:s + 1, :, :], by(kk, t, s), ALU.mult))
                    link(dve.tensor_tensor(lower[:, t, 0:s + 1, :, :], lower[:, t, 0:s + 1, :, :],
                                           term[:, 0:s + 1, :, :], ALU.subtract))
                if t:
                    link(dve.tensor_tensor(lower[:, t, 0:t, :, :], lower[:, t, 0:t, :, :],
                                           beta[:, t:t + 1, :, :].to_broadcast([P, t, TPB, FH]), ALU.mult))
            for t in range(STEPS):
                for s in range(t, -1, -1):
                    dst = coef[:, t, 0:s + 1, :, :] if s == t else term[:, 0:s + 1, :, :]
                    link(dve.tensor_tensor(dst, lower[:, s, 0:s + 1, :, :], by(kq, t, s), ALU.mult))
                    if s < t:
                        link(dve.tensor_tensor(coef[:, t, 0:s + 1, :, :], coef[:, t, 0:s + 1, :, :],
                                               term[:, 0:s + 1, :, :], ALU.add))
            dve.sem_inc(coef_done, 1)

            def add_output(b, t):
                dve.wait_ge(attended, b * STEPS + (t + 3))
                h = H[:, bass.ds(t * TPB + b, 1), :].rearrange("p o d -> p (o d)")
                dve.tensor_tensor(h, h, y_ps[:, t % 2, 0:D], ALU.add).then_inc(added, 1)

            def tile(b, half, first):
                def room(t):
                    dve.wait_ge(turned, b * STEPS + (t + 1))
                dve.wait_ge(v_out, b * STEPS + 3)
                room(0)
                dve.tensor_tensor(heads(mixed[:, 0:1, :]), heads(v[:, half, 0:1, :]), of_tile(b, 0, 1),
                                  ALU.mult).then_inc(mixed_done, 1)
                if not first:
                    add_output(b - 1, STEPS - 1)
                dve.wait_ge(v_out, b * STEPS + (STEPS + 2))
                dve.tensor_tensor(heads(prod3[:, :, :]), heads(v[:, half, :, :]), of_tile(b, 3, 4),
                                  ALU.mult).then_inc(scaled3, 1)
                dve.wait_ge(scaled, b * 2 + 1)
                room(1)
                dve.tensor_tensor(mixed[:, 1, :], prod1[:, half, 0, :], prod1[:, half, 1, :], ALU.add).then_inc(mixed_done, 1)
                add_output(b, 0)
                dve.wait_ge(scaled3, b + 1)
                dve.tensor_tensor(prod3[:, 0:2, :], prod3[:, 0:2, :], prod3[:, 2:4, :], ALU.add).then_inc(summing, 1)
                dve.wait_ge(scaled, b * 2 + 2)
                dve.tensor_tensor(prod2[:, half, 0, :], prod2[:, half, 0, :], prod2[:, half, 1, :], ALU.add).then_inc(summing, 1)
                dve.wait_ge(summing, b * 2 + 2)
                room(2)
                dve.tensor_tensor(mixed[:, 0, :], prod2[:, half, 0, :], prod2[:, half, 2, :], ALU.add).then_inc(mixed_done, 1)
                add_output(b, 1)
                room(3)
                dve.tensor_tensor(mixed[:, 1, :], prod3[:, 0, :], prod3[:, 1, :], ALU.add).then_inc(mixed_done, 1)
                add_output(b, 2)

            dve.wait_ge(coef_done, 1)
            tile(0, 0, True)
            with dve.Fori(0, TPB // 2 - 1) as i:
                tile(i * 2 + 1, 1, False)
                tile(i * 2 + 2, 0, False)
            tile(TPB - 1, 1, False)
            add_output(TPB - 1, STEPS - 1)


LE, LR = 8, 8
LORA_SCALE = 16 / LR


def lora_ffn(nc, tag, X, w, ident, fetch):
    with ExitStack() as stack:
        k = Kit(nc, stack)
        XN = k.sb(f"{tag}_XN", [P, TILES, D])
        XT = k.sb(f"{tag}_XT", [P, TOK])
        layer_norm(nc, f"{tag}_ln", X, XN, XT, ident, beside={"sync": fetch})
        small = k.sb(f"{tag}_small", [P, TILES, LE + LR])
        top = k.sb(f"{tag}_top", [P, TILES])
        gates = k.sb(f"{tag}_gates", [P, TILES, LE], BF16)
        outer = k.sb(f"{tag}_outer", [P, TILES, LE * LR])
        outer_t = k.sb(f"{tag}_outer_t", [LE * LR, 2, 4, P])
        small_ps = k.ps(f"{tag}_small_ps", [P, TILES, LE + LR])
        t_ps = k.ps(f"{tag}_t_ps", [LE * LR, 2, 4, P])
        y_ps = k.ps(f"{tag}_y_ps", [P, 2, 4, D])
        small_done = k.sem(f"{tag}_small_done")
        step_done = k.sem(f"{tag}_step_done")
        shifted = k.sem(f"{tag}_shifted")
        exped = k.sem(f"{tag}_exped")
        outer_done = k.sem(f"{tag}_outer_done")
        turned = k.sem(f"{tag}_turned")
        copied = k.sem(f"{tag}_copied")
        projected = k.sem(f"{tag}_projected")
        added = k.sem(f"{tag}_added")
        block = stack.enter_context(nc.Block())
        LSTEPS = TILES // 4

        @block.tensor
        def _(pe):
            for t in range(TILES):
                last = pe.matmul(small_ps[:, t, :], XT[:, t * P:(t + 1) * P], w["lora"][:, D:D + LE + LR],
                                 start=True, stop=True)
            last.then_inc(small_done, 1)

            def turn(s):
                if s >= 2:
                    pe.wait_ge(copied, s - 1)
                for t in range(4):
                    last = pe.transpose(t_ps[:, s % 2, t, :], outer[:, 4 * s + t, :], ident)
                last.then_inc(turned, 1)
            pe.wait_ge(outer_done, 1)
            turn(0)
            for s in range(LSTEPS):
                if s + 1 < LSTEPS:
                    turn(s + 1)
                pe.wait_ge(copied, s + 1)
                if s >= 2:
                    pe.wait_ge(added, s - 1)
                for t in range(4):
                    tile = 4 * s + t
                    pe.matmul(y_ps[:, s % 2, t, :], XT[:, tile * P:(tile + 1) * P], w["lora"][:, 0:D],
                              start=True, stop=False)
                    last = pe.matmul(y_ps[:, s % 2, t, :], outer_t[:, s % 2, t, :], w["lora_b"],
                                     start=False, stop=True)
                last.then_inc(projected, 1)

        @block.scalar
        def _(act):
            act.wait_ge(shifted, 1)
            act.activation(small[:, :, 0:LE], small[:, :, 0:LE], ACT.Exp).then_inc(exped, 1)
            for s in range(LSTEPS):
                act.wait_ge(turned, s + 1)
                if s >= 2:
                    act.wait_ge(projected, s - 1)
                act.copy(outer_t[:, s % 2, :, :], t_ps[:, s % 2, :, :]).then_inc(copied, 1)

        @block.vector
        def _(dve):
            link = counter(dve, step_done)
            dve.wait_ge(small_done, 1)
            logits, mid = small[:, :, 0:LE], small[:, :, LE:]
            link(dve.tensor_tensor(logits, small_ps[:, :, 0:LE], over_mid(w["router_b"], TILES), ALU.add))
            link(dve.tensor_scalar(mid, small_ps[:, :, LE:], LORA_SCALE, None, ALU.mult))
            link(dve.tensor_reduce(top[:, :], logits, AX, ALU.max))
            dve.tensor_tensor(logits, logits, over(top[:, :], LE), ALU.subtract).then_inc(shifted, 1)
            dve.wait_ge(exped, 1)
            link(dve.tensor_reduce(top[:, :], logits, AX, ALU.add))
            link(dve.reciprocal(top[:, :], top[:, :]))
            link(dve.tensor_tensor(gates[:, :, :], logits, over(top[:, :], LE), ALU.mult))
            dve.tensor_tensor(outer[:, :, :].rearrange("p t (e r) -> p t e r", r=LR), over(gates[:, :, :], LR),
                              mid.unsqueeze(2).to_broadcast([P, TILES, LE, LR]), ALU.mult).then_inc(outer_done, 1)
            for s in range(LSTEPS):
                x = X[:, 4 * s:4 * s + 4, :]
                link(dve.tensor_tensor(x, x, over_mid(w["base_b"], 4), ALU.add))
                dve.wait_ge(projected, s + 1)
                dve.tensor_tensor(x, x, y_ps[:, s % 2, :, :], ALU.add).then_inc(added, 1)


WEIGHTS = {
    "a": {"qkv": [P, 3 * D], "out": [P, D], "b_qk": [P, 2], "b_v": [D], "b_out": [D]},
    "b": {"qkv": [P, 3 * D], "out": [P, D], "b_qk": [P, 2], "b_v": [D], "b_out": [D], "decay": [1]},
    "m": {"norm": [P, 1], "gates": [P, GATES], "w1": [P, EXPERTS * F], "w2": [P, FT, D]},
    "f": {"qkv": [P, 3 * FW + FH], "out": [P, FW // P, D], "ln_g": [D], "ln_b": [D]},
    "l": {"lora": [P, D + LE + LR], "lora_b": [LE * LR, D], "router_b": [LE], "base_b": [D]},
}


def weights(tag, k, dram, names):
    loaded = k.sem(f"{tag}_loaded")
    tiles = {n: k.sb(f"{tag}_{n}", shape if len(shape) > 1 else [P] + shape) for n, shape in names.items()}
    tiles = {n: (t[:, :, :] if len(names[n]) == 3 else t[:, :]) for n, t in tiles.items()}

    def fetch(sp):
        for n, shape in names.items():
            src = dram[f"{tag[0]}_{n}"]
            if len(shape) == 1:
                src = src.partition_broadcast(P)
            sp.dma_start(tiles[n], src).then_inc(loaded, 16)
        sp.wait_ge(loaded, 16 * len(names))
    return tiles, fetch


def build(nc, t, out, stages=8, first=0):
    with ExitStack() as stack:
        k = Kit(nc, stack)
        X = k.sb("X", [P, TILES, D])
        ident = k.sb("ident", [P, P])
        parts_dram = nc.dram_tensor("qk_parts", [2, 3, D, TOK], BF16, kind="Internal").ap()
        shift_dram = nc.dram_tensor("shift", [HEADS, TOK], BF16, kind="Internal").ap()
        read = k.sem("x_read")
        ident_set = k.sem("ident_set")
        head_of = k.sb("head_of", [P, HEADS])
        head_of_set = k.sem("head_of_set")
        x_dram = t["x"].rearrange("b (t p) d -> p (b t) d", p=P)
        with nc.Block() as block:
            @block.sync
            def _(sp):
                sp.dma_start(X[:, :, :], x_dram).then_inc(read, 16)
                sp.wait_ge(read, 16)

            @block.gpsimd
            def _(pool):
                pool.memset(ident[:, :], 0.0).then_inc(ident_set, 1)
                pool.wait_ge(ident_set, 1)
                pool.affine_select(out=ident[:, :], in_=ident[:, :], compare_op=ALU.not_equal, fill=1.0,
                                   base=0, pattern=[[-1, P]], channel_multiplier=1).then_inc(ident_set, 1)
                pool.memset(head_of[:, :], 1.0).then_inc(head_of_set, 1)
                pool.wait_ge(head_of_set, 1)
                pool.affine_select(out=head_of[:, :], in_=head_of[:, :], compare_op=ALU.is_ge, fill=0.0,
                                   base=0, pattern=[[-HD, HEADS]], channel_multiplier=1).then_inc(head_of_set, 1)
                pool.wait_ge(head_of_set, 2)
                pool.affine_select(out=head_of[:, :], in_=head_of[:, :], compare_op=ALU.is_ge, fill=0.0,
                                   base=HD - 1, pattern=[[HD, HEADS]], channel_multiplier=-1).then_inc(head_of_set, 1)
        idn = ident[:, :]
        def layer(tag, body):
            with ExitStack() as own:
                body(*weights(tag, Kit(nc, own), t, WEIGHTS[tag[0]]) if tag[0] in WEIGHTS else ())

        parts, head = parts_dram, head_of[:, :]
        todo = [("a", lambda w, fetch: alibi_attention(nc, "a", X, w, idn, parts, head, fetch)),
                ("m0", lambda w, fetch: moe_ffn(nc, "m0", X, w, idn, fetch)),
                ("b", lambda w, fetch: decay_attention(nc, "b", X, w, idn, parts, head, fetch)),
                ("m1", lambda w, fetch: moe_ffn(nc, "m1", X, w, idn, fetch)),
                ("f", lambda w, fetch: fast_weights(nc, "f", X, w, idn, fetch)),
                ("l0", lambda w, fetch: lora_ffn(nc, "l0", X, w, idn, fetch)),
                ("c", lambda: centred_attention(nc, "c", X, idn, parts, shift_dram, head)),
                ("l1", lambda w, fetch: lora_ffn(nc, "l1", X, w, idn, fetch))]
        for tag, body in todo[first:stages]:
            with nc.cleanup_on_exit():
                layer(tag, body)

        written = k.sem("written")
        with nc.Block() as block:
            @block.sync
            def _(sp):
                sp.dma_start(out.rearrange("b (t p) d -> p (b t) d", p=P), X[:, :, :]).then_inc(written, 16)
                sp.wait_ge(written, 16)


def layout(i):
    import numpy as np
    c = np.ascontiguousarray
    x = i["L0_attn_a_x"]
    out = {"x": x}
    for tag, name, wqkv, bqkv, wout, bout in (
            ("a", "L0_attn_a", "Wqkv", "bqkv", "Wout", "bout"),
            ("b", "L0_attn_b", "Wqkv_w", "Wqkv_b", "out_w", "out_b")):
        turn = (lambda m: m) if tag == "a" else (lambda m: c(m.T))
        b = np.asarray(i[f"{name}_{bqkv}"])
        out |= {f"{tag}_qkv": turn(np.asarray(i[f"{name}_{wqkv}"])), f"{tag}_out": turn(np.asarray(i[f"{name}_{wout}"])),
                f"{tag}_b_qk": c(b.reshape(3, D)[:2].T), f"{tag}_b_v": c(b[2 * D:]), f"{tag}_b_out": i[f"{name}_{bout}"]}
    out["b_decay"] = i["L0_attn_b_distance_decay"]
    w_macro, w_micro = np.asarray(i["L0_ffn_w_macro"]), np.asarray(i["L0_ffn_w_micro"]).reshape(EXPERTS, D)
    out["m_norm"] = np.asarray(i["L0_ffn_norm_w"]).reshape(D, 1)
    out["m_gates"] = c(np.concatenate([w_macro, w_micro]).T)
    out["m_w1"] = c(np.asarray(i["L0_ffn_w1"]).reshape(EXPERTS * F, D).T)
    out["m_w2"] = c(np.asarray(i["L0_ffn_w2"]).reshape(EXPERTS, D, HALVES, P).transpose(3, 0, 2, 1).reshape(P, FT, D))
    heads = np.asarray(i["L1_attn_a_W_qkvb"]).reshape(FH, 3 * FD + 1, D)
    rows = [heads[:, n * FD:(n + 1) * FD].reshape(FW, D) for n in range(3)] + [heads[:, 3 * FD]]
    out["f_qkv"] = c(np.concatenate(rows).T)
    out["f_out"] = c(np.asarray(i["L1_attn_a_W_o"]).reshape(D, FW // P, P).transpose(2, 1, 0))
    out["f_ln_g"], out["f_ln_b"] = i["L1_attn_a_ln_g"], i["L1_attn_a_ln_b"]
    out["l_lora"] = c(np.concatenate([np.asarray(i["L1_ffn_base_w"]).T, np.asarray(i["L1_ffn_router_w"]).T,
                                      np.asarray(i["L1_ffn_lora_A"])], axis=1))
    out["l_lora_b"] = np.asarray(i["L1_ffn_lora_B"]).reshape(LE * LR, D)
    out["l_router_b"], out["l_base_b"] = i["L1_ffn_router_b"], i["L1_ffn_base_b"]
    return {n: c(np.asarray(a)) for n, a in out.items()}


def kernel(**inputs):
    import numpy as np
    import concourse.bacc as bacc
    from concourse.bass_utils import run_bass_kernel_spmd

    nc = bacc.Bacc("TRN2", target_bir_lowering=False, num_devices=1)
    arrays = layout(inputs)
    dram = {n: nc.dram_tensor(f"in_{n}", a.shape, mybir.dt.from_np(a.dtype), kind="ExternalInput").ap()
            for n, a in arrays.items()}
    out = nc.dram_tensor("out", (BATCH, SEQ, D), F32, kind="ExternalOutput").ap()
    build(nc, dram, out)
    r = run_bass_kernel_spmd(nc, [{f"in_{n}": a for n, a in arrays.items()}], core_ids=[0])
    return r.results[0]["out"]
```

```python
import math
from contextlib import ExitStack

import concourse.bass as bass
from concourse import mybir

ALU = mybir.AluOpType
ACT = mybir.ActivationFunctionType
F32 = mybir.dt.float32
BF16 = mybir.dt.bfloat16
I32 = mybir.dt.int32
AX = mybir.AxisListType.X

P = 128
D = 128
BATCH, SEQ = 4, 1024
TOK = BATCH * SEQ
TILES = TOK // P
TPB = SEQ // P
HEADS, HD = 16, 8
LN_EPS = 1e-5
CHUNK = 512
BANK = 512


class Kit:

    def __init__(self, nc, stack, shared=None):
        self.nc, self.stack = nc, stack
        self.shared = shared

    def sb(self, name, shape, dt=F32):
        return self.stack.enter_context(self.nc.sbuf_tensor(name, shape, dt))

    def ps(self, name, shape):
        return self.stack.enter_context(self.nc.psum_tensor(name, shape, F32))

    def sem(self, name):
        return self.nc.alloc_semaphore(name)


def counter(engine, sem, base=0):
    count = [0]

    def link(ins):
        count[0] += 1
        ins.then_inc(sem, 1)
        engine.wait_ge(sem, base + count[0])
    link.count = count
    return link


def over(ap, n):
    return ap.unsqueeze(len(ap.shape)).to_broadcast(list(ap.shape) + [n])


def over_mid(ap, n):
    return ap.unsqueeze(1).to_broadcast([ap.shape[0], n, ap.shape[1]])


def layer_norm(nc, tag, X, XN, XT, ident, gain=None, shift=None, residual=None,
               beside=None):
    beside = beside or {}
    GROUP = 8
    STEPS = TILES // GROUP
    with ExitStack() as stack:
        k = Kit(nc, stack)
        square = k.sb(f"{tag}_square", [P, GROUP, D])
        neg_mean = k.sb(f"{tag}_neg_mean", [P, TILES])
        var = k.sb(f"{tag}_var", [P, TILES])
        std = k.sb(f"{tag}_std", [P, TILES])
        rstd = k.sb(f"{tag}_rstd", [P, TILES])
        eps = k.sb(f"{tag}_eps", [P, 1])
        turned_ps = k.ps(f"{tag}_turned_ps", [P, 2, GROUP, P])
        step_done = k.sem(f"{tag}_step_done")
        mean_ready = k.sem(f"{tag}_mean_ready")
        squared = k.sem(f"{tag}_squared")
        std_ready = k.sem(f"{tag}_std_ready")
        normed = k.sem(f"{tag}_normed")
        turned = k.sem(f"{tag}_turned")
        copied = k.sem(f"{tag}_copied")
        block = stack.enter_context(nc.Block())
        cut = [slice(GROUP * s, GROUP * (s + 1)) for s in range(STEPS)]

        @block.vector
        def _(dve):
            link = counter(dve, step_done)
            link(dve.memset(eps[:], LN_EPS))

            def normalise_step(s):
                dve.wait_ge(std_ready, s + 1)
                link(dve.reciprocal(rstd[:, cut[s]], std[:, cut[s]]))
                for t in range(GROUP * s, GROUP * (s + 1)):
                    scaled = dve.tensor_scalar(XN[:, t, :], X[:, t, :], neg_mean[:, t:t + 1], rstd[:, t:t + 1],
                                               ALU.add, ALU.mult)
                if gain is not None:
                    c = cut[s]
                    link(scaled)
                    link(dve.tensor_tensor(XN[:, c, :], XN[:, c, :], over_mid(gain, GROUP), ALU.mult))
                    scaled = dve.tensor_tensor(XN[:, c, :], XN[:, c, :], over_mid(shift, GROUP), ALU.add)
                scaled.then_inc(normed, 1)

            for s, c in enumerate(cut):
                link(dve.tensor_reduce(neg_mean[:, c], X[:, c, :], AX, ALU.add))
                dve.tensor_scalar(neg_mean[:, c], neg_mean[:, c], -1.0 / D, None, ALU.mult).then_inc(mean_ready, 1)
                if s >= 2:
                    normalise_step(s - 2)
            for s in range(STEPS - 2, STEPS):
                normalise_step(s)

        @block.scalar
        def _(act):
            for s, c in enumerate(cut):
                act.wait_ge(mean_ready, s + 1)
                for t in range(GROUP):
                    n = GROUP * s + t
                    last = act.activation(square[:, t, :], X[:, n, :], ACT.Square, bias=neg_mean[:, n:n + 1],
                                          accum_out=var[:, n:n + 1])
                last.then_inc(squared, 1)
                act.wait_ge(squared, s + 1)
                act.activation(std[:, c], var[:, c], ACT.Sqrt, bias=eps[:, 0:1],
                               scale=1.0 / D).then_inc(std_ready, 1)
            if XT is not None:
                for s in range(STEPS):
                    act.wait_ge(turned, s + 1)
                    act.copy(XT[:, GROUP * P * s:GROUP * P * (s + 1)],
                             turned_ps[:, s % 2, :, :].rearrange("p t q -> p (t q)")).then_inc(copied, 1)
            if "scalar" in beside:
                beside["scalar"](act)

        if "sync" in beside:
            @block.sync
            def _(sp):
                beside["sync"](sp)

        if "gpsimd" in beside or residual is not None:
            @block.gpsimd
            def _(pool):
                if "gpsimd" in beside:
                    beside["gpsimd"](pool)
                if residual is not None:
                    for s, c in enumerate(cut):
                        pool.wait_ge(normed, s + 1)
                        pool.tensor_tensor(residual[:, c, :], residual[:, c, :], XN[:, c, :], ALU.add)

        if XT is not None:
            @block.tensor
            def _(pe):
                for s in range(STEPS):
                    pe.wait_ge(normed, s + 1)
                    if s >= 2:
                        pe.wait_ge(copied, s - 1)
                    for t in range(GROUP):
                        last = pe.transpose(turned_ps[:, s % 2, t, :], XN[:, GROUP * s + t, :], ident)
                    last.then_inc(turned, 1)


Q_PARTS = (0, 0, 1, 1, 0, 2)
K_PARTS = (0, 1, 0, 1, 2, 0)
ROWS = HD * len(Q_PARTS)
GH = 4
VW = 32
WIN = 2 * SEQ - P


def project_qkv(nc, tag, XT, w_qkv, b_qk, b_v, V, parts_dram, scale, head_of, longest2):
    CH = TOK // CHUNK
    UNITS = 2 * CH
    RING = 4
    BURSTS = UNITS // 4
    with ExitStack() as stack:
        kk = Kit(nc, stack)
        full = kk.sb(f"{tag}_full", [P, RING, CHUNK])
        rest = kk.sb(f"{tag}_rest", [P, RING, CHUNK])
        parts = kk.sb(f"{tag}_parts", [P, RING, 3, CHUNK], BF16)
        squares = kk.sb(f"{tag}_squares", [P, 2 * RING, CHUNK])
        qk_ps = kk.ps(f"{tag}_qk_ps", [P, RING, BANK])
        norm2_ps = kk.ps(f"{tag}_norm2_ps", [P, 2, BANK])
        v_ps = kk.ps(f"{tag}_v_ps", [P, 2, 4, D])
        projected = kk.sem(f"{tag}_projected")
        biased = kk.sem(f"{tag}_biased")
        squared = kk.sem(f"{tag}_squared")
        norm2_done = kk.sem(f"{tag}_norm2_done")
        longest_done = kk.sem(f"{tag}_longest_done")
        part1 = kk.sem(f"{tag}_part1")
        rest1 = kk.sem(f"{tag}_rest1")
        part2 = kk.sem(f"{tag}_part2")
        part3 = kk.sem(f"{tag}_part3")
        stored = [kk.sem(f"{tag}_stored{b}") for b in range(RING)]
        v_done = kk.sem(f"{tag}_v_done")
        v_out = kk.sem(f"{tag}_v_out")
        block = stack.enter_context(nc.Block())

        @block.tensor
        def _(pe):
            def norms(m):
                pe.wait_ge(squared, 4 * m + 4)
                if m >= 2:
                    pe.wait_ge(longest_done, m - 1)
                for j in range(4):
                    last = pe.matmul(norm2_ps[VW * j:VW * (j + 1), m % 2, :], head_of,
                                     squares[:, (4 * m + j) % (2 * RING), :], start=True, stop=True)
                last.then_inc(norm2_done, 1)

            def values(s):
                if s >= 2:
                    pe.wait_ge(v_out, s - 1)
                for t in range(4):
                    last = pe.matmul(v_ps[:, s % 2, t, :], XT[:, (4 * s + t) * P:(4 * s + t + 1) * P],
                                     w_qkv[:, 2 * D:3 * D], start=True, stop=True)
                last.then_inc(v_done, 1)

            for u in range(UNITS):
                c, w = divmod(u, 2)
                if u >= RING:
                    pe.wait_ge(biased, u - RING + 1)
                pe.matmul(qk_ps[:, u % RING, :], w_qkv[:, w * D:(w + 1) * D],
                          XT[:, c * CHUNK:(c + 1) * CHUNK], start=True, stop=True).then_inc(projected, 1)
                if u % 4 == 1 and u > 4:
                    norms(u // 4 - 1)
                if w == 1:
                    values(c)
            norms(BURSTS - 1)

        @block.vector
        def _(dve):
            def take(u):
                w, b = u % 2, u % RING
                dve.wait_ge(projected, u + 1)
                if u >= RING:
                    dve.wait_ge(squared, u - RING + 1)
                dve.tensor_scalar(full[:, b, :], qk_ps[:, b, :], b_qk[:, w:w + 1],
                                  scale if w == 0 else 1.0, ALU.add, ALU.mult).then_inc(biased, 1)

            def rest_of(u):
                b = u % RING
                dve.wait_ge(part1, u + 1)
                dve.wait_ge(biased, u + 1)
                if u >= RING:
                    dve.wait_ge(part3, u - RING + 1)
                dve.tensor_tensor(rest[:, b, :], full[:, b, :], parts[:, b, 0, :],
                                  ALU.subtract).then_inc(rest1, 1)

            def longest(m):
                dve.wait_ge(norm2_done, m + 1)
                dve.tensor_reduce(longest2[:, m:m + 1], norm2_ps[:, m % 2, :], AX, ALU.max).then_inc(longest_done, 1)

            def bias_values(s):
                dve.wait_ge(v_done, s + 1)
                dve.tensor_tensor(V[:, 4 * s:4 * s + 4, :], v_ps[:, s % 2, :, :], over_mid(b_v, 4),
                                  ALU.add).then_inc(v_out, 1)

            for u in range(UNITS + 1):
                if u < UNITS:
                    take(u)
                if u >= 1:
                    rest_of(u - 1)
                if u % 4 == 3 and u > 4:
                    longest(u // 4 - 1)
                if u % 2 == 1 and u > 2:
                    bias_values(u // 2 - 1)
            bias_values(TILES // 4 - 1)
            longest(BURSTS - 1)

        @block.scalar
        def _(act):
            for u in range(UNITS + 1):
                b = u % RING
                if u < UNITS:
                    act.wait_ge(biased, u + 1)
                    if u >= RING:
                        act.wait_ge(stored[b], 16 * (u // RING))
                    act.copy(parts[:, b, 0, :], full[:, b, :]).then_inc(part1, 1)
                    if u >= 2 * RING:
                        act.wait_ge(norm2_done, u // 4 - 1)
                    act.activation(squares[:, u % (2 * RING), :], full[:, b, :], ACT.Square).then_inc(squared, 1)
                if u >= 1:
                    act.wait_ge(rest1, u)
                    act.copy(parts[:, (u - 1) % RING, 1, :], rest[:, (u - 1) % RING, :]).then_inc(part2, 1)

        @block.gpsimd
        def _(pool):
            for u in range(UNITS):
                b = u % RING
                pool.wait_ge(part2, u + 1)
                pool.tensor_tensor(parts[:, b, 2, :], rest[:, b, :], parts[:, b, 1, :],
                                   ALU.subtract).then_inc(part3, 1)

        @block.sync
        def _(sp):
            for u in range(UNITS):
                c, w = divmod(u, 2)
                sp.wait_ge(part3, u + 1)
                sp.dma_start(parts_dram[w].rearrange("s f t -> f s t")[:, :, c * CHUNK:(c + 1) * CHUNK],
                             parts[:, u % RING, :, :]).then_inc(stored[u % RING], 16)
            for b in range(RING):
                sp.wait_ge(stored[b], 16 * (UNITS // RING))


class Operands:
    SHIFT_ROW = 64

    def __init__(self, tag, k):
        self.q_rows = k.sb(f"{tag}_q_rows", [P, 2, GH, SEQ], BF16)
        self.k_rows = k.sb(f"{tag}_k_rows", [P, 2, GH, SEQ], BF16)
        self.v_cols = k.sb(f"{tag}_v_cols", [P, 2, TPB, GH, VW])
        self.cleared = k.sem(f"{tag}_cleared")

    def clear(self, pool):
        pool.memset(self.q_rows[:].bitcast(F32), 0.0).then_inc(self.cleared, 1)
        pool.memset(self.k_rows[:].bitcast(F32), 0.0).then_inc(self.cleared, 1)
        pool.memset(self.v_cols[:], 0.0).then_inc(self.cleared, 1)
        pool.wait_ge(self.cleared, 3)
        pool.memset(self.k_rows[self.SHIFT_ROW:self.SHIFT_ROW + 1, :, :, :], 1.0).then_inc(self.cleared, 1)
        pool.wait_ge(self.cleared, 4)
        pool.memset(self.v_cols[:, :, :, :, HD:HD + 1], 1.0)


SAFE_SCORE = 60.0
SAFE_FACTOR_SCORE = 30.0


def bound_scores(nc, tag, longest2, safe, wide, ident):
    with ExitStack() as stack:
        k = Kit(nc, stack)
        longest = k.sb(f"{tag}_longest", [P, 1])
        of_head = k.sb(f"{tag}_of_head", [1, 2, VW])
        bound = k.sb(f"{tag}_bound", [1, VW])
        top = k.sb(f"{tag}_top", [1, 1])
        row_ps = k.ps(f"{tag}_row_ps", [1, P])
        step_done = k.sem(f"{tag}_step_done")
        row_done = k.sem(f"{tag}_row_done")
        with nc.Block() as block:
            @block.vector
            def _(dve):
                link = counter(dve, step_done)
                link(dve.tensor_reduce(longest[:, :], longest2[:, :], AX, ALU.max))
                dve.wait_ge(row_done, 1)
                groups = row_ps[:, :].rearrange("o (a w h) -> o w h a", a=2, w=2)
                link(dve.tensor_reduce(of_head[:, :, :], groups, AX, ALU.max))
                link(dve.tensor_tensor(bound[:, :], of_head[:, 0, :], of_head[:, 1, :], ALU.mult))
                link(dve.tensor_reduce(top[:, :], bound[:, :], AX, ALU.max))
                dve.tensor_scalar(wide[:, :], top[:, :], safe ** 2, None, ALU.is_gt)

            @block.tensor
            def _(pe):
                pe.wait_ge(step_done, 1)
                pe.matmul(row_ps[:, :], longest[:, :], ident, start=True, stop=True).then_inc(row_done, 1)


def attend(nc, tag, V, operands, parts_dram, tables, op, out_all, ident):
    QT = TPB
    UNITS = QT * GH
    RING = 6
    LAG = 3
    AHEAD = 4
    with ExitStack() as stack:
        k = Kit(nc, stack)
        q_rows, k_rows, v_cols = operands.q_rows, operands.k_rows, operands.v_cols
        table = tables["buffer"]
        probs = k.sb(f"{tag}_probs", [P, RING, SEQ])
        row_max = k.sb(f"{tag}_row_max", [P, UNITS])
        tick = k.sb(f"{tag}_tick", [P, UNITS + 1])
        zero = k.sb(f"{tag}_zero", [P, 1])
        neg_max = k.sb(f"{tag}_neg_max", [P, UNITS])
        probs_t = k.sb(f"{tag}_probs_t", [P, 2, GH, TPB, P])
        out_t = k.sb(f"{tag}_out_t", [P, P])
        inv_sum = k.sb(f"{tag}_inv_sum", [P, QT, GH])
        s_ps = k.ps(f"{tag}_s_ps", [P, 2, SEQ])
        t_ps = k.ps(f"{tag}_t_ps", [P, 2, 4, P])
        o_ps = k.ps(f"{tag}_o_ps", [P, BANK])
        ot_ps = k.ps(f"{tag}_ot_ps", [P, BANK])
        loaded = [k.sem(f"{tag}_loaded{half}") for half in range(2)]
        group_done = k.sem(f"{tag}_group_done")
        zero_set = k.sem(f"{tag}_zero_set")
        table_set = k.sem(f"{tag}_table_set")
        v_set = k.sem(f"{tag}_v_set")
        scored = k.sem(f"{tag}_scored")
        maxed = k.sem(f"{tag}_maxed")
        negated = k.sem(f"{tag}_negated")
        exped = k.sem(f"{tag}_exped")
        turned = k.sem(f"{tag}_turned")
        left_out = k.sem(f"{tag}_left_out")
        right_out = k.sem(f"{tag}_right_out")
        summed = k.sem(f"{tag}_summed")
        o_out = k.sem(f"{tag}_o_out")
        o_turned = k.sem(f"{tag}_o_turned")
        inverted = k.sem(f"{tag}_inverted")
        normed = k.sem(f"{tag}_normed")
        block = stack.enter_context(nc.Block())
        LOADS = 2 * len(Q_PARTS)

        @block.sync
        def _(sp):
            with sp.Fori(0, HEADS // GH) as hg:
                with sp.Fori(0, BATCH // 2) as bp:
                    for half in range(2):
                        sp.wait_ge(group_done, hg * 4 + bp * 2 + (half + 1))
                        for rows, which, order in ((q_rows, 0, Q_PARTS), (k_rows, 1, K_PARTS)):
                            for n, part in enumerate(order):
                                src = parts_dram[which, part].rearrange("(h e) t -> e h t", e=HD)
                                sp.dma_start(
                                    rows[n * HD:(n + 1) * HD, half, :, :],
                                    src[:, bass.ds(hg * GH, GH), bass.ds(bp * (2 * SEQ) + half * SEQ, SEQ)],
                                ).then_inc(loaded[half], 16)

        @block.gpsimd
        def _(pool):
            pool.memset(zero[:, :], 0.0).then_inc(zero_set, 1)
            pool.wait_ge(zero_set, 1)
            with pool.Fori(0, HEADS // GH) as hg:
                if tables.get("per_group"):
                    for j in range(GH):
                        if j == 0:
                            pool.wait_ge(tables["free"], hg + 1)
                        pool.wait_ge(zero_set, 1)
                        pool.tensor_tensor(table[:, j, :], tables["distance"][:, :],
                                           tables["slopes"][:, bass.ds(hg * GH + j, 1)].to_broadcast([P, WIN]),
                                           ALU.mult).then_inc(table_set, 1)
                with pool.Fori(0, BATCH // 2) as bp:
                    for half in range(2):
                        g = hg * 4 + bp * 2
                        pool.wait_ge(group_done, g + (half + 1))
                        src = V[:, bass.ds(bp * (2 * TPB) + half * TPB, TPB), bass.ds(hg * (GH * HD), GH * HD)]
                        pool.tensor_copy(v_cols[:, half, :, :, 0:HD],
                                         src.rearrange("p t (h e) -> p t h e", e=HD)).then_inc(v_set, 1)
                        for n in range(UNITS):
                            pool.wait_ge(maxed, (g + half) * UNITS + (n + 1))
                            pool.tensor_tensor(neg_max[:, n:n + 1], zero[:, :], row_max[:, n:n + 1],
                                               ALU.subtract).then_inc(negated, 1)

        @block.tensor
        def _(pe):
            pe.sem_inc(group_done, 2)
            with pe.Fori(0, HEADS // GH) as hg:
                with pe.Fori(0, BATCH // 2) as bp:
                    for half in range(2):
                        g = hg * 4 + (bp * 2 + half)

                        def scores(n):
                            qt, j = divmod(n, GH)
                            if n >= 2:
                                pe.wait_ge(maxed, g * UNITS + (n - 1))
                            for c in range(2):
                                last = pe.matmul(s_ps[:, n % 2, c * BANK:(c + 1) * BANK],
                                                 q_rows[:, half, j, qt * P:(qt + 1) * P],
                                                 k_rows[:, half, j, c * BANK:(c + 1) * BANK],
                                                 start=True, stop=True)
                            last.then_inc(scored, 1)

                        def turn(n):
                            pe.wait_ge(exped, g * UNITS + (n + 1))
                            for side in range(2):
                                if n >= 1:
                                    pe.wait_ge((left_out, right_out)[side], g * UNITS + n)
                                for t in range(4):
                                    kt = 4 * side + t
                                    last = pe.transpose(t_ps[:, side, t, :],
                                                        probs[:, n % RING, kt * P:(kt + 1) * P], ident)
                                last.then_inc(turned, 1)

                        def sum_up(qt):
                            pe.wait_ge(left_out, g * UNITS + GH * (qt + 1))
                            pe.wait_ge(right_out, g * UNITS + GH * (qt + 1))
                            if qt >= 1:
                                pe.wait_ge(o_out, g * QT + qt)
                            for kt in range(TPB):
                                for j in range(GH):
                                    last = pe.matmul(o_ps[VW * j:VW * (j + 1), 0:P], v_cols[:, half, kt, j, :],
                                                     probs_t[:, qt % 2, j, kt, :], start=(kt == 0),
                                                     stop=(kt == TPB - 1))
                            last.then_inc(summed, 1)

                        def turn_sum(qt):
                            pe.wait_ge(o_out, g * QT + (qt + 1))
                            if qt >= 1:
                                pe.wait_ge(normed, g * QT + qt)
                            pe.transpose(ot_ps[:, 0:P], out_t[:, :], ident).then_inc(o_turned, 1)

                        pe.wait_ge(loaded[half], (hg * 2 + bp + 1) * (16 * LOADS))
                        pe.wait_ge(v_set, g + 1)
                        for n in range(AHEAD):
                            scores(n)
                        for n in range(UNITS):
                            if n + AHEAD < UNITS:
                                scores(n + AHEAD)
                            turn(n)
                            if n % GH == 1 and n > GH:
                                sum_up(n // GH - 1)
                            if n % GH == 2 and n > GH:
                                turn_sum(n // GH - 1)
                        sum_up(QT - 1)
                        pe.wait_ge(o_out, g * QT + QT)
                        pe.wait_ge(normed, g * QT + (QT - 1))
                        pe.transpose(ot_ps[:, 0:P], out_t[:, :], ident).then_inc(o_turned, 1)
                        pe.wait_ge(o_turned, g * QT + QT)
                        pe.sem_inc(group_done, 1)

        @block.vector
        def _(dve):
            if tables.get("per_group"):
                dve.sem_inc(tables["free"], 1)
            with dve.Fori(0, HEADS // GH) as hg:
                if tables.get("per_group"):
                    dve.wait_ge(table_set, (hg + 1) * GH)
                    dve.memset(tick[:, UNITS:UNITS + 1], 0.0)
                with dve.Fori(0, BATCH // 2) as bp:
                    for half in range(2):
                        g = hg * 4 + (bp * 2 + half)

                        def left(n):
                            dve.wait_ge(turned, g * (2 * UNITS) + (2 * n + 1))
                            if n // GH >= 2:
                                dve.wait_ge(summed, g * QT + (n // GH - 1))
                            dve.tensor_copy(probs_t[:, (n // GH) % 2, n % GH, 0:4, :],
                                            t_ps[:, 0, :, :]).then_inc(left_out, 1)

                        def norm(qt):
                            dve.wait_ge(o_turned, g * QT + (qt + 1))
                            heads = ot_ps[:, 0:P].rearrange("p (h e) -> p h e", e=VW)
                            dve.reciprocal(inv_sum[:, qt, :], heads[:, :, HD]).then_inc(inverted, 1)
                            dve.wait_ge(inverted, g * QT + (qt + 1))
                            dst = out_all[:, bass.ds(bp * (2 * TPB) + (half * TPB + qt), 1),
                                          bass.ds(hg * (GH * HD), GH * HD)]
                            dve.tensor_tensor(dst.rearrange("p o (h e) -> p (o h) e", e=HD),
                                              heads[:, :, 0:HD], over(inv_sum[:, qt, :], HD),
                                              ALU.mult).then_inc(normed, 1)

                        for n in range(UNITS):
                            qt, j = divmod(n, GH)
                            dve.wait_ge(scored, g * UNITS + (n + 1))
                            if n >= RING:
                                dve.wait_ge(turned, g * (2 * UNITS) + 2 * (n - RING + 1))
                            dve.memset(tick[:, n:n + 1], 0.0)
                            at = SEQ - P - qt * P
                            t = table[:, j if tables.get("per_group") else 0, at:at + SEQ]
                            dve.tensor_tensor_reduce(out=probs[:, n % RING, :], in0=s_ps[:, n % 2, :], in1=t,
                                                     scale=1.0, scalar=-3e38, op0=op, op1=ALU.max,
                                                     accum_out=row_max[:, n:n + 1]).then_inc(maxed, 1)
                            if n >= LAG:
                                left(n - LAG)
                            if n % GH == GH - 1 and n >= 2 * GH:
                                norm(n // GH - 2)
                        for n in range(UNITS - LAG, UNITS):
                            left(n)
                        norm(QT - 2)
                        norm(QT - 1)
                if tables.get("per_group"):
                    dve.wait_ge(maxed, (hg + 1) * (BATCH * UNITS))
                    dve.sem_inc(tables["free"], 1)

        @block.scalar
        def _(act):
            with act.Fori(0, HEADS // GH) as hg:
                with act.Fori(0, BATCH // 2) as bp:
                    for half in range(2):
                        g = hg * 4 + (bp * 2 + half)

                        def right(n):
                            act.wait_ge(turned, g * (2 * UNITS) + (2 * n + 2))
                            if n // GH >= 2:
                                act.wait_ge(summed, g * QT + (n // GH - 1))
                            act.copy(probs_t[:, (n // GH) % 2, n % GH, 4:8, :],
                                     t_ps[:, 1, :, :]).then_inc(right_out, 1)

                        def take_sum(qt):
                            act.wait_ge(summed, g * QT + (qt + 1))
                            if qt >= 1:
                                act.wait_ge(o_turned, g * QT + qt)
                            act.copy(out_t[:, :], o_ps[:, 0:P]).then_inc(o_out, 1)

                        for n in range(UNITS):
                            act.wait_ge(negated, g * UNITS + (n + 1))
                            act.activation(probs[:, n % RING, :], probs[:, n % RING, :], ACT.Exp,
                                           bias=neg_max[:, n:n + 1]).then_inc(exped, 1)
                            if n >= 1:
                                right(n - 1)
                            if n % GH == 2 and n > GH:
                                take_sum(n // GH - 1)
                        right(UNITS - 1)
                        take_sum(QT - 1)


def attend_transposed(nc, tag, V, operands, parts_dram, out_t, shift_dram=None, table=None, slopes=None,
                      factor=None):
    by_dve = table is not None
    by_pool = slopes is not None
    OWN = GH - by_pool
    JT = TPB
    UNITS = JT * GH
    NG = (HEADS // GH) * BATCH
    SLOTS = 3
    with ExitStack() as stack:
        k = Kit(nc, stack)
        q_rows, k_rows, v_cols = operands.q_rows, operands.k_rows, operands.v_cols
        probs = k.sb(f"{tag}_probs", [P, 2, GH, SEQ])
        s_ps = k.ps(f"{tag}_s_ps", [P, SLOTS, SEQ])
        o_ps = k.ps(f"{tag}_o_ps", [P, 2, BANK])
        loaded = [k.sem(f"{tag}_loaded{half}") for half in range(2)]
        v_set = k.sem(f"{tag}_v_set")
        scored = k.sem(f"{tag}_scored")
        exped = k.sem(f"{tag}_exped")
        summed = k.sem(f"{tag}_summed")
        o_out = k.sem(f"{tag}_o_out")
        block = stack.enter_context(nc.Block())
        adjusted = k.sem(f"{tag}_adjusted") if by_dve else None
        first_exped = k.sem(f"{tag}_first_exped") if by_pool else None
        damped = k.sem(f"{tag}_damped") if by_pool else None
        factor_set = k.sem(f"{tag}_factor_set") if by_pool else None
        slot_read = adjusted if by_dve else exped

        def count_of(g, n):
            return g * (JT * OWN) + ((n // GH) * OWN + (n % GH + 1 - by_pool))
        LOADS = 2 * len(Q_PARTS) + (not by_dve)

        @block.sync
        def _(sp):
            with sp.Fori(0, HEADS // GH) as hg:
                with sp.Fori(0, BATCH // 2) as bp:
                    for half in range(2):
                        sp.wait_ge(o_out, hg * 8 + bp * 4 + (2 * half + 2))
                        at = bass.ds(bp * (2 * SEQ) + half * SEQ, SEQ)
                        for rows, which, order in ((q_rows, 0, Q_PARTS), (k_rows, int(by_dve), K_PARTS)):
                            for n, part in enumerate(order):
                                src = parts_dram[which, part].rearrange("(h e) t -> e h t", e=HD)
                                sp.dma_start(rows[n * HD:(n + 1) * HD, half, :, :],
                                             src[:, bass.ds(hg * GH, GH), at]).then_inc(loaded[half], 16)
                        if not by_dve:
                            sp.dma_start(q_rows[operands.SHIFT_ROW:operands.SHIFT_ROW + 1, half, :, :],
                                         shift_dram.unsqueeze(0)[:, bass.ds(hg * GH, GH), at]
                                         ).then_inc(loaded[half], 16)

        @block.gpsimd
        def _(pool):
            with pool.Fori(0, HEADS // GH) as hg:
                with pool.Fori(0, BATCH // 2) as bp:
                    for half in range(2):
                        pool.wait_ge(o_out, hg * 8 + bp * 4 + (2 * half + 2))
                        src = V[:, bass.ds(bp * (2 * TPB) + half * TPB, TPB), bass.ds(hg * (GH * HD), GH * HD)]
                        pool.tensor_copy(v_cols[:, half, :, :, 0:HD],
                                         src.rearrange("p t (h e) -> p t h e", e=HD)).then_inc(v_set, 1)
                        if by_pool:
                            for J in range(JT):
                                if J == 0:
                                    pool.wait_ge(factor_set, hg + 1)
                                pool.wait_ge(first_exped, (hg * 4 + (bp * 2 + half)) * JT + (J + 1))
                                first, at = probs[:, J % 2, 0, :], SEQ - P - J * P
                                pool.tensor_tensor(first, first, factor[:, at:at + SEQ], ALU.mult).then_inc(damped, 1)

        @block.tensor
        def _(pe):
            pe.sem_inc(summed, 2)

            def scores(half, n, i):
                g = i * 2 + half
                J, j = divmod(n, GH)
                if n == 0:
                    pe.wait_ge(loaded[half], i * (16 * LOADS) + 16 * LOADS)
                back = n - SLOTS if n >= SLOTS else max(m for m in range(-SLOTS, 0) if (m + UNITS) % SLOTS == n)
                if by_pool and back % GH == 0:
                    pe.wait_ge(first_exped, g * JT + (back // GH + 1))
                else:
                    pe.wait_ge(slot_read, count_of(g, back) + SLOTS)
                for c in range(2):
                    last = pe.matmul(s_ps[:, n % SLOTS, c * BANK:(c + 1) * BANK],
                                     k_rows[:, half, j, J * P:(J + 1) * P],
                                     q_rows[:, half, j, c * BANK:(c + 1) * BANK], start=True, stop=True)
                last.then_inc(scored, 1)

            def sum_up(half, J, c, i):
                g = i * 2 + half
                if c == 0:
                    if J == 0:
                        pe.wait_ge(o_out, g * 2 + 4)
                        pe.wait_ge(v_set, g + 1)
                    pe.wait_ge(exped, count_of(g, GH * J + GH - 1) + SLOTS)
                    if by_pool:
                        pe.wait_ge(damped, g * JT + (J + 1))
                for j in range(GH):
                    last = pe.matmul(o_ps[VW * j:VW * (j + 1), c, :], v_cols[:, half, J, j, :],
                                     probs[:, J % 2, j, c * BANK:(c + 1) * BANK], start=(J == 0),
                                     stop=(J == JT - 1))
                if c == 1:
                    last.then_inc(summed, 1)

            def pair(i, final):
                for half in range(2):
                    for n in range(UNITS):
                        m = n + SLOTS
                        if m < UNITS:
                            scores(half, m, i)
                        elif half == 0:
                            scores(1, m - UNITS, i)
                        elif not final:
                            scores(0, m - UNITS, i + 1)
                        if n % GH == GH - 1:
                            sum_up(half, n // GH, 0, i)
                            if n + 1 == UNITS:
                                sum_up(half, n // GH, 1, i)
                        if n % GH == 1 and n > GH:
                            sum_up(half, n // GH - 1, 1, i)

            for n in range(SLOTS):
                scores(0, n, 0)
            with pe.Fori(0, NG // 2 - 1) as i:
                pair(i, False)
            pair(NG // 2 - 1, True)

        @block.scalar
        def _(act):
            act.sem_inc(exped, SLOTS)

            def take_sums(g):
                act.wait_ge(summed, g * JT + (JT + 2))
                for c in range(2):
                    dst = out_t[:, bass.ds(g, 1), c * BANK:(c + 1) * BANK].rearrange("p o q -> p (o q)")
                    act.copy(dst, o_ps[:, c, :]).then_inc(o_out, 1)

            def group(g, first):
                for n in range(UNITS):
                    J, j = divmod(n, GH)
                    out = probs[:, J % 2, j, :]
                    if by_pool and j == 0:
                        act.wait_ge(scored, g * UNITS + (n + 1))
                        act.wait_ge(summed, g * JT + (J + 1))
                        act.activation(out, s_ps[:, n % SLOTS, :], ACT.Exp).then_inc(first_exped, 1)
                        continue
                    if by_dve:
                        act.wait_ge(adjusted, count_of(g, n) + SLOTS)
                        act.activation(out, out, ACT.Exp).then_inc(exped, 1)
                        if n == 1 and not first:
                            take_sums(g - 1)
                        continue
                    act.wait_ge(scored, g * UNITS + (n + 1))
                    if j == 0:
                        act.wait_ge(summed, g * JT + (J + 1))
                    act.activation(out, s_ps[:, n % SLOTS, :], ACT.Exp).then_inc(exped, 1)

            def make_factor(hg):
                act.activation(factor, table[:, :], ACT.Exp, scale=slopes[:, bass.ds(hg * GH, 1)]).then_inc(factor_set, 1)

            if by_pool:
                make_factor(0)
                group(0, True)
                with act.Fori(1, BATCH) as b:
                    group(b, False)
                with act.Fori(1, HEADS // GH) as hg:
                    act.wait_ge(damped, hg * (BATCH * JT))
                    make_factor(hg)
                    with act.Fori(0, BATCH) as b:
                        group(hg * BATCH + b, False)
                take_sums(NG - 1)
            elif by_dve:
                group(0, True)
                with act.Fori(1, NG) as g:
                    group(g, False)
                take_sums(NG - 1)
            else:
                with act.Fori(0, NG) as g:
                    group(g, False)

        @block.vector
        def _(dve):
            dve.sem_inc(o_out, 4)
            if not by_dve:
                with dve.Fori(0, NG) as g:
                    dve.wait_ge(summed, g * JT + (JT + 2))
                    for c in range(2):
                        dst = out_t[:, bass.ds(g, 1), c * BANK:(c + 1) * BANK].rearrange("p o q -> p (o q)")
                        dve.tensor_copy(dst, o_ps[:, c, :]).then_inc(o_out, 1)
                return
            dve.sem_inc(adjusted, SLOTS)
            with dve.Fori(0, HEADS // GH) as hg:
                with dve.Fori(0, BATCH) as b:
                    g = hg * BATCH + b
                    for n in range(UNITS):
                        J, j = divmod(n, GH)
                        if by_pool and j == 0:
                            continue
                        dve.wait_ge(scored, g * UNITS + (n + 1))
                        if j == by_pool:
                            dve.wait_ge(summed, g * JT + (J + 1))
                        near = table[:, SEQ - P - J * P:2 * SEQ - P - J * P]
                        out, scores_ = probs[:, J % 2, j, :], s_ps[:, n % SLOTS, :]
                        if slopes is None:
                            ins = dve.tensor_tensor(out, scores_, near, ALU.mult)
                        else:
                            ins = dve.scalar_tensor_tensor(out=out, in0=near, scalar=slopes[:, bass.ds(hg * GH + j, 1)],
                                                           in1=scores_, op0=ALU.mult, op1=ALU.add)
                        ins.then_inc(adjusted, 1)


def normalise(nc, tag, out_t, out_all, ident, residual=None):
    NH = HEADS // GH
    with ExitStack() as stack:
        k = Kit(nc, stack)
        inv = k.sb(f"{tag}_inv", [P, TILES, HEADS])
        t_ps = k.ps(f"{tag}_t_ps", [P, 4, NH, P])
        turned = k.sem(f"{tag}_turned")
        inverted = k.sem(f"{tag}_inverted")
        normed = k.sem(f"{tag}_normed")
        block = stack.enter_context(nc.Block())

        @block.tensor
        def _(pe):
            for t in range(TILES):
                b, qt = divmod(t, TPB)
                if t >= 4:
                    pe.wait_ge(normed, t - 3)
                for hg in range(NH):
                    last = pe.transpose(t_ps[:, t % 4, hg, :], out_t[:, hg * BATCH + b, qt * P:(qt + 1) * P], ident)
                last.then_inc(turned, 1)

        if residual is not None:
            @block.gpsimd
            def _(pool):
                for t in range(TILES):
                    pool.wait_ge(normed, t + 1)
                    pool.tensor_tensor(residual[:, t, :], residual[:, t, :], out_all[:, t, :], ALU.add)

        @block.vector
        def _(dve):
            for t in range(TILES):
                heads = t_ps[:, t % 4, :, :].rearrange("p g (h e) -> p (g h) e", e=VW)
                dve.wait_ge(turned, t + 1)
                dve.reciprocal(inv[:, t, :], heads[:, :, HD]).then_inc(inverted, 1)
                dve.wait_ge(inverted, t + 1)
                dve.tensor_tensor(out_all[:, t, :].rearrange("p (h e) -> p h e", e=HD), heads[:, :, 0:HD],
                                  over(inv[:, t, :], HD), ALU.mult).then_inc(normed, 1)


def project_out(nc, tag, out_all, w_out, b_out, X, ident):
    with ExitStack() as stack:
        k = Kit(nc, stack)
        out_t = k.sb(f"{tag}_out_t", [P, 2, 4, P])
        t_ps = k.ps(f"{tag}_t_ps", [P, 2, 4, P])
        y_ps = k.ps(f"{tag}_y_ps", [P, 2, 4, D])
        turned = k.sem(f"{tag}_turned")
        copied = k.sem(f"{tag}_copied")
        projected = k.sem(f"{tag}_projected")
        biased = k.sem(f"{tag}_biased")
        added = k.sem(f"{tag}_added")
        block = stack.enter_context(nc.Block())
        STEPS = TILES // 4

        @block.tensor
        def _(pe):
            def turn(s):
                if s >= 2:
                    pe.wait_ge(copied, s - 1)
                for t in range(4):
                    last = pe.transpose(t_ps[:, s % 2, t, :], out_all[:, 4 * s + t, :], ident)
                last.then_inc(turned, 1)
            turn(0)
            for s in range(STEPS):
                if s + 1 < STEPS:
                    turn(s + 1)
                pe.wait_ge(copied, s + 1)
                if s >= 2:
                    pe.wait_ge(added, s - 1)
                for t in range(4):
                    last = pe.matmul(y_ps[:, s % 2, t, :], out_t[:, s % 2, t, :], w_out, start=True, stop=True)
                last.then_inc(projected, 1)

        @block.scalar
        def _(act):
            for s in range(STEPS):
                act.wait_ge(turned, s + 1)
                if s >= 2:
                    act.wait_ge(projected, s - 1)
                act.copy(out_t[:, s % 2, :, :], t_ps[:, s % 2, :, :]).then_inc(copied, 1)

        @block.vector
        def _(dve):
            for s in range(STEPS):
                x = X[:, 4 * s:4 * s + 4, :]
                dve.tensor_tensor(x, x, over_mid(b_out, 4), ALU.add).then_inc(biased, 1)
                dve.wait_ge(projected, s + 1)
                dve.wait_ge(biased, s + 1)
                dve.tensor_tensor(x, x, y_ps[:, s % 2, :, :], ALU.add).then_inc(added, 1)


def alibi_slopes():
    start = 2.0 ** (-2.0 ** (-(math.log2(HEADS) - 3)))
    return [start ** i for i in range(HEADS)]


class Distances:

    def __init__(self, tag, k):
        self.distance = k.sb(f"{tag}_distance", [P, WIN])
        self.signed = self.distance[:, :].bitcast(I32)
        self.counted = k.sem(f"{tag}_counted")

    def count(self, pool):
        pool.iota(self.signed, pattern=[[1, WIN]], base=-(SEQ - P), channel_multiplier=-1).then_inc(self.counted, 1)

    def take(self, act):
        act.wait_ge(self.counted, 1)
        return act.activation(self.distance[:, :], self.signed, ACT.Abs)


def attention_layer(nc, tag, X, w, ident, parts_dram, head_of, fetch, attend_all, gpsimd, scalar, safe):
    with ExitStack() as stack:
        k = Kit(nc, stack)
        XN = k.sb(f"{tag}_XN", [P, TILES, D])
        V = k.sb(f"{tag}_V", [P, TILES, D])
        longest2 = k.sb(f"{tag}_longest2", [P, TOK // CHUNK // 2])
        wide = k.sb(f"{tag}_wide", [1, 1], I32)
        operands = Operands(tag, k)

        def clear_too(pool):
            gpsimd(pool)
            operands.clear(pool)
        with ExitStack() as inner:
            XT = Kit(nc, inner).sb(f"{tag}_XT", [P, TOK])
            layer_norm(nc, f"{tag}_ln", X, XN, XT, ident,
                       beside={"sync": fetch, "gpsimd": clear_too, "scalar": scalar})
            project_qkv(nc, f"{tag}_qkv", XT, w["qkv"], w["b_qk"], w["b_v"], V, parts_dram,
                        1.0 / math.sqrt(HD), head_of, longest2)
        bound_scores(nc, f"{tag}_bound", longest2, safe, wide, ident)
        attend_all(wide, V, operands, XN)
        project_out(nc, f"{tag}_out", XN, w["out"], w["b_out"], X, ident)


def choose(nc, wide, direct, general):
    is_wide = nc.values_load(wide[0:1, 0:1], min_val=0, max_val=1)
    with nc.If(is_wide == 1):
        general()
    with nc.Else():
        direct()


def alibi_attention(nc, tag, X, w, ident, parts_dram, head_of, fetch):
    with ExitStack() as stack:
        k = Kit(nc, stack)
        distances = Distances(tag, k)
        slopes = k.sb(f"{tag}_slopes", [P, HEADS])
        free = k.sem(f"{tag}_table_free")

        def gpsimd(pool):
            distances.count(pool)
            for h, s in enumerate(alibi_slopes()):
                pool.memset(slopes[:, h:h + 1], -s)

        def attend_all(wide, V, operands, out):
            def direct():
                with ExitStack() as inner:
                    out_t = Kit(nc, inner).sb(f"{tag}_out_t", [P, (HEADS // GH) * BATCH, SEQ])
                    factor = out[:, :, :].rearrange("p t d -> p (t d)")[:, 0:WIN]
                    attend_transposed(nc, f"{tag}_direct", V, operands, parts_dram, out_t,
                                      table=distances.distance, slopes=slopes, factor=factor)
                    normalise(nc, f"{tag}_norm", out_t, out, ident)

            def general():
                with ExitStack() as inner:
                    table = Kit(nc, inner).sb(f"{tag}_table", [P, GH, WIN])
                    attend(nc, f"{tag}_att", V, operands, parts_dram, {"buffer": table, "per_group": True,
                           "distance": distances.distance, "slopes": slopes, "free": free}, ALU.add, out, ident)
            choose(nc, wide, direct, general)
        attention_layer(nc, tag, X, w, ident, parts_dram, head_of, fetch, attend_all, gpsimd,
                        lambda act: distances.take(act), SAFE_FACTOR_SCORE)


def decay_attention(nc, tag, X, w, ident, parts_dram, head_of, fetch):
    with ExitStack() as stack:
        k = Kit(nc, stack)
        distances = Distances(tag, k)
        table = distances.distance[:, :].unsqueeze(1)
        rate = k.sb(f"{tag}_rate", [P, 1])
        table_step = k.sem(f"{tag}_table_step")
        decay_in = k.sem(f"{tag}_decay_in")

        def fetch_and_tell(sp):
            fetch(sp)
            sp.sem_inc(decay_in, 1)

        def make_table(act):
            distances.take(act).then_inc(table_step, 1)
            act.wait_ge(decay_in, 1)
            act.activation(rate[:, :], w["decay"], ACT.Abs).then_inc(table_step, 1)
            act.wait_ge(table_step, 2)
            act.mul(rate[:, :], rate[:, :], -1.0).then_inc(table_step, 1)
            act.wait_ge(table_step, 3)
            act.activation(table[:, 0, :], table[:, 0, :], ACT.Exp, scale=rate[:, 0:1])

        def attend_all(wide, V, operands, out):
            def direct():
                with ExitStack() as inner:
                    out_t = Kit(nc, inner).sb(f"{tag}_out_t", [P, (HEADS // GH) * BATCH, SEQ])
                    attend_transposed(nc, f"{tag}_direct", V, operands, parts_dram, out_t, table=table[:, 0, :])
                    normalise(nc, f"{tag}_norm", out_t, out, ident)

            def general():
                attend(nc, f"{tag}_att", V, operands, parts_dram, {"buffer": table}, ALU.mult, out, ident)
            choose(nc, wide, direct, general)
        attention_layer(nc, tag, X, w, ident, parts_dram, head_of, fetch_and_tell, attend_all,
                        distances.count, make_table, SAFE_SCORE)


def centred_attention(nc, tag, X, ident, parts_dram, shift_dram, head_of):
    with ExitStack() as stack:
        k = Kit(nc, stack)
        XN = k.sb(f"{tag}_XN", [P, TILES, D])
        operands = Operands(tag, k)
        with ExitStack() as inner:
            XT = Kit(nc, inner).sb(f"{tag}_XT", [P, TOK])
            layer_norm(nc, f"{tag}_ln", X, XN, XT, ident, beside={"gpsimd": operands.clear})
            centre_and_split(nc, f"{tag}_split", XT, parts_dram, shift_dram, head_of)
        out_t = k.sb(f"{tag}_out_t", [P, (HEADS // GH) * BATCH, SEQ])
        attend_transposed(nc, f"{tag}_att", XN, operands, parts_dram, out_t, shift_dram=shift_dram)
        normalise(nc, f"{tag}_norm", out_t, XN, ident, residual=X)


def centre_and_split(nc, tag, XT, parts_dram, shift_dram, head_of):
    with ExitStack() as stack:
        k = Kit(nc, stack)
        total = k.sb(f"{tag}_total", [P, BATCH])
        rest = k.sb(f"{tag}_rest", [P, TOK])
        parts = k.sb(f"{tag}_parts", [P, 3, TOK], BF16)
        squares = k.sb(f"{tag}_squares", [P, TOK])
        norm2 = k.sb(f"{tag}_norm2", [HEADS, TOK])
        norm = k.sb(f"{tag}_norm", [HEADS, TOK])
        longest = k.sb(f"{tag}_longest", [HEADS, BATCH])
        shift = k.sb(f"{tag}_shift", [HEADS, TOK], BF16)
        norm_ps = k.ps(f"{tag}_norm_ps", [HEADS, TOK])
        step_done = k.sem(f"{tag}_step_done")
        centred = k.sem(f"{tag}_centred")
        part1 = k.sem(f"{tag}_part1")
        rest1 = k.sem(f"{tag}_rest1")
        part2 = k.sem(f"{tag}_part2")
        part3 = k.sem(f"{tag}_part3")
        stored = k.sem(f"{tag}_stored")
        squared = k.sem(f"{tag}_squared")
        norm2_done = k.sem(f"{tag}_norm2_done")
        norm_done = k.sem(f"{tag}_norm_done")
        shift_done = k.sem(f"{tag}_shift_done")
        block = stack.enter_context(nc.Block())
        cut = [slice(b * SEQ, (b + 1) * SEQ) for b in range(BATCH)]

        @block.vector
        def _(dve):
            link = counter(dve, step_done)
            for b, c in enumerate(cut):
                link(dve.tensor_reduce(total[:, b:b + 1], XT[:, c], AX, ALU.add))
                link(dve.tensor_scalar(total[:, b:b + 1], total[:, b:b + 1], 1.0 / SEQ, None, ALU.mult))
                dve.tensor_scalar(XT[:, c], XT[:, c], total[:, b:b + 1], None, ALU.subtract).then_inc(centred, 1)
            for b, c in enumerate(cut):
                dve.wait_ge(centred, b + 1)
                dve.wait_ge(part1, b + 1)
                dve.tensor_tensor(rest[:, c], XT[:, c], parts[:, 0, c], ALU.subtract).then_inc(rest1, 1)
            for b, c in enumerate(cut):
                dve.wait_ge(rest1, b + 1)
                dve.wait_ge(part2, b + 1)
                dve.tensor_tensor(parts[:, 2, c], rest[:, c], parts[:, 1, c], ALU.subtract).then_inc(part3, 1)
            for b, c in enumerate(cut):
                dve.wait_ge(norm_done, 2 * (b + 1))
                link(dve.tensor_reduce(longest[:, b:b + 1], norm[:, c], AX, ALU.max))
                link(dve.scalar_tensor_tensor(out=norm[:, c], in0=norm[:, c], scalar=longest[:, b:b + 1],
                                              in1=norm2[:, c], op0=ALU.mult, op1=ALU.add))
                dve.tensor_scalar(shift[:, c], norm[:, c], -0.5, None, ALU.mult).then_inc(shift_done, 1)

        @block.tensor
        def _(pe):
            for n in range(TOK // BANK):
                pe.wait_ge(squared, n // (SEQ // BANK) + 1)
                pe.matmul(norm_ps[:, n * BANK:(n + 1) * BANK], head_of, squares[:, n * BANK:(n + 1) * BANK],
                          start=True, stop=True).then_inc(norm2_done, 1)

        @block.scalar
        def _(act):
            for b, c in enumerate(cut):
                act.wait_ge(centred, b + 1)
                act.copy(parts[:, 0, c], XT[:, c]).then_inc(part1, 1)
                act.activation(squares[:, c], XT[:, c], ACT.Square).then_inc(squared, 1)
            for b, c in enumerate(cut):
                act.wait_ge(rest1, b + 1)
                act.copy(parts[:, 1, c], rest[:, c]).then_inc(part2, 1)
            for b, c in enumerate(cut):
                act.wait_ge(norm2_done, (b + 1) * (SEQ // BANK))
                act.activation(norm[:, c], norm_ps[:, c], ACT.Sqrt).then_inc(norm_done, 1)
                act.copy(norm2[:, c], norm_ps[:, c]).then_inc(norm_done, 1)

        @block.sync
        def _(sp):
            for b, c in enumerate(cut):
                sp.wait_ge(part3, b + 1)
                sp.dma_start(parts_dram[0].rearrange("s f t -> f s t")[:, :, c], parts[:, :, c]).then_inc(stored, 16)
            for b, c in enumerate(cut):
                sp.wait_ge(shift_done, b + 1)
                sp.dma_start(shift_dram[:, c], shift[:, c]).then_inc(stored, 16)
            sp.wait_ge(stored, 16 * 2 * BATCH)


GROUPS, PER_GROUP = 4, 2
EXPERTS = GROUPS * PER_GROUP
F = 256
FT = EXPERTS * F // P
HALVES = F // P
GATES = GROUPS + EXPERTS
LOOPS = 2
RMS_EPS = 1e-6
GATE_EPS = 1e-9
CT = CHUNK // P
CHUNKS = TOK // CHUNK


def mixture(nc, tag, X, Z, w, ident, fetch):
    UP_BANKS = 2
    NC = LOOPS * CHUNKS
    with ExitStack() as stack:
        k = Kit(nc, stack)
        scratch = k.sb(f"{tag}_scratch", [P, CT, D])
        ms = k.sb(f"{tag}_ms", [P, CT])
        std = k.sb(f"{tag}_std", [P, CT])
        eps = k.sb(f"{tag}_eps", [P, 2])
        square = k.sb(f"{tag}_square", [P, CT, D])
        neg_mean = k.sb(f"{tag}_neg_mean", [P, CT])
        var = k.sb(f"{tag}_var", [P, CT])
        ln_std = k.sb(f"{tag}_ln_std", [P, CT])
        warm = k.sb(f"{tag}_warm", [P, 1])
        ZT = k.sb(f"{tag}_ZT", [P, 2, CHUNK])
        logits = k.sb(f"{tag}_logits", [P, CT, GATES])
        exps = k.sb(f"{tag}_exps", [P, CT, GATES])
        top = k.sb(f"{tag}_top", [P, CT, 1 + GROUPS])
        total = k.sb(f"{tag}_total", [P, CT, 1 + GROUPS])
        beats = k.sb(f"{tag}_beats", [P, CT, GROUPS, GROUPS])
        ties = k.sb(f"{tag}_ties", [P, CT, GROUPS, GROUPS])
        rank = k.sb(f"{tag}_rank", [P, CT, GROUPS])
        pair = k.sb(f"{tag}_pair", [P, CT])
        best = k.sb(f"{tag}_best", [P, CT, GROUPS])
        inv_best = k.sb(f"{tag}_inv_best", [P, CT, GROUPS])
        second = k.sb(f"{tag}_second", [P, CT, GROUPS])
        combine = k.sb(f"{tag}_combine", [P, 2, CT, EXPERTS])
        hidden = k.sb(f"{tag}_hidden", [P, FT, CHUNK])
        weighted = k.sb(f"{tag}_weighted", [P, EXPERTS, D])
        mixed = k.sb(f"{tag}_mixed", [P, D])
        turned_ps = k.ps(f"{tag}_turned_ps", [P, CT, P])
        gate_ps = k.ps(f"{tag}_gate_ps", [P, BANK])
        up_ps = k.ps(f"{tag}_up_ps", [P, UP_BANKS, BANK])
        down_ps = k.ps(f"{tag}_down_ps", [P, 2, EXPERTS, D])
        chain = k.sem(f"{tag}_chain")
        ms_ready = k.sem(f"{tag}_ms_ready")
        std_ready = k.sem(f"{tag}_std_ready")
        normed = k.sem(f"{tag}_normed")
        turned = k.sem(f"{tag}_turned")
        zt_out = k.sem(f"{tag}_zt_out")
        gated = k.sem(f"{tag}_gated")
        logits_out = k.sem(f"{tag}_logits_out")
        shifted = k.sem(f"{tag}_shifted")
        exped = k.sem(f"{tag}_exped")
        up_done = k.sem(f"{tag}_up_done")
        silu_done = k.sem(f"{tag}_silu_done")
        down_done = k.sem(f"{tag}_down_done")
        down_out = k.sem(f"{tag}_down_out")
        summed = k.sem(f"{tag}_summed")
        z_added = k.sem(f"{tag}_z_added")
        mean_ready = k.sem(f"{tag}_mean_ready")
        squared = k.sem(f"{tag}_squared")
        ln_std_ready = k.sem(f"{tag}_ln_std_ready")
        ln_done = k.sem(f"{tag}_ln_done")
        mean_step = k.sem(f"{tag}_mean_step")
        inverted = k.sem(f"{tag}_inverted")
        before_set = k.sem(f"{tag}_before_set")
        weights_in = k.sem(f"{tag}_weights_in")
        block = stack.enter_context(nc.Block())

        def over_chunks(engine, chunk):
            with engine.Fori(0, CHUNKS // 2 - 1) as i:
                chunk(i * 2, 0, False, True)
                chunk(i * 2 + 1, 1, False, True)
            with engine.Fori(CHUNKS // 2 - 1, NC // 2 - 1) as i:
                chunk(i * 2, 0, False, False)
                chunk(i * 2 + 1, 1, False, False)
            chunk(NC - 2, 0, False, False)
            chunk(NC - 1, 1, True, False)

        @block.sync
        def _(sp):
            fetch(sp)
            sp.sem_inc(weights_in, 1)

        @block.gpsimd
        def _(pool):
            pool.memset(w["before"], 0.0).then_inc(before_set, 1)
            pool.wait_ge(before_set, 1)
            for g in range(1, GROUPS):
                pool.memset(w["before"][:, g, 0:g], 1.0).then_inc(before_set, 1)
            with pool.Fori(0, CHUNKS) as m:
                pool.wait_ge(z_added, m * CT + (LOOPS * TILES + CT))
                x = X[:, bass.ds(m * CT, CT), :]
                pool.tensor_tensor(x, x, Z[:, bass.ds(m * CT + LOOPS * TILES, CT), :], ALU.add)

        @block.tensor
        def _(pe):
            pe.sem_inc(down_done, CT)

            def turn(m):
                pe.wait_ge(normed, m + 1)
                pe.wait_ge(zt_out, m + 1)
                for t in range(CT):
                    last = pe.transpose(turned_ps[:, t, :], scratch[:, t, :], ident)
                last.then_inc(turned, 1)

            def gates(m, half):
                pe.wait_ge(zt_out, m + 2)
                pe.wait_ge(logits_out, m + 1)
                for t in range(CT):
                    last = pe.matmul(gate_ps[:, t * GATES:(t + 1) * GATES], ZT[:, half, t * P:(t + 1) * P],
                                     w["gates"], start=True, stop=True)
                last.then_inc(gated, 1)

            def chunk(n, half, final, more):
                for f in range(FT):
                    pe.wait_ge(silu_done, n * FT + (f + 1))
                    pe.matmul(up_ps[:, f % UP_BANKS, :], w["w1"][:, f * P:(f + 1) * P], ZT[:, half, :],
                              start=True, stop=True).then_inc(up_done, 1)
                for t in range(CT):
                    pe.wait_ge(down_out, n * CT + (t + 1))
                    for e in range(EXPERTS):
                        for h in range(HALVES):
                            if t == 0 and h == 0:
                                pe.wait_ge(silu_done, n * FT + ((e + 1) * HALVES + UP_BANKS))
                            last = pe.matmul(down_ps[:, t % 2, e, :],
                                             hidden[:, e * HALVES + h, t * P:(t + 1) * P],
                                             w["w2"][:, e * HALVES + h, :], start=(h == 0),
                                             stop=(h == HALVES - 1))
                    last.then_inc(down_done, 1)
                    if t == 0 and not final:
                        turn(n + 1)
                    if t == 1 and not final:
                        gates(n + 1, 1 - half)

            turn(0)
            pe.wait_ge(weights_in, 1)
            gates(0, 0)
            over_chunks(pe, chunk)

        @block.scalar
        def _(act):
            act.sem_inc(silu_done, UP_BANKS)
            act.sem_inc(zt_out, 1)

            def spread_of_x(m):
                act.wait_ge(mean_ready, m + 1)
                for t in range(CT):
                    last = act.activation(square[:, t, :], X[:, bass.ds(m * CT + t, 1), :].rearrange("p o d -> p (o d)"),
                                          ACT.Square, bias=neg_mean[:, t:t + 1], accum_out=var[:, t:t + 1])
                last.then_inc(squared, 1)
                act.wait_ge(squared, m + 1)
                act.activation(ln_std[:, :], var[:, :], ACT.Sqrt, bias=eps[:, 1:2], scale=1.0 / D
                               ).then_inc(ln_std_ready, 1)

            def prepare(m, half, more):
                act.wait_ge(ms_ready, m + 1)
                act.activation(std[:, :], ms[:, :], ACT.Sqrt, bias=eps[:, 0:1], scale=1.0 / D).then_inc(std_ready, 1)
                if more:
                    spread_of_x(m + 1)
                act.wait_ge(turned, m + 1)
                act.activation(ZT[:, half, :], turned_ps[:, :, :].rearrange("p t q -> p (t q)"), ACT.Copy,
                               scale=w["norm"]).then_inc(zt_out, 1)
                act.wait_ge(shifted, m + 1)
                act.activation(exps[:, :, :], logits[:, :, :], ACT.Exp).then_inc(exped, 1)
                act.activation(warm[:, :], eps[:, 0:1], ACT.Silu)

            def chunk(n, half, final, more):
                act.wait_ge(down_done, n * CT + CT)
                for f in range(FT):
                    act.wait_ge(up_done, n * FT + (f + 1))
                    act.activation(hidden[:, f, :], up_ps[:, f % UP_BANKS, :], ACT.Silu).then_inc(silu_done, 1)
                if not final:
                    prepare(n + 1, 1 - half, more)

            spread_of_x(0)
            spread_of_x(1)
            act.wait_ge(weights_in, 1)
            prepare(0, 0, False)
            over_chunks(act, chunk)

        @block.vector
        def _(dve):
            LINKS = 29
            dve.sem_inc(down_out, 2)
            dve.sem_inc(logits_out, 1)
            dve.sem_inc(z_added, TILES)
            dve.memset(eps[:, 0:1], RMS_EPS).then_inc(chain, 1)
            dve.memset(eps[:, 1:2], LN_EPS).then_inc(chain, 1)
            dve.wait_ge(chain, 2)

            def chunk_rows(m):
                return Z[:, bass.ds(m * CT, CT), :]

            def means_of_x(m):
                x = X[:, bass.ds(m * CT, CT), :]
                dve.tensor_reduce(neg_mean[:, :], x, AX, ALU.add).then_inc(mean_step, 1)
                dve.wait_ge(mean_step, m + 1)
                dve.tensor_scalar(neg_mean[:, :], neg_mean[:, :], -1.0 / D, None, ALU.mult).then_inc(mean_ready, 1)

            def layer_norm_of_x(m):
                dve.wait_ge(ln_std_ready, m + 1)
                dve.reciprocal(ln_std[:, :], ln_std[:, :]).then_inc(inverted, 1)
                dve.wait_ge(inverted, m + 1)
                for t in range(CT):
                    z, x = (a[:, bass.ds(m * CT + t, 1), :].rearrange("p o d -> p (o d)") for a in (Z, X))
                    last = dve.tensor_scalar(z, x, neg_mean[:, t:t + 1], ln_std[:, t:t + 1], ALU.add, ALU.mult)
                last.then_inc(ln_done, 1)
                dve.wait_ge(ln_done, m + 1)

            def mean_square(m, link):
                dve.wait_ge(z_added, m * CT + CT)
                link(dve.tensor_tensor(scratch[:, :, :], chunk_rows(m), chunk_rows(m), ALU.mult))
                dve.tensor_reduce(ms[:, :], scratch[:, :, :], AX, ALU.add).then_inc(ms_ready, 1)

            def normalised(m, link):
                dve.wait_ge(std_ready, m + 1)
                link(dve.reciprocal(std[:, :], std[:, :]))
                dve.tensor_tensor(scratch[:, :, :], chunk_rows(m), over(std[:, :], D), ALU.mult).then_inc(normed, 1)

            def shifted_logits(m, link):
                dve.wait_ge(gated, m + 1)
                dve.tensor_copy(logits[:, :, :], gate_ps[:, 0:CT * GATES].rearrange("p (t g) -> p t g", g=GATES)
                                ).then_inc(logits_out, 1)
                dve.wait_ge(logits_out, m + 2)
                coarse = logits[:, :, 0:GROUPS]
                fine = logits[:, :, GROUPS:].rearrange("p t (g e) -> p t g e", e=PER_GROUP)
                link(dve.tensor_reduce(top[:, :, 0], coarse, AX, ALU.max))
                link(dve.tensor_reduce(top[:, :, 1:], fine, AX, ALU.max))
                link(dve.tensor_tensor(coarse, coarse, over(top[:, :, 0], GROUPS), ALU.subtract))
                dve.tensor_tensor(fine, fine, over(top[:, :, 1:], PER_GROUP), ALU.subtract).then_inc(shifted, 1)

            def gate_weights(m, half, link):
                dve.wait_ge(exped, m + 1)
                coarse = exps[:, :, 0:GROUPS]
                fine = exps[:, :, GROUPS:].rearrange("p t (g e) -> p t g e", e=PER_GROUP)
                link(dve.tensor_reduce(total[:, :, 0], coarse, AX, ALU.add))
                link(dve.tensor_reduce(total[:, :, 1:], fine, AX, ALU.add))
                link(dve.reciprocal(total[:, :, :], total[:, :, :]))
                link(dve.tensor_tensor(coarse, coarse, over(total[:, :, 0], GROUPS), ALU.mult))
                link(dve.tensor_tensor(fine, fine, over(total[:, :, 1:], PER_GROUP), ALU.mult))
                mine = over(coarse, GROUPS)
                others = coarse.unsqueeze(2).to_broadcast([P, CT, GROUPS, GROUPS])
                before = w["before"].unsqueeze(1).to_broadcast([P, CT, GROUPS, GROUPS])
                link(dve.tensor_tensor(beats[:, :, :, :], others, mine, ALU.is_gt))
                link(dve.tensor_tensor(ties[:, :, :, :], others, mine, ALU.is_equal))
                link(dve.tensor_tensor(ties[:, :, :, :], ties[:, :, :, :], before, ALU.mult))
                link(dve.tensor_tensor(beats[:, :, :, :], beats[:, :, :, :], ties[:, :, :, :], ALU.add))
                link(dve.tensor_reduce(rank[:, :, :], beats[:, :, :, :], AX, ALU.add))
                link(dve.tensor_scalar(rank[:, :, :], rank[:, :, :], 2.0, None, ALU.is_lt))
                link(dve.tensor_tensor(rank[:, :, :], rank[:, :, :], coarse, ALU.mult))
                link(dve.tensor_reduce(pair[:, :], rank[:, :, :], AX, ALU.add))
                link(dve.tensor_scalar(pair[:, :], pair[:, :], GATE_EPS, None, ALU.add))
                link(dve.reciprocal(pair[:, :], pair[:, :]))
                link(dve.tensor_tensor(rank[:, :, :], rank[:, :, :], over(pair[:, :], GROUPS), ALU.mult))
                link(dve.tensor_reduce(best[:, :, :], fine, AX, ALU.max))
                link(dve.tensor_scalar(inv_best[:, :, :], best[:, :, :], GATE_EPS, None, ALU.add))
                link(dve.reciprocal(inv_best[:, :, :], inv_best[:, :, :]))
                link(dve.tensor_tensor(best[:, :, :], best[:, :, :], inv_best[:, :, :], ALU.mult))
                link(dve.tensor_tensor(rank[:, :, :], rank[:, :, :], best[:, :, :], ALU.mult))
                link(dve.tensor_tensor(second[:, :, :], fine[:, :, :, 1], fine[:, :, :, 0], ALU.is_gt))
                out = combine[:, half, :, :].rearrange("p t (g e) -> p t g e", e=PER_GROUP)
                link(dve.tensor_tensor(out[:, :, :, 1], rank[:, :, :], second[:, :, :], ALU.mult))
                link(dve.tensor_tensor(out[:, :, :, 0], rank[:, :, :], out[:, :, :, 1], ALU.subtract))

            def mix(n, half, t):
                tile = n * CT + t
                dve.wait_ge(down_done, tile + (1 + CT))
                dve.tensor_tensor(weighted[:, :, :], down_ps[:, t % 2, :, :], over(combine[:, half, t, :], D),
                                  ALU.mult).then_inc(down_out, 1)
                dve.wait_ge(down_out, tile + 3)
                dve.tensor_reduce(mixed[:, :], weighted[:, :, :].rearrange("p e d -> p d e"), AX,
                                  ALU.add).then_inc(summed, 1)
                dve.wait_ge(summed, tile + 1)
                now, then = (Z[:, bass.ds(at, 1), :].rearrange("p o d -> p (o d)") for at in (tile, tile + TILES))
                dve.tensor_tensor(then, now, mixed[:, :], ALU.add).then_inc(z_added, 1)

            def chunk(n, half, final, more):
                link = counter(dve, chain, n * LINKS + (2 + LINKS))
                if final:
                    for t in range(CT):
                        mix(n, half, t)
                    return
                mean_square(n + 1, link)
                if more:
                    means_of_x(n + 2)
                normalised(n + 1, link)
                if more:
                    layer_norm_of_x(n + 2)
                mix(n, half, 0)
                shifted_logits(n + 1, link)
                mix(n, half, 1)
                mix(n, half, 2)
                gate_weights(n + 1, 1 - half, link)
                mix(n, half, 3)
                assert link.count[0] == LINKS, link.count[0]

            for m in range(2):
                means_of_x(m)
                layer_norm_of_x(m)
            link = counter(dve, chain, 2)
            mean_square(0, link)
            normalised(0, link)
            shifted_logits(0, link)
            dve.wait_ge(before_set, GROUPS)
            gate_weights(0, 0, link)
            assert link.count[0] == LINKS, link.count[0]
            over_chunks(dve, chunk)


def moe_ffn(nc, tag, X, w, ident, fetch):
    with ExitStack() as stack:
        k = Kit(nc, stack)
        Z = k.sb(f"{tag}_Z", [P, (LOOPS + 1) * TILES, D])
        w["before"] = k.sb(f"{tag}_before", [P, GROUPS, GROUPS])[:, :, :]
        mixture(nc, f"{tag}_mix", X, Z[:, :, :], w, ident, fetch)


STEPS = BATCH
FH, FD = 16, 64
FW = FH * FD


def fast_weights(nc, tag, X, w, ident, fetch):
    with ExitStack() as stack:
        k = Kit(nc, stack)
        H = k.sb(f"{tag}_H", [P, TILES, D])
        HT = k.sb(f"{tag}_HT", [P, TOK])
        layer_norm(nc, f"{tag}_ln", X, H, HT, ident, beside={"sync": fetch})
        recur(nc, f"{tag}_recur", H, HT[:, :], w, ident)
        layer_norm(nc, f"{tag}_ln2", H, H, None, ident, gain=w["ln_g"], shift=w["ln_b"], residual=X)


def recur(nc, tag, H, HT, w, ident):
    with ExitStack() as stack:
        k = Kit(nc, stack)
        kk = k.sb(f"{tag}_kk", [P, STEPS, STEPS, TPB, FH])
        kq = k.sb(f"{tag}_kq", [P, STEPS, STEPS, TPB, FH])
        sums = k.sb(f"{tag}_sums", [P, 2, STEPS, TPB, FH])
        dots(nc, f"{tag}_dots", HT, w, kk, kq, sums, ident)
        combine_values(nc, f"{tag}_values", H, HT, w, kk, kq, sums, ident)


def heads(ap):
    return ap.rearrange("p s (h e) -> p s h e", e=FD)


def one(ap):
    return ap.rearrange("p s o h -> p s (o h)")


def stage_tokens(act, HT, ht, b):
    src = HT.rearrange("p (s t) -> p s t", s=STEPS)[:, :, bass.ds(b * P, P)]
    return act.copy(ht, src)


def dots(nc, tag, HT, w, kk, kq, sums, ident):
    FT8 = FW // P
    UNITS = 2 * STEPS
    BURSTS = 6
    BANKS = BURSTS // 2
    SLOTS = 4
    GROUP_ROWS = 2 * FH
    PRODUCTS = ([("kk", 1, 0), ("kq", 0, 0), ("kq", 1, 0), ("kq", 1, 1)]
                + [("kk", 2, s) for s in range(2)] + [("kk", 3, s) for s in range(3)]
                + [("kq", 2, s) for s in range(3)] + [("kq", 3, s) for s in range(4)])
    POOLS = (("kk", 1), ("kq", 0), ("kq", 1), ("kq", 3))
    DVES = (("kk", 2), ("kk", 3), ("kq", 2))

    def place(kind, t):
        at = [i for i, p in enumerate(PRODUCTS) if p[:2] == (kind, t)]
        return at[0], len(at)

    with ExitStack() as stack:
        k = Kit(nc, stack)
        ones = k.sb(f"{tag}_ones", [P, 2, FT8, GROUP_ROWS])
        vecs = k.sb(f"{tag}_vecs", [P, 2, UNITS, CHUNK])
        low = k.sb(f"{tag}_low", [P, SLOTS, CHUNK])
        prods = k.sb(f"{tag}_prods", [P, 2, len(PRODUCTS), CHUNK])
        summed_sb = k.sb(f"{tag}_summed_sb", [P, BANKS, CHUNK])
        vec_ps = k.ps(f"{tag}_vec_ps", [P, SLOTS, BANK])
        sum_ps = k.ps(f"{tag}_sum_ps", [P, BANKS, BANK])
        ones_set = k.sem(f"{tag}_ones_set")
        projected = k.sem(f"{tag}_projected")
        negated = k.sem(f"{tag}_negated")
        low_done = k.sem(f"{tag}_low_done")
        vec_out = k.sem(f"{tag}_vec_out")
        pool_prods = k.sem(f"{tag}_pool_prods")
        dve_prods = k.sem(f"{tag}_dve_prods")
        reduced = k.sem(f"{tag}_reduced")
        sums_out = k.sem(f"{tag}_sums_out")
        turned = k.sem(f"{tag}_turned")
        turned_out = k.sem(f"{tag}_turned_out")
        block = stack.enter_context(nc.Block())

        @block.tensor
        def _(pe):
            pe.sem_inc(reduced, 2 * BURSTS)
            pe.wait_ge(ones_set, 5)

            def project(B, c, u):
                pe.wait_ge(vec_out, (B * FT8 + c) * UNITS + (u + 1))
                at = (FW if u < STEPS else 0) + c * P
                pe.matmul(vec_ps[:, u % SLOTS, :], w["qkv"][:, at:at + P],
                          HT[:, bass.ds(B * CHUNK + (u % STEPS) * SEQ, CHUNK)], start=True,
                          stop=True).then_inc(projected, 1)

            def sum_burst(B, c, burst):
                it, (bank, half) = B * FT8 + c, divmod(burst, 2)
                if burst >= 2:
                    kinds = {PRODUCTS[4 * burst - 8 + j][:2] for j in range(4)}
                    pools = [POOLS.index(x) for x in kinds if x in POOLS]
                    dves = [DVES.index(x) for x in kinds if x in DVES]
                    if pools:
                        pe.wait_ge(pool_prods, it * len(POOLS) + (max(pools) + 1))
                    if dves:
                        pe.wait_ge(dve_prods, it * len(DVES) + (max(dves) + 1))
                for j in range(4):
                    moving = vecs[:, c % 2, 4 * burst + j, :] if burst < 2 else prods[:, c % 2, 4 * burst - 8 + j, :]
                    last = pe.matmul(sum_ps[GROUP_ROWS * j:GROUP_ROWS * (j + 1), bank, :], ones[:, half, c, :],
                                     moving, start=(c == 0 and half == 0), stop=(c == FT8 - 1 and half == 1))
                last.then_inc(reduced, 1)

            with pe.Fori(0, TPB // CT) as B:
                pe.wait_ge(turned_out, B * BANKS + 1)
                for c in range(FT8):
                    for u in range(UNITS):
                        project(B, c, u)
                        if c and u >= UNITS - BURSTS:
                            if u == UNITS - BURSTS:
                                pe.wait_ge(vec_out, (B * FT8 + c) * UNITS + SLOTS)
                            sum_burst(B, c - 1, u - (UNITS - BURSTS))
                pe.wait_ge(vec_out, (B * FT8 + FT8) * UNITS + SLOTS)
                for burst in range(BURSTS):
                    sum_burst(B, FT8 - 1, burst)
                for bank in range(BANKS):
                    pe.wait_ge(sums_out, B * BANKS + (bank + 1))
                    for t in range(CT):
                        last = pe.transpose(vec_ps[:, bank, t * P:(t + 1) * P],
                                            summed_sb[:, bank, t * P:(t + 1) * P], ident)
                    last.then_inc(turned, 1)

        @block.scalar
        def _(act):
            with act.Fori(0, TPB // CT) as B:
                for c in range(FT8):
                    for u in range(UNITS):
                        n = (B * FT8 + c) * UNITS + (u + 1)
                        act.wait_ge(projected, n)
                        act.wait_ge(vec_out, n)
                        act.activation(low[:, u % SLOTS, :], vec_ps[:, u % SLOTS, :], ACT.Relu,
                                       scale=-1.0).then_inc(negated, 1)
                        act.wait_ge(negated, n)
                        act.activation(low[:, u % SLOTS, :], low[:, u % SLOTS, :], ACT.Exp,
                                       scale=-1.0).then_inc(low_done, 1)
                for bank in range(BANKS):
                    act.wait_ge(reduced, (B * FT8 + (FT8 - 1)) * BURSTS + (2 * bank + 2 + 2 * BURSTS))
                    act.copy(summed_sb[:, bank, :], sum_ps[:, bank, :]).then_inc(sums_out, 1)

        def multiply(engine, c, kind, t):
            at, n = place(kind, t)
            other = t if kind == "kk" else STEPS + t
            return engine.tensor_tensor(prods[:, c % 2, at:at + n, :], vecs[:, c % 2, 0:n, :],
                                        vecs[:, c % 2, other:other + 1, :].to_broadcast([P, n, CHUNK]), ALU.mult)

        @block.gpsimd
        def _(pool):
            pool.memset(ones[:, :, :, :], 1.0).then_inc(ones_set, 1)
            for half in range(2):
                for step, (base, sign) in enumerate(((0, 1), (FD - 1, -1))):
                    pool.wait_ge(ones_set, 2 * half + step + 1)
                    pool.affine_select(out=ones[:, half, :, :], in_=ones[:, half, :, :], compare_op=ALU.is_ge,
                                       fill=0.0, base=base + sign * half * FH * FD,
                                       pattern=[[sign * P, FT8], [-sign * FD, GROUP_ROWS]],
                                       channel_multiplier=sign).then_inc(ones_set, 1)
            with pool.Fori(0, TPB // CT) as B:
                for c in range(FT8):
                    for kind, t in POOLS:
                        other = t if kind == "kk" else STEPS + t
                        pool.wait_ge(vec_out, (B * FT8 + c) * UNITS + (other + 1 + SLOTS))
                        multiply(pool, c, kind, t).then_inc(pool_prods, 1)

        @block.vector
        def _(dve):
            dve.sem_inc(vec_out, SLOTS)
            dve.sem_inc(turned_out, 1)

            def take(B, c, u):
                it = B * FT8 + c
                dve.wait_ge(low_done, it * UNITS + (u + 1))
                if u == 0:
                    dve.wait_ge(reduced, it * BURSTS + BURSTS)
                dve.scalar_tensor_tensor(out=vecs[:, c % 2, u, :], in0=vec_ps[:, u % SLOTS, :], scalar=0.0,
                                         in1=low[:, u % SLOTS, :], op0=ALU.max, op1=ALU.add).then_inc(vec_out, 1)

            def own_products(B, c, m):
                dve.wait_ge(vec_out, (B * FT8 + c) * UNITS + (UNITS + SLOTS))
                multiply(dve, c, *DVES[m]).then_inc(dve_prods, 1)

            with dve.Fori(0, TPB // CT) as B:
                for c in range(FT8):
                    for u in range(UNITS):
                        take(B, c, u)
                        if c and u % 2 == 0 and u // 2 < len(DVES):
                            own_products(B, c - 1, u // 2)
                for m in range(len(DVES)):
                    own_products(B, FT8 - 1, m)
                for bank in range(BANKS):
                    dve.wait_ge(turned, B * BANKS + (bank + 1))
                    rows = vec_ps[:, bank, :].rearrange("p (t r) -> p t r", r=P)
                    for a in range(8 * bank, 8 * (bank + 1)):
                        if a < UNITS:
                            dst = sums[:, a // STEPS, a % STEPS]
                        else:
                            kind, t, s = PRODUCTS[a - UNITS]
                            dst = (kk if kind == "kk" else kq)[:, t, s]
                        at = GROUP_ROWS * (a % 4) + FH * (a // 4 % 2)
                        last = dve.tensor_copy(dst[:, bass.ds(B * CT, CT), :], rows[:, :, at:at + FH])
                    last.then_inc(turned_out, 1)


def combine_values(nc, tag, H, HT, w, kk, kq, sums, ident):
    with ExitStack() as stack:
        k = Kit(nc, stack)
        ht = k.sb(f"{tag}_ht", [P, 2, STEPS, P])
        v = k.sb(f"{tag}_v", [P, 2, STEPS, FW])
        prod1 = k.sb(f"{tag}_prod1", [P, 2, 2, FW])
        prod2 = k.sb(f"{tag}_prod2", [P, 2, 3, FW])
        prod3 = k.sb(f"{tag}_prod3", [P, 4, FW])
        mixed = k.sb(f"{tag}_mixed", [P, 2, FW])
        mixed_t = k.sb(f"{tag}_mixed_t", [P, 2, FW // P, P])
        beta = k.sb(f"{tag}_beta", [P, STEPS, TPB, FH])
        lower = mixed[:, :, :].rearrange("p a (t r b h) -> p (a t) r b h", t=2, r=STEPS, b=TPB)
        coef = k.sb(f"{tag}_coef", [P, STEPS, STEPS, TPB, FH])
        term = k.sb(f"{tag}_term", [P, STEPS, TPB, FH])
        v_ps = k.ps(f"{tag}_v_ps", [P, 2, FW])
        turned_ps = k.ps(f"{tag}_turned_ps", [P, FW // P, P])
        y_ps = k.ps(f"{tag}_y_ps", [P, 2, BANK])
        beta_ps = y_ps[:, 1, :].rearrange("p (t h) -> p t h", h=FH)
        beta_done = k.sem(f"{tag}_beta_done")
        beta_exp = k.sem(f"{tag}_beta_exp")
        chain = k.sem(f"{tag}_chain")
        coef_done = k.sem(f"{tag}_coef_done")
        ht_set = k.sem(f"{tag}_ht_set")
        projected = k.sem(f"{tag}_projected")
        v_out = k.sem(f"{tag}_v_out")
        scaled = k.sem(f"{tag}_scaled")
        scaled3 = k.sem(f"{tag}_scaled3")
        summing = k.sem(f"{tag}_summing")
        mixed_done = k.sem(f"{tag}_mixed_done")
        turned = k.sem(f"{tag}_turned")
        copied = k.sem(f"{tag}_copied")
        attended = k.sem(f"{tag}_attended")
        added = k.sem(f"{tag}_added")
        block = stack.enter_context(nc.Block())

        @block.tensor
        def _(pe):
            pe.sem_inc(turned, 2)
            pe.sem_inc(attended, 2)

            def project(b, half, s):
                pe.wait_ge(v_out, b * STEPS + (s + 1))
                for c in range(FW // BANK):
                    at = 2 * FW + c * BANK
                    last = pe.matmul(v_ps[:, s % 2, c * BANK:(c + 1) * BANK], ht[:, half, s, :],
                                     w["qkv"][:, at:at + BANK], start=True, stop=True)
                last.then_inc(projected, 1)

            def tile(b, half, final):
                if not final:
                    pe.wait_ge(ht_set, b + 2)
                for t in range(STEPS):
                    n = b * STEPS + (t + 1)
                    pe.wait_ge(mixed_done, n + STEPS)
                    pe.wait_ge(copied, n)
                    for c in range(FW // P):
                        last = pe.transpose(turned_ps[:, c, :], mixed[:, t % 2, c * P:(c + 1) * P], ident)
                    last.then_inc(turned, 1)
                    if not final:
                        project(b + 1, 1 - half, t)
                    pe.wait_ge(copied, n + 1)
                    pe.wait_ge(added, n)
                    for c in range(FW // P):
                        last = pe.matmul(y_ps[:, t % 2, 0:D], mixed_t[:, t % 2, c, :], w["out"][:, c, :],
                                         start=(c == 0), stop=(c == FW // P - 1))
                    last.then_inc(attended, 1)

            for t in range(TILES):
                last = pe.matmul(beta_ps[:, t, :], HT[:, t * P:(t + 1) * P], w["qkv"][:, 3 * FW:3 * FW + FH],
                                 start=True, stop=True)
            last.then_inc(beta_done, 1)
            pe.wait_ge(ht_set, 1)
            for s in range(STEPS):
                project(0, 0, s)
            with pe.Fori(0, TPB // 2 - 1) as i:
                tile(i * 2, 0, False)
                tile(i * 2 + 1, 1, False)
            tile(TPB - 2, 0, False)
            tile(TPB - 1, 1, True)

        @block.scalar
        def _(act):
            act.sem_inc(v_out, 2)
            act.sem_inc(copied, 1)

            def take_value(b, half, s):
                act.wait_ge(projected, b * STEPS + (s + 1))
                act.copy(v[:, half, s, :], v_ps[:, s % 2, :]).then_inc(v_out, 1)

            def tile(b, half, final):
                if not final:
                    stage_tokens(act, HT, ht[:, 1 - half, :, :], b + 1).then_inc(ht_set, 1)
                for t in range(STEPS):
                    n = b * STEPS + (t + 1)
                    act.wait_ge(turned, n + 2)
                    act.wait_ge(attended, n)
                    act.copy(mixed_t[:, t % 2, :, :], turned_ps[:, :, :]).then_inc(copied, 1)
                    if not final:
                        if t == 0:
                            act.wait_ge(mixed_done, b * STEPS + STEPS)
                        take_value(b + 1, 1 - half, t)

            act.wait_ge(beta_done, 1)
            act.activation(beta[:, :, :, :].rearrange("p s b h -> p (s b) h"), beta_ps[:, :, :], ACT.Exp,
                           scale=-1.0).then_inc(beta_exp, 1)
            stage_tokens(act, HT, ht[:, 0, :, :], 0).then_inc(ht_set, 1)
            for s in range(STEPS):
                take_value(0, 0, s)
            with act.Fori(0, TPB // 2 - 1) as i:
                tile(i * 2, 0, False)
                tile(i * 2 + 1, 1, False)
            tile(TPB - 2, 0, False)
            tile(TPB - 1, 1, True)

        def of_tile(b, t, n):
            return over(one(coef[:, t, 0:n, bass.ds(b, 1), :]), FD)

        @block.gpsimd
        def _(pool):
            pool.wait_ge(coef_done, 1)
            with pool.Fori(0, TPB // 2) as i:
                for half in range(2):
                    b = i * 2 + half
                    for t, prod in ((1, prod1), (2, prod2)):
                        pool.wait_ge(v_out, b * STEPS + (t + 3))
                        pool.tensor_tensor(heads(prod[:, half, :, :]), heads(v[:, half, 0:t + 1, :]),
                                           of_tile(b, t, t + 1), ALU.mult).then_inc(scaled, 1)

        @block.vector
        def _(dve):
            dve.sem_inc(mixed_done, STEPS)
            dve.sem_inc(added, 2)
            link = counter(dve, chain)
            link(dve.reciprocal(sums[:, :, :, :, :], sums[:, :, :, :, :]))
            inv_k, inv_q = sums[:, 0, :, :, :], sums[:, 1, :, :, :]
            link(dve.tensor_scalar(inv_q, inv_q, FD ** -0.5, None, ALU.mult))
            for t in range(STEPS):
                for table, inv, n in ((kk, inv_k, t), (kq, inv_q, t + 1)):
                    if n:
                        row = table[:, t, 0:n, :, :]
                        link(dve.tensor_tensor(row, row, inv_k[:, 0:n, :, :], ALU.mult))
                        link(dve.tensor_tensor(row, row, inv[:, t:t + 1, :, :].to_broadcast([P, n, TPB, FH]), ALU.mult))
            dve.wait_ge(beta_exp, 1)
            link(dve.tensor_scalar(beta[:, :, :, :], beta[:, :, :, :], 1.0, None, ALU.add))
            link(dve.reciprocal(beta[:, :, :, :], beta[:, :, :, :]))

            def by(table, t, s):
                return table[:, t, s:s + 1, :, :].to_broadcast([P, s + 1, TPB, FH])
            for t in range(STEPS):
                link(dve.tensor_copy(lower[:, t, t, :, :], beta[:, t, :, :]))
                if t:
                    link(dve.memset(lower[:, t, 0:t, :, :], 0.0))
                for s in range(t):
                    link(dve.tensor_tensor(term[:, 0:s + 1, :, :], lower[:, s, 0:s + 1, :, :], by(kk, t, s), ALU.mult))
                    link(dve.tensor_tensor(lower[:, t, 0:s + 1, :, :], lower[:, t, 0:s + 1, :, :],
                                           term[:, 0:s + 1, :, :], ALU.subtract))
                if t:
                    link(dve.tensor_tensor(lower[:, t, 0:t, :, :], lower[:, t, 0:t, :, :],
                                           beta[:, t:t + 1, :, :].to_broadcast([P, t, TPB, FH]), ALU.mult))
            for t in range(STEPS):
                for s in range(t, -1, -1):
                    dst = coef[:, t, 0:s + 1, :, :] if s == t else term[:, 0:s + 1, :, :]
                    link(dve.tensor_tensor(dst, lower[:, s, 0:s + 1, :, :], by(kq, t, s), ALU.mult))
                    if s < t:
                        link(dve.tensor_tensor(coef[:, t, 0:s + 1, :, :], coef[:, t, 0:s + 1, :, :],
                                               term[:, 0:s + 1, :, :], ALU.add))
            dve.sem_inc(coef_done, 1)

            def add_output(b, t):
                dve.wait_ge(attended, b * STEPS + (t + 3))
                h = H[:, bass.ds(t * TPB + b, 1), :].rearrange("p o d -> p (o d)")
                dve.tensor_tensor(h, h, y_ps[:, t % 2, 0:D], ALU.add).then_inc(added, 1)

            def tile(b, half, first):
                def room(t):
                    dve.wait_ge(turned, b * STEPS + (t + 1))
                dve.wait_ge(v_out, b * STEPS + 3)
                room(0)
                dve.tensor_tensor(heads(mixed[:, 0:1, :]), heads(v[:, half, 0:1, :]), of_tile(b, 0, 1),
                                  ALU.mult).then_inc(mixed_done, 1)
                if not first:
                    add_output(b - 1, STEPS - 1)
                dve.wait_ge(v_out, b * STEPS + (STEPS + 2))
                dve.tensor_tensor(heads(prod3[:, :, :]), heads(v[:, half, :, :]), of_tile(b, 3, 4),
                                  ALU.mult).then_inc(scaled3, 1)
                dve.wait_ge(scaled, b * 2 + 1)
                room(1)
                dve.tensor_tensor(mixed[:, 1, :], prod1[:, half, 0, :], prod1[:, half, 1, :], ALU.add).then_inc(mixed_done, 1)
                add_output(b, 0)
                dve.wait_ge(scaled3, b + 1)
                dve.tensor_tensor(prod3[:, 0:2, :], prod3[:, 0:2, :], prod3[:, 2:4, :], ALU.add).then_inc(summing, 1)
                dve.wait_ge(scaled, b * 2 + 2)
                dve.tensor_tensor(prod2[:, half, 0, :], prod2[:, half, 0, :], prod2[:, half, 1, :], ALU.add).then_inc(summing, 1)
                dve.wait_ge(summing, b * 2 + 2)
                room(2)
                dve.tensor_tensor(mixed[:, 0, :], prod2[:, half, 0, :], prod2[:, half, 2, :], ALU.add).then_inc(mixed_done, 1)
                add_output(b, 1)
                room(3)
                dve.tensor_tensor(mixed[:, 1, :], prod3[:, 0, :], prod3[:, 1, :], ALU.add).then_inc(mixed_done, 1)
                add_output(b, 2)

            dve.wait_ge(coef_done, 1)
            tile(0, 0, True)
            with dve.Fori(0, TPB // 2 - 1) as i:
                tile(i * 2 + 1, 1, False)
                tile(i * 2 + 2, 0, False)
            tile(TPB - 1, 1, False)
            add_output(TPB - 1, STEPS - 1)


LE, LR = 8, 8
LORA_SCALE = 16 / LR


def lora_ffn(nc, tag, X, w, ident, fetch):
    with ExitStack() as stack:
        k = Kit(nc, stack)
        XN = k.sb(f"{tag}_XN", [P, TILES, D])
        XT = k.sb(f"{tag}_XT", [P, TOK])
        layer_norm(nc, f"{tag}_ln", X, XN, XT, ident, beside={"sync": fetch})
        small = k.sb(f"{tag}_small", [P, TILES, LE + LR])
        top = k.sb(f"{tag}_top", [P, TILES])
        gates = k.sb(f"{tag}_gates", [P, TILES, LE], BF16)
        outer = k.sb(f"{tag}_outer", [P, TILES, LE * LR])
        outer_t = k.sb(f"{tag}_outer_t", [LE * LR, 2, 4, P])
        small_ps = k.ps(f"{tag}_small_ps", [P, TILES, LE + LR])
        t_ps = k.ps(f"{tag}_t_ps", [LE * LR, 2, 4, P])
        y_ps = k.ps(f"{tag}_y_ps", [P, 2, 4, D])
        small_done = k.sem(f"{tag}_small_done")
        step_done = k.sem(f"{tag}_step_done")
        shifted = k.sem(f"{tag}_shifted")
        exped = k.sem(f"{tag}_exped")
        outer_done = k.sem(f"{tag}_outer_done")
        turned = k.sem(f"{tag}_turned")
        copied = k.sem(f"{tag}_copied")
        projected = k.sem(f"{tag}_projected")
        added = k.sem(f"{tag}_added")
        block = stack.enter_context(nc.Block())
        LSTEPS = TILES // 4

        @block.tensor
        def _(pe):
            for t in range(TILES):
                last = pe.matmul(small_ps[:, t, :], XT[:, t * P:(t + 1) * P], w["lora"][:, D:D + LE + LR],
                                 start=True, stop=True)
            last.then_inc(small_done, 1)

            def turn(s):
                if s >= 2:
                    pe.wait_ge(copied, s - 1)
                for t in range(4):
                    last = pe.transpose(t_ps[:, s % 2, t, :], outer[:, 4 * s + t, :], ident)
                last.then_inc(turned, 1)
            pe.wait_ge(outer_done, 1)
            turn(0)
            for s in range(LSTEPS):
                if s + 1 < LSTEPS:
                    turn(s + 1)
                pe.wait_ge(copied, s + 1)
                if s >= 2:
                    pe.wait_ge(added, s - 1)
                for t in range(4):
                    tile = 4 * s + t
                    pe.matmul(y_ps[:, s % 2, t, :], XT[:, tile * P:(tile + 1) * P], w["lora"][:, 0:D],
                              start=True, stop=False)
                    last = pe.matmul(y_ps[:, s % 2, t, :], outer_t[:, s % 2, t, :], w["lora_b"],
                                     start=False, stop=True)
                last.then_inc(projected, 1)

        @block.scalar
        def _(act):
            act.wait_ge(shifted, 1)
            act.activation(small[:, :, 0:LE], small[:, :, 0:LE], ACT.Exp).then_inc(exped, 1)
            for s in range(LSTEPS):
                act.wait_ge(turned, s + 1)
                if s >= 2:
                    act.wait_ge(projected, s - 1)
                act.copy(outer_t[:, s % 2, :, :], t_ps[:, s % 2, :, :]).then_inc(copied, 1)

        @block.vector
        def _(dve):
            link = counter(dve, step_done)
            dve.wait_ge(small_done, 1)
            logits, mid = small[:, :, 0:LE], small[:, :, LE:]
            link(dve.tensor_tensor(logits, small_ps[:, :, 0:LE], over_mid(w["router_b"], TILES), ALU.add))
            link(dve.tensor_scalar(mid, small_ps[:, :, LE:], LORA_SCALE, None, ALU.mult))
            link(dve.tensor_reduce(top[:, :], logits, AX, ALU.max))
            dve.tensor_tensor(logits, logits, over(top[:, :], LE), ALU.subtract).then_inc(shifted, 1)
            dve.wait_ge(exped, 1)
            link(dve.tensor_reduce(top[:, :], logits, AX, ALU.add))
            link(dve.reciprocal(top[:, :], top[:, :]))
            link(dve.tensor_tensor(gates[:, :, :], logits, over(top[:, :], LE), ALU.mult))
            dve.tensor_tensor(outer[:, :, :].rearrange("p t (e r) -> p t e r", r=LR), over(gates[:, :, :], LR),
                              mid.unsqueeze(2).to_broadcast([P, TILES, LE, LR]), ALU.mult).then_inc(outer_done, 1)
            for s in range(LSTEPS):
                x = X[:, 4 * s:4 * s + 4, :]
                link(dve.tensor_tensor(x, x, over_mid(w["base_b"], 4), ALU.add))
                dve.wait_ge(projected, s + 1)
                dve.tensor_tensor(x, x, y_ps[:, s % 2, :, :], ALU.add).then_inc(added, 1)


WEIGHTS = {
    "a": {"qkv": [P, 3 * D], "out": [P, D], "b_qk": [P, 2], "b_v": [D], "b_out": [D]},
    "b": {"qkv": [P, 3 * D], "out": [P, D], "b_qk": [P, 2], "b_v": [D], "b_out": [D], "decay": [1]},
    "m": {"norm": [P, 1], "gates": [P, GATES], "w1": [P, EXPERTS * F], "w2": [P, FT, D]},
    "f": {"qkv": [P, 3 * FW + FH], "out": [P, FW // P, D], "ln_g": [D], "ln_b": [D]},
    "l": {"lora": [P, D + LE + LR], "lora_b": [LE * LR, D], "router_b": [LE], "base_b": [D]},
}


def weights(tag, k, dram, names):
    loaded = k.sem(f"{tag}_loaded")
    tiles = {n: k.sb(f"{tag}_{n}", shape if len(shape) > 1 else [P] + shape) for n, shape in names.items()}
    tiles = {n: (t[:, :, :] if len(names[n]) == 3 else t[:, :]) for n, t in tiles.items()}

    def fetch(sp):
        for n, shape in names.items():
            src = dram[f"{tag[0]}_{n}"]
            if len(shape) == 1:
                src = src.partition_broadcast(P)
            sp.dma_start(tiles[n], src).then_inc(loaded, 16)
        sp.wait_ge(loaded, 16 * len(names))
    return tiles, fetch


def build(nc, t, out, stages=8, first=0):
    with ExitStack() as stack:
        k = Kit(nc, stack)
        X = k.sb("X", [P, TILES, D])
        ident = k.sb("ident", [P, P])
        parts_dram = nc.dram_tensor("qk_parts", [2, 3, D, TOK], BF16, kind="Internal").ap()
        shift_dram = nc.dram_tensor("shift", [HEADS, TOK], BF16, kind="Internal").ap()
        read = k.sem("x_read")
        ident_set = k.sem("ident_set")
        head_of = k.sb("head_of", [P, VW])
        head_of_set = k.sem("head_of_set")
        x_dram = t["x"].rearrange("b (t p) d -> p (b t) d", p=P)
        with nc.Block() as block:
            @block.sync
            def _(sp):
                sp.dma_start(X[:, :, :], x_dram).then_inc(read, 16)
                sp.wait_ge(read, 16)

            @block.gpsimd
            def _(pool):
                pool.memset(ident[:, :], 0.0).then_inc(ident_set, 1)
                pool.wait_ge(ident_set, 1)
                pool.affine_select(out=ident[:, :], in_=ident[:, :], compare_op=ALU.not_equal, fill=1.0,
                                   base=0, pattern=[[-1, P]], channel_multiplier=1).then_inc(ident_set, 1)
                pool.memset(head_of[:, :], 1.0).then_inc(head_of_set, 1)
                pool.wait_ge(head_of_set, 1)
                pool.affine_select(out=head_of[:, :], in_=head_of[:, :], compare_op=ALU.is_ge, fill=0.0,
                                   base=0, pattern=[[-HD, VW]], channel_multiplier=1).then_inc(head_of_set, 1)
                pool.wait_ge(head_of_set, 2)
                pool.affine_select(out=head_of[:, :], in_=head_of[:, :], compare_op=ALU.is_ge, fill=0.0,
                                   base=HD - 1, pattern=[[HD, VW]], channel_multiplier=-1).then_inc(head_of_set, 1)
        idn = ident[:, :]
        def layer(tag, body):
            with ExitStack() as own:
                body(*weights(tag, Kit(nc, own), t, WEIGHTS[tag[0]]) if tag[0] in WEIGHTS else ())

        parts, head = parts_dram, head_of[:, :]
        todo = [("a", lambda w, fetch: alibi_attention(nc, "a", X, w, idn, parts, head, fetch)),
                ("m0", lambda w, fetch: moe_ffn(nc, "m0", X, w, idn, fetch)),
                ("b", lambda w, fetch: decay_attention(nc, "b", X, w, idn, parts, head, fetch)),
                ("m1", lambda w, fetch: moe_ffn(nc, "m1", X, w, idn, fetch)),
                ("f", lambda w, fetch: fast_weights(nc, "f", X, w, idn, fetch)),
                ("l0", lambda w, fetch: lora_ffn(nc, "l0", X, w, idn, fetch)),
                ("c", lambda: centred_attention(nc, "c", X, idn, parts, shift_dram, head[:, 0:HEADS])),
                ("l1", lambda w, fetch: lora_ffn(nc, "l1", X, w, idn, fetch))]
        for tag, body in todo[first:stages]:
            with nc.cleanup_on_exit():
                layer(tag, body)

        written = k.sem("written")
        with nc.Block() as block:
            @block.sync
            def _(sp):
                sp.dma_start(out.rearrange("b (t p) d -> p (b t) d", p=P), X[:, :, :]).then_inc(written, 16)
                sp.wait_ge(written, 16)


def layout(i):
    import numpy as np
    c = np.ascontiguousarray
    x = i["L0_attn_a_x"]
    out = {"x": x}
    for tag, name, wqkv, bqkv, wout, bout in (
            ("a", "L0_attn_a", "Wqkv", "bqkv", "Wout", "bout"),
            ("b", "L0_attn_b", "Wqkv_w", "Wqkv_b", "out_w", "out_b")):
        turn = (lambda m: m) if tag == "a" else (lambda m: c(m.T))
        b = np.asarray(i[f"{name}_{bqkv}"])
        out |= {f"{tag}_qkv": turn(np.asarray(i[f"{name}_{wqkv}"])), f"{tag}_out": turn(np.asarray(i[f"{name}_{wout}"])),
                f"{tag}_b_qk": c(b.reshape(3, D)[:2].T), f"{tag}_b_v": c(b[2 * D:]), f"{tag}_b_out": i[f"{name}_{bout}"]}
    out["b_decay"] = i["L0_attn_b_distance_decay"]
    w_macro, w_micro = np.asarray(i["L0_ffn_w_macro"]), np.asarray(i["L0_ffn_w_micro"]).reshape(EXPERTS, D)
    out["m_norm"] = np.asarray(i["L0_ffn_norm_w"]).reshape(D, 1)
    out["m_gates"] = c(np.concatenate([w_macro, w_micro]).T)
    out["m_w1"] = c(np.asarray(i["L0_ffn_w1"]).reshape(EXPERTS * F, D).T)
    out["m_w2"] = c(np.asarray(i["L0_ffn_w2"]).reshape(EXPERTS, D, HALVES, P).transpose(3, 0, 2, 1).reshape(P, FT, D))
    heads = np.asarray(i["L1_attn_a_W_qkvb"]).reshape(FH, 3 * FD + 1, D)
    rows = [heads[:, n * FD:(n + 1) * FD].reshape(FW, D) for n in range(3)] + [heads[:, 3 * FD]]
    out["f_qkv"] = c(np.concatenate(rows).T)
    out["f_out"] = c(np.asarray(i["L1_attn_a_W_o"]).reshape(D, FW // P, P).transpose(2, 1, 0))
    out["f_ln_g"], out["f_ln_b"] = i["L1_attn_a_ln_g"], i["L1_attn_a_ln_b"]
    out["l_lora"] = c(np.concatenate([np.asarray(i["L1_ffn_base_w"]).T, np.asarray(i["L1_ffn_router_w"]).T,
                                      np.asarray(i["L1_ffn_lora_A"])], axis=1))
    out["l_lora_b"] = np.asarray(i["L1_ffn_lora_B"]).reshape(LE * LR, D)
    out["l_router_b"], out["l_base_b"] = i["L1_ffn_router_b"], i["L1_ffn_base_b"]
    return {n: c(np.asarray(a)) for n, a in out.items()}


def kernel(**inputs):
    import numpy as np
    import concourse.bacc as bacc
    from concourse.bass_utils import run_bass_kernel_spmd

    nc = bacc.Bacc("TRN2", target_bir_lowering=False, num_devices=1)
    arrays = layout(inputs)
    dram = {n: nc.dram_tensor(f"in_{n}", a.shape, mybir.dt.from_np(a.dtype), kind="ExternalInput").ap()
            for n, a in arrays.items()}
    out = nc.dram_tensor("out", (BATCH, SEQ, D), F32, kind="ExternalOutput").ap()
    build(nc, dram, out)
    r = run_bass_kernel_spmd(nc, [{f"in_{n}": a for n, a in arrays.items()}], core_ids=[0])
    return r.results[0]["out"]
```
